# Optimizing a Trainium2 kernel written in Bass

```python
import numpy as np
import jax
import jax.numpy as jnp

def _softmax(x, axis=-1):
    return jax.nn.softmax(x, axis=axis)

def _gelu(x):
    return jax.nn.gelu(x, approximate=True)

def _silu(x):
    return jax.nn.silu(x)

def _sigmoid(x):
    return jax.nn.sigmoid(x)

def _layernorm(x, axis=-1, eps=1e-05):
    m = jnp.mean(x, axis=axis, keepdims=True)
    v = jnp.var(x, axis=axis, keepdims=True)
    return (x - m) / jnp.sqrt(v + eps)

def _scatter_add(tgt, idx, src, axis=0):
    return tgt.at[idx].add(src)

def _segment_sum(src, seg, n):
    return jax.ops.segment_sum(src, seg, n)
kernel_name = 'mk_vit_tower_d1_tok_img768_r4_60bb96'

def setup_inputs(seed: int=0):
    np.random.seed(seed)
    _w = jnp.asarray

    def _rec_inputs():
        import jax
        import jax.numpy as jnp
        _rk = jax.random.key(seed)
        x = 7.57192e-06 + 1.00007 * jax.random.normal(jax.random.fold_in(_rk, 1), (16, 3, 96, 96), jnp.float32)
        return x
    x = _rec_inputs()

    def _L0_tok_setup():
        import jax, jax.numpy as jnp
        import numpy as np
        K = 4
        STRIDE = 4
        EPS = 1e-05
        SLOPE = 0.01

        def conv2d(x, w, b, stride):
            out = jax.lax.conv_general_dilated(x, w, (stride, stride), 'VALID', dimension_numbers=('NCHW', 'OIHW', 'NCHW'))
            return out + b[None, :, None, None]

        def batchnorm(x, g, b, m, v):
            inv = g / jnp.sqrt(v + EPS)
            return x * inv[None, :, None, None] + (b - m * inv)[None, :, None, None]

        def leaky_relu(x):
            return jnp.where(x >= 0, x, SLOPE * x)

        def deform_conv(x, offset, w, b):
            B, C, H, W = x.shape
            Ho, Wo = (offset.shape[2], offset.shape[3])
            KK = K * K
            off = offset.reshape(B, KK, 2, Ho, Wo)
            kh = jnp.repeat(jnp.arange(K), K).astype(x.dtype)
            kw = jnp.tile(jnp.arange(K), K).astype(x.dtype)
            base_y = (jnp.arange(Ho) * STRIDE).astype(x.dtype)
            base_x = (jnp.arange(Wo) * STRIDE).astype(x.dtype)
            py = base_y[None, None, :, None] + kh[None, :, None, None] + off[:, :, 0]
            px = base_x[None, None, None, :] + kw[None, :, None, None] + off[:, :, 1]
            y0 = jnp.floor(py)
            x0 = jnp.floor(px)
            wy = py - y0
            wx = px - x0

            def corner(yc, xc):
                yi = yc.astype(jnp.int32)
                xi = xc.astype(jnp.int32)
                valid = (yi >= 0) & (yi < H) & (xi >= 0) & (xi < W)
                yi = jnp.clip(yi, 0, H - 1)
                xi = jnp.clip(xi, 0, W - 1)
                v = jax.vmap(lambda img, a, c: img[:, a, c])(x, yi, xi)
                return v * valid[:, None].astype(x.dtype)
            v00 = corner(y0, x0)
            v01 = corner(y0, x0 + 1)
            v10 = corner(y0 + 1, x0)
            v11 = corner(y0 + 1, x0 + 1)
            wy_ = wy[:, None]
            wx_ = wx[:, None]
            sampled = v00 * (1 - wy_) * (1 - wx_) + v01 * (1 - wy_) * wx_ + v10 * wy_ * (1 - wx_) + v11 * wy_ * wx_
            out = jnp.einsum('bckhw,ock->bohw', sampled, w.reshape(w.shape[0], C, KK))
            return out + b[None, :, None, None]
        key = jax.random.key(seed)
        ks = jax.random.split(key, 16)
        f32 = jnp.float32
        inp = {'x': jax.random.normal(ks[0], (64, 3, 224, 224), f32), 'stem_w': jax.random.normal(ks[1], (96, 3, 4, 4), f32) * 0.1, 'stem_b': jax.random.normal(ks[2], (96,), f32) * 0.05, 'bn1_g': jax.random.uniform(ks[3], (96,), f32, 0.5, 1.5), 'bn1_b': jax.random.normal(ks[4], (96,), f32) * 0.05, 'bn1_m': jax.random.normal(ks[5], (96,), f32) * 0.05, 'bn1_v': jax.random.uniform(ks[6], (96,), f32, 0.5, 1.5), 'off_w': jax.random.normal(ks[7], (32, 96, 4, 4), f32) * 0.02, 'off_b': jax.random.normal(ks[8], (32,), f32) * 0.02, 'dcn_w': jax.random.normal(ks[9], (192, 96, 4, 4), f32) * 0.05, 'dcn_b': jax.random.normal(ks[10], (192,), f32) * 0.05, 'bn2_g': jax.random.uniform(ks[11], (192,), f32, 0.5, 1.5), 'bn2_b': jax.random.normal(ks[12], (192,), f32) * 0.05, 'bn2_m': jax.random.normal(ks[13], (192,), f32) * 0.05, 'bn2_v': jax.random.uniform(ks[14], (192,), f32, 0.5, 1.5)}
        return inp
    _L0_tok_all = _L0_tok_setup()
    _L0_tok_in = {k: v for k, v in _L0_tok_all.items() if k in ('stem_w', 'stem_b', 'bn1_g', 'bn1_b', 'bn1_m', 'bn1_v', 'off_w', 'off_b', 'dcn_w', 'dcn_b', 'bn2_g', 'bn2_b', 'bn2_m', 'bn2_v')}
    del _L0_tok_all

    def _L0_attn_setup():
        import jax, jax.numpy as jnp
        import numpy as np
        N_HEADS, D_MODEL, D_HEAD = (12, 192, 64)
        INIT_RANGE = 0.02
        B, P = (4, 512)
        key = jax.random.key(seed)
        ks = jax.random.split(key, 6)
        std = INIT_RANGE
        return {'normalized_resid_pre': jax.random.normal(ks[0], (B, P, D_MODEL), dtype=jnp.float32), 'Qs': jax.random.normal(ks[1], (N_HEADS, D_MODEL, D_HEAD), dtype=jnp.float32) * std, 'Ks': jax.random.normal(ks[2], (N_HEADS, D_MODEL, D_HEAD), dtype=jnp.float32) * std, 'Vs': jax.random.normal(ks[3], (N_HEADS, D_MODEL, D_HEAD), dtype=jnp.float32) * std, 'O': jax.random.normal(ks[4], (N_HEADS, D_HEAD, D_MODEL), dtype=jnp.float32) * std, 'Qbs': jnp.zeros((N_HEADS, D_HEAD), dtype=jnp.float32), 'Kbs': jnp.zeros((N_HEADS, D_HEAD), dtype=jnp.float32), 'Vbs': jnp.zeros((N_HEADS, D_HEAD), dtype=jnp.float32), 'Ob': jnp.zeros((D_MODEL,), dtype=jnp.float32)}
    _L0_attn_all = _L0_attn_setup()
    _L0_attn_in = {k: v for k, v in _L0_attn_all.items() if k in ('Qs', 'Ks', 'Vs', 'O', 'Qbs', 'Kbs', 'Vbs', 'Ob')}
    del _L0_attn_all

    def _L0_ffn_setup():
        import jax, jax.numpy as jnp
        import numpy as np
        DIM = 192
        FF = 768
        E = 8
        K = 2
        H = 12
        HD = DIM // H
        LN_EPS = 1e-05

        def _layernorm(x, g, b):
            m = jnp.mean(x, axis=-1, keepdims=True)
            v = jnp.var(x, axis=-1, keepdims=True)
            return (x - m) * jax.lax.rsqrt(v + LN_EPS) * g + b

        def _attention(x, Wqkv, Wproj):
            B, T, D = x.shape
            qkv = (x @ Wqkv).reshape(B, T, 3, H, HD)
            q, k, v = (qkv[:, :, 0], qkv[:, :, 1], qkv[:, :, 2])
            scores = jnp.einsum('bqhd,bkhd->bhqk', q, k) * jnp.float32(HD) ** (-0.5)
            attn = jax.nn.softmax(scores, axis=-1)
            out = jnp.einsum('bhqk,bkhd->bqhd', attn, v).reshape(B, T, D)
            return out @ Wproj

        def _moe(x, Wrouter, W1, W2):
            B, T, D = x.shape
            xf = x.reshape(-1, D)
            N = xf.shape[0]
            logits = xf @ Wrouter
            topk_w, topk_idx = jax.lax.top_k(logits, K)
            topk_w = jax.nn.softmax(topk_w.astype(jnp.float32), axis=-1).astype(x.dtype)
            we = jnp.zeros((N, E), x.dtype).at[jnp.arange(N)[:, None], topk_idx].add(topk_w)

            def body(acc, expert):
                W1e, W2e, we_e = expert
                h = jax.nn.gelu(xf @ W1e, approximate=False)
                return (acc + we_e[:, None] * (h @ W2e), None)
            out, _ = jax.lax.scan(body, jnp.zeros_like(xf), (W1, W2, we.T))
            return out.reshape(B, T, D)
        key = jax.random.key(seed)
        ks = jax.random.split(key, 7)
        B, T = (4, 256)
        init = lambda k, shape, fan: jax.random.normal(k, shape, jnp.float32) * fan ** (-0.5)
        return {'x': jax.random.normal(ks[0], (B, T, DIM), jnp.float32), 'Wqkv': init(ks[1], (DIM, 3 * DIM), DIM), 'Wproj': init(ks[2], (DIM, DIM), DIM), 'Wrouter': init(ks[3], (DIM, E), DIM), 'W1': init(ks[4], (E, DIM, FF), DIM), 'W2': init(ks[5], (E, FF, DIM), FF), 'ln1_g': jnp.ones((DIM,), jnp.float32), 'ln1_b': jnp.zeros((DIM,), jnp.float32), 'ln2_g': jnp.ones((DIM,), jnp.float32), 'ln2_b': jnp.zeros((DIM,), jnp.float32)}
    _L0_ffn_all = _L0_ffn_setup()
    _L0_ffn_in = {k: v for k, v in _L0_ffn_all.items() if k in ('Wqkv', 'Wproj', 'Wrouter', 'W1', 'W2', 'ln1_g', 'ln1_b', 'ln2_g', 'ln2_b')}
    del _L0_ffn_all
    return {'x': x, 'L0_tok_stem_w': _L0_tok_in['stem_w'], 'L0_tok_stem_b': _L0_tok_in['stem_b'], 'L0_tok_bn1_g': _L0_tok_in['bn1_g'], 'L0_tok_bn1_b': _L0_tok_in['bn1_b'], 'L0_tok_bn1_m': _L0_tok_in['bn1_m'], 'L0_tok_bn1_v': _L0_tok_in['bn1_v'], 'L0_tok_off_w': _L0_tok_in['off_w'], 'L0_tok_off_b': _L0_tok_in['off_b'], 'L0_tok_dcn_w': _L0_tok_in['dcn_w'], 'L0_tok_dcn_b': _L0_tok_in['dcn_b'], 'L0_tok_bn2_g': _L0_tok_in['bn2_g'], 'L0_tok_bn2_b': _L0_tok_in['bn2_b'], 'L0_tok_bn2_m': _L0_tok_in['bn2_m'], 'L0_tok_bn2_v': _L0_tok_in['bn2_v'], 'L0_attn_Qs': _L0_attn_in['Qs'], 'L0_attn_Ks': _L0_attn_in['Ks'], 'L0_attn_Vs': _L0_attn_in['Vs'], 'L0_attn_O': _L0_attn_in['O'], 'L0_attn_Qbs': _L0_attn_in['Qbs'], 'L0_attn_Kbs': _L0_attn_in['Kbs'], 'L0_attn_Vbs': _L0_attn_in['Vbs'], 'L0_attn_Ob': _L0_attn_in['Ob'], 'L0_ffn_Wqkv': _L0_ffn_in['Wqkv'], 'L0_ffn_Wproj': _L0_ffn_in['Wproj'], 'L0_ffn_Wrouter': _L0_ffn_in['Wrouter'], 'L0_ffn_W1': _L0_ffn_in['W1'], 'L0_ffn_W2': _L0_ffn_in['W2'], 'L0_ffn_ln1_g': _L0_ffn_in['ln1_g'], 'L0_ffn_ln1_b': _L0_ffn_in['ln1_b'], 'L0_ffn_ln2_g': _L0_ffn_in['ln2_g'], 'L0_ffn_ln2_b': _L0_ffn_in['ln2_b']}

def reference(x, L0_tok_stem_w, L0_tok_stem_b, L0_tok_bn1_g, L0_tok_bn1_b, L0_tok_bn1_m, L0_tok_bn1_v, L0_tok_off_w, L0_tok_off_b, L0_tok_dcn_w, L0_tok_dcn_b, L0_tok_bn2_g, L0_tok_bn2_b, L0_tok_bn2_m, L0_tok_bn2_v, L0_attn_Qs, L0_attn_Ks, L0_attn_Vs, L0_attn_O, L0_attn_Qbs, L0_attn_Kbs, L0_attn_Vbs, L0_attn_Ob, L0_ffn_Wqkv, L0_ffn_Wproj, L0_ffn_Wrouter, L0_ffn_W1, L0_ffn_W2, L0_ffn_ln1_g, L0_ffn_ln1_b, L0_ffn_ln2_g, L0_ffn_ln2_b):
    import jax
    import jax.numpy as jnp

    def _L0_tok_ref(x, stem_w, stem_b, bn1_g, bn1_b, bn1_m, bn1_v, off_w, off_b, dcn_w, dcn_b, bn2_g, bn2_b, bn2_m, bn2_v):
        import jax, jax.numpy as jnp
        import numpy as np
        K = 4
        STRIDE = 4
        EPS = 1e-05
        SLOPE = 0.01

        def conv2d(x, w, b, stride):
            out = jax.lax.conv_general_dilated(x, w, (stride, stride), 'VALID', dimension_numbers=('NCHW', 'OIHW', 'NCHW'))
            return out + b[None, :, None, None]

        def batchnorm(x, g, b, m, v):
            inv = g / jnp.sqrt(v + EPS)
            return x * inv[None, :, None, None] + (b - m * inv)[None, :, None, None]

        def leaky_relu(x):
            return jnp.where(x >= 0, x, SLOPE * x)

        def deform_conv(x, offset, w, b):
            B, C, H, W = x.shape
            Ho, Wo = (offset.shape[2], offset.shape[3])
            KK = K * K
            off = offset.reshape(B, KK, 2, Ho, Wo)
            kh = jnp.repeat(jnp.arange(K), K).astype(x.dtype)
            kw = jnp.tile(jnp.arange(K), K).astype(x.dtype)
            base_y = (jnp.arange(Ho) * STRIDE).astype(x.dtype)
            base_x = (jnp.arange(Wo) * STRIDE).astype(x.dtype)
            py = base_y[None, None, :, None] + kh[None, :, None, None] + off[:, :, 0]
            px = base_x[None, None, None, :] + kw[None, :, None, None] + off[:, :, 1]
            y0 = jnp.floor(py)
            x0 = jnp.floor(px)
            wy = py - y0
            wx = px - x0

            def corner(yc, xc):
                yi = yc.astype(jnp.int32)
                xi = xc.astype(jnp.int32)
                valid = (yi >= 0) & (yi < H) & (xi >= 0) & (xi < W)
                yi = jnp.clip(yi, 0, H - 1)
                xi = jnp.clip(xi, 0, W - 1)
                v = jax.vmap(lambda img, a, c: img[:, a, c])(x, yi, xi)
                return v * valid[:, None].astype(x.dtype)
            v00 = corner(y0, x0)
            v01 = corner(y0, x0 + 1)
            v10 = corner(y0 + 1, x0)
            v11 = corner(y0 + 1, x0 + 1)
            wy_ = wy[:, None]
            wx_ = wx[:, None]
            sampled = v00 * (1 - wy_) * (1 - wx_) + v01 * (1 - wy_) * wx_ + v10 * wy_ * (1 - wx_) + v11 * wy_ * wx_
            out = jnp.einsum('bckhw,ock->bohw', sampled, w.reshape(w.shape[0], C, KK))
            return out + b[None, :, None, None]
        h = conv2d(x, stem_w, stem_b, 4)
        h = leaky_relu(batchnorm(h, bn1_g, bn1_b, bn1_m, bn1_v))
        offset = conv2d(h, off_w, off_b, 4)
        h = deform_conv(h, offset, dcn_w, dcn_b)
        h = leaky_relu(batchnorm(h, bn2_g, bn2_b, bn2_m, bn2_v))
        B, C, Ho, Wo = h.shape
        return h.reshape(B, C, Ho * Wo).transpose(0, 2, 1)

    def _L0_attn_ref(normalized_resid_pre, Qs, Ks, Vs, O, Qbs, Kbs, Vbs, Ob):
        import jax, jax.numpy as jnp
        import numpy as np
        N_HEADS, D_MODEL, D_HEAD = (12, 192, 64)
        INIT_RANGE = 0.02
        B, P = (4, 512)
        x = normalized_resid_pre
        q = jnp.einsum('bpd,hdk->bphk', x, Qs) + Qbs
        k = jnp.einsum('bpd,hdk->bphk', x, Ks) + Kbs
        v = jnp.einsum('bpd,hdk->bphk', x, Vs) + Vbs
        scores = jnp.einsum('bqhk,bmhk->bhqm', q, k) / jnp.sqrt(jnp.asarray(D_HEAD, x.dtype))
        pattern = jax.nn.softmax(scores, axis=-1)
        z = jnp.einsum('bmhk,bhqm->bqhk', v, pattern)
        attn_out = jnp.einsum('bqhk,hkd->bqd', z, O) + Ob
        return attn_out

    def _L0_ffn_ref(x, Wqkv, Wproj, Wrouter, W1, W2, ln1_g, ln1_b, ln2_g, ln2_b):
        import jax, jax.numpy as jnp
        import numpy as np
        DIM = 192
        FF = 768
        E = 8
        K = 2
        H = 12
        HD = DIM // H
        LN_EPS = 1e-05

        def _layernorm(x, g, b):
            m = jnp.mean(x, axis=-1, keepdims=True)
            v = jnp.var(x, axis=-1, keepdims=True)
            return (x - m) * jax.lax.rsqrt(v + LN_EPS) * g + b

        def _attention(x, Wqkv, Wproj):
            B, T, D = x.shape
            qkv = (x @ Wqkv).reshape(B, T, 3, H, HD)
            q, k, v = (qkv[:, :, 0], qkv[:, :, 1], qkv[:, :, 2])
            scores = jnp.einsum('bqhd,bkhd->bhqk', q, k) * jnp.float32(HD) ** (-0.5)
            attn = jax.nn.softmax(scores, axis=-1)
            out = jnp.einsum('bhqk,bkhd->bqhd', attn, v).reshape(B, T, D)
            return out @ Wproj

        def _moe(x, Wrouter, W1, W2):
            B, T, D = x.shape
            xf = x.reshape(-1, D)
            N = xf.shape[0]
            logits = xf @ Wrouter
            topk_w, topk_idx = jax.lax.top_k(logits, K)
            topk_w = jax.nn.softmax(topk_w.astype(jnp.float32), axis=-1).astype(x.dtype)
            we = jnp.zeros((N, E), x.dtype).at[jnp.arange(N)[:, None], topk_idx].add(topk_w)

            def body(acc, expert):
                W1e, W2e, we_e = expert
                h = jax.nn.gelu(xf @ W1e, approximate=False)
                return (acc + we_e[:, None] * (h @ W2e), None)
            out, _ = jax.lax.scan(body, jnp.zeros_like(xf), (W1, W2, we.T))
            return out.reshape(B, T, D)
        x = x + _attention(_layernorm(x, ln1_g, ln1_b), Wqkv, Wproj)
        x = x + _moe(_layernorm(x, ln2_g, ln2_b), Wrouter, W1, W2)
        return x
    h = _L0_tok_ref(x, L0_tok_stem_w, L0_tok_stem_b, L0_tok_bn1_g, L0_tok_bn1_b, L0_tok_bn1_m, L0_tok_bn1_v, L0_tok_off_w, L0_tok_off_b, L0_tok_dcn_w, L0_tok_dcn_b, L0_tok_bn2_g, L0_tok_bn2_b, L0_tok_bn2_m, L0_tok_bn2_v)
    h = h + _L0_attn_ref(_layernorm(h, axis=-1), L0_attn_Qs, L0_attn_Ks, L0_attn_Vs, L0_attn_O, L0_attn_Qbs, L0_attn_Kbs, L0_attn_Vbs, L0_attn_Ob)
    h = h + _L0_ffn_ref(_layernorm(h, axis=-1), L0_ffn_Wqkv, L0_ffn_Wproj, L0_ffn_Wrouter, L0_ffn_W1, L0_ffn_W2, L0_ffn_ln1_g, L0_ffn_ln1_b, L0_ffn_ln2_g, L0_ffn_ln2_b)
    return h

_drawn_inputs = setup_inputs


def setup_inputs(seed=0):
    import zlib

    import numpy as np

    out = dict(_drawn_inputs(seed))
    spreads = {'L0_attn_Qbs': (0.0, 0.8),
     'L0_attn_Kbs': (0.0, 0.8),
     'L0_attn_Vbs': (0.0, 0.1),
     'L0_attn_Ob': (0.0, 0.1),
     'L0_ffn_ln1_g': (1.0, 0.2),
     'L0_ffn_ln1_b': (0.0, 0.1),
     'L0_ffn_ln2_g': (1.0, 0.2),
     'L0_ffn_ln2_b': (0.0, 0.1)}
    factors = {'L0_attn_Qs': 4.265, 'L0_attn_Ks': 4.889}
    for name, (base, spread) in spreads.items():
        noise = np.random.default_rng([zlib.crc32(name.encode()), seed]).standard_normal(out[name].shape)
        drawn = base * np.exp(spread * noise) if base else spread * noise
        out[name] = jnp.asarray(drawn.astype(out[name].dtype))
    for name, factor in factors.items():
        out[name] = (out[name] * factor).astype(out[name].dtype)
    return out
```

```python
import concourse.bass as bass
from concourse import mybir
from contextlib import ExitStack

F32 = mybir.dt.float32
BF16 = mybir.dt.bfloat16
U32 = mybir.dt.uint32
ALU = mybir.AluOpType
ACT = mybir.ActivationFunctionType
AX = mybir.AxisListType

B, CIN, IMG = 16, 3, 96
KS = 4
SIDE = IMG // KS
PIX = SIDE * SIDE
HALF = PIX // 2
C1 = 96
TAPS = KS * KS
SIDE2 = SIDE // KS
TPI = SIDE2 * SIDE2
NTOK = B * TPI
KPATCH = CIN * TAPS
DIM = 192
DC = 2
CH = DIM // DC
ROWS = 5
TILE = ROWS * SIDE
NT = -(-SIDE // ROWS)
LAST = PIX - (NT - 1) * TILE
IPG = 3
GT = IPG * TPI
GROUPS = [(g * GT, min(GT, NTOK - g * GT)) for g in range(-(-NTOK // GT))]
NG = len(GROUPS)
HEADS = 12
FF = 768
EXPERTS = 8
FT = FF // 128
EPS = 1e-5
SLOPE = 0.01
QUAD = 4
BIG = 2.0 ** 100


class Steps:

    def __init__(self, eng, sem):
        self.eng, self.sem, self.n = eng, sem, 0

    def done(self, ins):
        ins.then_inc(self.sem, 1)
        self.n += 1
        return self.n

    def wait(self, n=None):
        self.eng.wait_ge(self.sem, self.n if n is None else n)


def pixel_rows(t):
    return TILE if t < NT - 1 else LAST


def stage_offsets(nc, P, D):
    ctx = ExitStack()
    with ctx:
        def sb(name, shape, dt=F32):
            return ctx.enter_context(nc.sbuf_tensor(name, shape, dt))

        def sem(name):
            return ctx.enter_context(nc.semaphore(name))

        ps = P["ps"]
        stem_raw = sb("stem_raw", [KPATCH + 1, C1])
        stem_par = sb("stem_par", [KPATCH + 1, 4, C1])
        bias_row = sb("bias_row", [KPATCH + 1, 1])
        stem_inv = sb("stem_inv", [KPATCH + 1, C1])
        stem_pow = sb("stem_pow", [KPATCH + 1, C1])
        stem_shift = sb("stem_shift", [KPATCH + 1, C1])
        exponent = sb("exponent", [128, DIM])
        dcn_par = sb("dcn_par", [C1 + 1, 4, DIM])
        dcn_inv = sb("dcn_inv", [C1 + 1, DIM])
        dcn_pow = sb("dcn_pow", [C1 + 1, DIM])
        dcn_shift = sb("dcn_shift", [C1 + 1, DIM])
        off_w = sb("off_w", [C1, TAPS, 3, 32])
        off_b = sb("off_b", [C1, 1])
        grid_raw = sb("grid_raw", [C1 + 3, NTOK])
        spread_raw = sb("spread_raw", [C1 + 3, 2, TAPS, 128])
        h_lin = sb("h_lin", [C1, 4, HALF])
        h_act = sb("h_act", [C1, 2, QUAD, PIX])
        off = sb("off", [C1, 2, QUAD * TPI])
        off_p = sb("off_p", [C1, 2, QUAD * TPI], BF16)
        off_r = sb("off_r", [C1, 2, QUAD * TPI])

        stem_loaded = sem("stem_loaded")
        patches_loaded = [sem(f"patches_loaded{q}") for q in range(B // QUAD)]
        off_loaded = sem("off_loaded")
        dcn_loaded = sem("dcn_loaded")
        exponent_set = sem("exponent_set")
        pool_step = sem("pool_step")
        stem_inv_ready = sem("stem_inv_ready")
        dcn_inv_ready = sem("dcn_inv_ready")
        prep_step = sem("prep_step")
        stem_w_ready = sem("stem_w_ready")
        dcn_w_ready = sem("dcn_w_ready")
        h_ready = sem("h_ready")
        h_copied = sem("h_copied")
        h_done = sem("h_done")
        off_ready = sem("off_ready")
        off_copied = sem("off_copied")
        part_step = sem("part_step")
        ones_set = sem("ones_set")
        NH = 2 * B

        with nc.Block() as block:
            @block.sync
            def _(sp):
                sp.dma_start(stem_raw[0:KPATCH, :], D["stem_w"]).then_inc(stem_loaded, 16)
                sp.dma_start(stem_raw[KPATCH:KPATCH + 1, :], D["stem_par"][0:1, :]).then_inc(stem_loaded, 16)
                for i in range(4):
                    sp.dma_start(stem_par[:, i, :], D["stem_par"][1 + i:2 + i, :].to_broadcast((KPATCH + 1, C1))).then_inc(stem_loaded, 16)
                sp.dma_start(bias_row[:, :], D["bias_row"]).then_inc(stem_loaded, 16)
                for q in range(B // QUAD):
                    sp.wait_ge(ones_set, 1)
                    sp.dma_start(P["patches"][0:KPATCH, QUAD * q:QUAD * (q + 1), :], D["patches"][:, QUAD * q:QUAD * (q + 1), :]).then_inc(patches_loaded[q], 16)
                    if q == 0:
                        for i in range(3):
                            sp.dma_start(off_w[:, :, i, :], D["off_w"]).then_inc(off_loaded, 16)
                            sp.dma_start(off_b[32 * i:32 * (i + 1), :], D["off_b"]).then_inc(off_loaded, 16)
                        sp.dma_start(grid_raw[C1:C1 + 3, :], D["grid"]).then_inc(off_loaded, 16)
                        sp.dma_start(spread_raw[:, :, :, :], D["spread"]).then_inc(off_loaded, 16)
                for i in range(4):
                    sp.dma_start(dcn_par[:, i, :], D["dcn_par"][1 + i:2 + i, :].to_broadcast((C1 + 1, DIM))).then_inc(dcn_loaded, 16)
                sp.dma_start(P["dcn_w"][0:C1, :, :], D["dcn_w"]).then_inc(dcn_loaded, 16)
                sp.dma_start(P["dcn_w"][C1:C1 + 1, 0, :], D["dcn_par"][0:1, :]).then_inc(dcn_loaded, 16)
                sp.wait_ge(dcn_loaded, 16 * 6)

            @block.gpsimd
            def _(pool):
                nc.gpsimd.memset(exponent[:, :], -0.5).then_inc(exponent_set, 1)
                steps = Steps(pool, pool_step)
                for par, inv, loaded, n, ready in ((stem_par, stem_inv, stem_loaded, 7, stem_inv_ready), (dcn_par, dcn_inv, dcn_loaded, 6, dcn_inv_ready)):
                    pool.wait_ge(loaded, 16 * n)
                    steps.done(nc.gpsimd.tensor_scalar(inv[:, :], par[:, 3, :], EPS, None, ALU.add))
                    steps.wait()
                    pool.wait_ge(exponent_set, 1)
                    p = stem_pow if inv is stem_inv else dcn_pow
                    rows, cols = (KPATCH + 1, C1) if inv is stem_inv else (C1 + 1, DIM)
                    nc.gpsimd.tensor_tensor(p[:, :], inv[:, :], exponent[0:rows, 0:cols], ALU.pow).then_inc(ready, 1)

            @block.vector
            def _(dve):
                def split(dve, parts, q):
                    s, cols = q % 2, slice(q * QUAD * TPI, (q + 1) * QUAD * TPI)
                    dve.wait_ge(off_copied, q + 1)
                    nc.vector.tensor_copy(P["parts"][0:32, cols], off[0:32, s, :])
                    parts.done(nc.vector.tensor_copy(off_p[:, s, :], off[:, s, :]))
                    parts.wait()
                    parts.done(nc.vector.tensor_tensor(off_r[:, s, :], off[:, s, :], off_p[:, s, :], ALU.subtract))
                    parts.wait()
                    nc.vector.tensor_copy(P["parts"][32:64, cols], off_r[32:64, s, :])
                    parts.done(nc.vector.tensor_copy(off_p[64:96, s, :], off_r[64:96, s, :]))
                    parts.wait()
                    nc.vector.tensor_tensor(P["parts"][64:96, cols], off_r[64:96, s, :], off_p[64:96, s, :], ALU.subtract)

                steps = Steps(dve, prep_step)
                nc.vector.memset(P["patches"][:, :, :], 1.0).then_inc(ones_set, 1)
                nc.vector.memset(P["samples"][C1:C1 + 1, 0, :], 1.0)
                dve.wait_ge(stem_inv_ready, 1)
                steps.done(nc.vector.tensor_tensor(stem_inv[:, :], stem_pow[:, :], stem_par[:, 0, :], ALU.mult))
                steps.wait()
                steps.done(nc.vector.tensor_tensor(stem_raw[:, :], stem_raw[:, :], stem_inv[:, :], ALU.mult))
                steps.done(nc.vector.tensor_tensor(stem_shift[:, :], stem_par[:, 2, :], stem_inv[:, :], ALU.mult))
                steps.wait()
                steps.done(nc.vector.tensor_tensor(stem_shift[:, :], stem_par[:, 1, :], stem_shift[:, :], ALU.subtract))
                steps.wait()
                nc.vector.scalar_tensor_tensor(P["stem_w"][:, :], stem_shift[:, :], bias_row[:, 0:1], stem_raw[:, :], ALU.mult, ALU.add).then_inc(stem_w_ready, 1)
                dve.wait_ge(off_loaded, 16 * 8)
                nc.vector.tensor_copy(P["parts"][C1:C1 + 3, :], grid_raw[C1:C1 + 3, :])
                nc.vector.tensor_copy(P["spread"][:, :, :, :], spread_raw[:, :, :, :])
                parts = Steps(dve, part_step)
                for q in range(B // QUAD):
                    for i in range(2 * QUAD):
                        n = 2 * QUAD * q + i
                        dve.wait_ge(h_copied, n + 1)
                        if q >= 2:
                            dve.wait_ge(off_ready, q - 1)
                        nc.vector.scalar_tensor_tensor(h_act[:, q % 2, i // 2, (i % 2) * HALF:(i % 2 + 1) * HALF], ps[0:C1, n % 4, 0:HALF], SLOPE, h_lin[:, n % 4, :], ALU.mult, ALU.max).then_inc(h_done, 1)
                    if q >= 1:
                        split(dve, parts, q - 1)
                split(dve, parts, B // QUAD - 1)
                dve.wait_ge(dcn_inv_ready, 1)
                steps.done(nc.vector.tensor_tensor(dcn_inv[:, :], dcn_pow[:, :], dcn_par[:, 0, :], ALU.mult))
                steps.wait()
                steps.done(nc.vector.tensor_tensor(dcn_shift[:, :], dcn_par[:, 2, :], dcn_inv[:, :], ALU.mult))
                steps.wait()
                steps.done(nc.vector.tensor_tensor(dcn_shift[:, :], dcn_par[:, 1, :], dcn_shift[:, :], ALU.subtract))
                steps.done(nc.vector.tensor_tensor(P["dcn_w"][0:C1, :, :], P["dcn_w"][0:C1, :, :], dcn_inv[0:C1, :].unsqueeze(1).to_broadcast((C1, TAPS, DIM)), ALU.mult))
                steps.done(nc.vector.tensor_tensor(P["dcn_w"][C1:C1 + 1, 0, :], P["dcn_w"][C1:C1 + 1, 0, :], dcn_inv[C1:C1 + 1, :], ALU.mult))
                steps.wait()
                nc.vector.tensor_tensor(P["dcn_w"][C1:C1 + 1, 0, :], P["dcn_w"][C1:C1 + 1, 0, :], dcn_shift[C1:C1 + 1, :], ALU.add).then_inc(dcn_w_ready, 1)

            @block.scalar
            def _(act):
                def bias_offsets(act, q):
                    act.wait_ge(off_ready, q + 1)
                    if q >= 2:
                        act.wait_ge(part_step, 3 * (q - 1))
                    nc.scalar.activation(off[:, q % 2, :], ps[0:C1, 4 + q % 2, 0:QUAD * TPI], ACT.Identity, bias=off_b[:, 0:1]).then_inc(off_copied, 1)

                act.wait_ge(off_loaded, 16 * 8)
                for q in range(B // QUAD):
                    for i in range(2 * QUAD):
                        n = 2 * QUAD * q + i
                        act.wait_ge(h_ready, n + 1)
                        if n >= 4:
                            act.wait_ge(h_done, n - 3)
                        nc.scalar.activation(h_lin[:, n % 4, :], ps[0:C1, n % 4, 0:HALF], ACT.Copy).then_inc(h_copied, 1)
                    if q >= 1:
                        bias_offsets(act, q - 1)
                bias_offsets(act, B // QUAD - 1)

            @block.tensor
            def _(pe):
                def offsets(q):
                    pe.wait_ge(h_done, 2 * QUAD * (q + 1))
                    if q >= 2:
                        pe.wait_ge(off_copied, q - 1)
                    view = h_act[:, q % 2, :, :].rearrange("c i (y u x v) -> c i y u x v", u=KS, v=KS, x=SIDE2)
                    for k in range(TAPS):
                        ins = nc.tensor.matmul(ps[0:C1, 4 + q % 2, 0:QUAD * TPI], off_w[:, k, :, :].rearrange("c a b -> c (a b)"), view[:, :, :, k // KS, :, k % KS],
                                               start=(k == 0), stop=(k == TAPS - 1))
                    ins.then_inc(off_ready, 1)

                pe.wait_ge(stem_w_ready, 1)
                for q in range(B // QUAD):
                    pe.wait_ge(patches_loaded[q], 16)
                    for i in range(2 * QUAD):
                        n = 2 * QUAD * q + i
                        if n >= 4:
                            pe.wait_ge(h_done, n - 3)
                        nc.tensor.matmul(ps[0:C1, n % 4, 0:HALF], P["stem_w"][:, :], P["patches"][:, QUAD * q + i // 2, (i % 2) * HALF:(i % 2 + 1) * HALF],
                                         start=True, stop=True).then_inc(h_ready, 1)
                        if i == 2:
                            if q == 1:
                                pe.wait_ge(off_loaded, 16 * 8)
                            if q >= 1:
                                offsets(q - 1)
                offsets(B // QUAD - 1)


def stage_sampling(nc, P, D):
    ctx = ExitStack()
    with ctx:
        def sb(name, shape, dt=F32):
            return ctx.enter_context(nc.sbuf_tensor(name, shape, dt))

        def sem(name):
            return ctx.enter_context(nc.semaphore(name))

        ps = P["ps"]
        dist_x = sb("dist_x", [TILE, PIX])
        hat_x = sb("hat_x", [TILE, 2, PIX])
        dist_y = sb("dist_y", [TILE, NT, PIX])
        weights = sb("weights", [TILE, 2, NT, PIX])
        hT_lin = sb("hT_lin", [TILE, 2, NT * C1])
        hT = sb("hT", [TILE, 2, NT, C1])
        lin = sb("lin", [GT, 2, DIM])
        stats = sb("stats", [GT, NG, 6])
        mv = sb("mv", [GT, NG, 2])
        var_eps = sb("var_eps", [GT, NG])
        rstd = sb("rstd", [GT, NG])
        xhat = sb("xhat", [GT, 2, DIM])

        hT_ready = sem("hT_ready")
        hT_copied = sem("hT_copied")
        hT_done = sem("hT_done")
        dx_ready = sem("dx_ready")
        dy_ready = sem("dy_ready")
        dist_x_ready = sem("dist_x_ready")
        hat_x_ready = sem("hat_x_ready")
        dist_y_ready = sem("dist_y_ready")
        fall_ready = sem("fall_ready")
        weights_ready = sem("weights_ready")
        samples_ready = sem("samples_ready")
        samples_copied = sem("samples_copied")
        conv_ready = sem("conv_ready")
        conv_copied = sem("conv_copied")
        h_ready = sem("tokens_ready")
        stats_ready = sem("stats_ready")
        mv_ready = sem("mv_ready")
        pool_step = sem("norm_step")
        rstd_ready = sem("rstd_ready")
        xhat_ready = sem("xhat_ready")
        xT_ready = sem("xT_ready")
        xT_copied = sem("xT_copied")

        with nc.Block() as block:
            @block.tensor
            def _(pe):
                def positions(b):
                    if b >= 1:
                        pe.wait_ge(dist_x_ready, b)
                    for axis, bank, ready in ((1, 0, dx_ready), (0, 2, dy_ready)):
                        if axis == 0 and b >= 1:
                            pe.wait_ge(dist_y_ready, NT * b)
                        for k in range(TAPS):
                            ins = nc.tensor.matmul(ps[:, bank + k // 8, (k % 8) * TPI:(k % 8 + 1) * TPI], P["spread"][:, axis, k, :], P["parts"][:, b * TPI:(b + 1) * TPI], start=True, stop=True)
                        ins.then_inc(ready, 1)

                def stem_T(b):
                    if b >= 2:
                        pe.wait_ge(hT_done, b - 1)
                    for t in range(NT):
                        ins = nc.tensor.matmul(ps[0:pixel_rows(t), 6 + b % 2, t * C1:(t + 1) * C1], P["patches"][:, b, t * TILE:t * TILE + pixel_rows(t)], P["stem_w"][:, :], start=True, stop=True)
                    ins.then_inc(hT_ready, 1)

                def sample(b, half):
                    pe.wait_ge(hT_done, b + 1)
                    if b >= 1:
                        pe.wait_ge(samples_copied, 2 * b + half - 1)
                    for t in range(NT):
                        pe.wait_ge(weights_ready, NT * b + t + 1)
                        ins = nc.tensor.matmul(ps[0:C1, 4 + half, 0:HALF], hT[0:pixel_rows(t), b % 2, t, :], weights[0:pixel_rows(t), b % 2, t, half * HALF:(half + 1) * HALF],
                                               start=(t == 0), stop=(t == NT - 1))
                    ins.then_inc(samples_ready, 1)

                stem_T(0)
                positions(0)
                for b in range(B):
                    if b + 1 < B:
                        positions(b + 1)
                        stem_T(b + 1)
                    sample(b, 0)
                    sample(b, 1)

                def conv(g):
                    t0, n = GROUPS[g]
                    pe.wait_ge(samples_copied, 2 * min(B, IPG * (g + 1)))
                    if g < 2:
                        pe.wait_ge(dist_x_ready, B)
                    else:
                        pe.wait_ge(h_ready, g - 1)
                    for k in range(TAPS):
                        rows = C1 + (k == 0)
                        ins = nc.tensor.matmul(ps[0:n, g % 2, 0:DIM], P["samples"][0:rows, k, t0:t0 + n], P["dcn_w"][0:rows, k, :], start=(k == 0), stop=(k == TAPS - 1))
                    ins.then_inc(conv_ready, 1)

                def transpose(g):
                    t0, n = GROUPS[g]
                    pe.wait_ge(xhat_ready, g + 1)
                    if g < 2:
                        pe.wait_ge(dist_y_ready, NT * B)
                    else:
                        pe.wait_ge(xT_copied, g - 1)
                    for c in range(DC):
                        ins = nc.tensor.transpose(ps[0:CH, 2 + g % 2, c * GT:c * GT + n], xhat[0:n, g % 2, c * CH:(c + 1) * CH], P["ident"][0:n, 0:n])
                    ins.then_inc(xT_ready, 1)

                for g in range(NG):
                    conv(g)
                    if g >= 1:
                        transpose(g - 1)
                transpose(NG - 1)

            @block.scalar
            def _(act):
                def copy_hT(b):
                    act.wait_ge(hT_ready, b + 1)
                    if b >= 2:
                        act.wait_ge(hT_done, b - 1)
                    nc.scalar.activation(hT_lin[:, b % 2, 0:(NT - 1) * C1], ps[0:TILE, 6 + b % 2, 0:(NT - 1) * C1], ACT.Copy).then_inc(hT_copied, 1)
                    nc.scalar.activation(hT_lin[0:LAST, b % 2, (NT - 1) * C1:NT * C1], ps[0:LAST, 6 + b % 2, (NT - 1) * C1:NT * C1], ACT.Copy).then_inc(hT_copied, 1)

                def hats(b):
                    act.wait_ge(dx_ready, b + 1)
                    if b >= 1:
                        act.wait_ge(hat_x_ready, b)
                    nc.scalar.activation(dist_x[:, :].rearrange("p (a c) -> p a c", a=2), ps[0:TILE, 0:2, 0:HALF], ACT.Abs).then_inc(dist_x_ready, 1)
                    act.wait_ge(dist_x_ready, b + 1)
                    if b >= 2:
                        act.wait_ge(weights_ready, NT * (b - 1))
                    nc.scalar.activation(hat_x[:, b % 2, :], dist_x[:, :], ACT.Relu, bias=P["row_shift"][0:TILE, NT:NT + 1], scale=-1.0).then_inc(hat_x_ready, 1)

                def distance_y(b, t):
                    if t == 0:
                        act.wait_ge(dy_ready, b + 1)
                    if b >= 1:
                        act.wait_ge(weights_ready, NT * (b - 1) + t + 1)
                    nc.scalar.activation(dist_y[:, t, :].rearrange("p (a c) -> p a c", a=2), ps[0:TILE, 2:4, 0:HALF], ACT.Abs, bias=P["row_shift"][0:TILE, t:t + 1]).then_inc(dist_y_ready, 1)

                def copy_samples(b, half):
                    act.wait_ge(samples_ready, 2 * b + half + 1)
                    nc.scalar.activation(P["samples"][0:C1, 8 * half:8 * (half + 1), b * TPI:(b + 1) * TPI], ps[0:C1, 4 + half, 0:HALF].rearrange("p (k t) -> p k t", k=8), ACT.Copy).then_inc(samples_copied, 1)

                copy_hT(0)
                hats(0)
                for t in range(NT):
                    distance_y(0, t)
                for b in range(B):
                    if b + 1 < B:
                        hats(b + 1)
                        distance_y(b + 1, 0)
                        copy_hT(b + 1)
                        distance_y(b + 1, 1)
                        distance_y(b + 1, 2)
                    copy_samples(b, 0)
                    if b + 1 < B:
                        distance_y(b + 1, 3)
                        distance_y(b + 1, 4)
                    copy_samples(b, 1)

                def copy_T(g):
                    t0, n = GROUPS[g]
                    act.wait_ge(xT_ready, g + 1)
                    nc.scalar.activation(P["xT"][0:CH, :, t0:t0 + n], ps[0:CH, 2 + g % 2, 0:DC * GT].rearrange("p (c t) -> p c t", c=DC)[:, :, 0:n], ACT.Copy).then_inc(xT_copied, 1)

                for g in range(NG):
                    t0, n = GROUPS[g]
                    act.wait_ge(conv_ready, g + 1)
                    if g >= 2:
                        act.wait_ge(h_ready, g - 1)
                    nc.scalar.activation(lin[0:n, g % 2, :], ps[0:n, g % 2, 0:DIM], ACT.Copy).then_inc(conv_copied, 1)
                    if g >= 1:
                        copy_T(g - 1)
                copy_T(NG - 1)

            @block.vector
            def _(dve):
                nc.vector.memset(P["xT"][CH:CH + 1, :, :], 1.0)

                def leaky_T(b):
                    dve.wait_ge(hT_copied, 2 * b + 2)
                    if b >= 2:
                        dve.wait_ge(samples_ready, 2 * (b - 1))
                    full, last = (NT - 1) * C1, slice((NT - 1) * C1, NT * C1)
                    nc.vector.scalar_tensor_tensor(hT[:, b % 2, 0:NT - 1, :].rearrange("p t c -> p (t c)"), ps[0:TILE, 6 + b % 2, 0:full], SLOPE, hT_lin[:, b % 2, 0:full], ALU.mult, ALU.max)
                    nc.vector.scalar_tensor_tensor(hT[0:LAST, b % 2, NT - 1, :], ps[0:LAST, 6 + b % 2, last], SLOPE, hT_lin[0:LAST, b % 2, last], ALU.mult, ALU.max).then_inc(hT_done, 1)

                def falls(b, t):
                    dve.wait_ge(dist_y_ready, NT * b + t + 1)
                    r = pixel_rows(t)
                    nc.vector.tensor_scalar(dist_y[0:r, t, :], dist_y[0:r, t, :], -1.0, 1.0, ALU.mult, ALU.add).then_inc(fall_ready, 1)

                def products(b, t):
                    dve.wait_ge(fall_ready, NT * b + t + 1)
                    r = pixel_rows(t)
                    if t == 0:
                        dve.wait_ge(hat_x_ready, b + 1)
                        if b >= 2:
                            dve.wait_ge(samples_ready, 2 * (b - 1))
                    nc.vector.scalar_tensor_tensor(weights[0:r, b % 2, t, :], dist_y[0:r, t, :], 0.0, hat_x[0:r, b % 2, :], ALU.max, ALU.mult).then_inc(weights_ready, 1)

                def all_weights(b):
                    falls(b, 0)
                    for t in range(NT):
                        if t + 1 < NT:
                            falls(b, t + 1)
                        products(b, t)

                leaky_T(0)
                all_weights(0)
                for b in range(1, B):
                    falls(b, 0)
                    leaky_T(b)
                    for t in range(NT):
                        if t + 1 < NT:
                            falls(b, t + 1)
                        products(b, t)

                for g in range(NG):
                    t0, n = GROUPS[g]
                    h = P["h"][0:n, g, :]
                    dve.wait_ge(conv_copied, g + 1)
                    nc.vector.scalar_tensor_tensor(h, ps[0:n, g % 2, 0:DIM], SLOPE, lin[0:n, g % 2, :], ALU.mult, ALU.max).then_inc(h_ready, 1)
                    dve.wait_ge(h_ready, g + 1)
                    nc.vector.bn_stats(stats[0:n, g, :], h).then_inc(stats_ready, 1)
                    dve.wait_ge(stats_ready, g + 1)
                    nc.vector.bn_aggr(mv[0:n, g, :], stats[0:n, g, :]).then_inc(mv_ready, 1)
                    dve.wait_ge(rstd_ready, g + 1)
                    if g >= 2:
                        dve.wait_ge(xT_ready, g - 1)
                    nc.vector.tensor_scalar(xhat[0:n, g % 2, :], h, mv[0:n, g, 0:1], rstd[0:n, g:g + 1], ALU.subtract, ALU.mult).then_inc(xhat_ready, 1)

            @block.gpsimd
            def _(pool):
                steps = Steps(pool, pool_step)
                for g in range(NG):
                    n = GROUPS[g][1]
                    pool.wait_ge(mv_ready, g + 1)
                    steps.done(nc.gpsimd.tensor_scalar(var_eps[0:n, g:g + 1], mv[0:n, g, 1:2], EPS, None, ALU.add))
                    steps.wait()
                    nc.gpsimd.tensor_tensor(rstd[0:n, g:g + 1], var_eps[0:n, g:g + 1], P["minus_half"][0:n, 0:1], ALU.pow).then_inc(rstd_ready, 1)


def stage_attention(nc, P, D, layer):
    hd = (64, 32)[layer]
    per = 128 // hd
    tiles = HEADS // per
    width = HEADS * hd
    scale = (64 ** -0.5, 16 ** -0.5)[layer]
    rows0 = CH + (layer == 0)
    HPU = 3
    UPG = HEADS // HPU
    NU = NG * UPG
    tag = f"a{layer}_"
    ctx = ExitStack()
    with ctx:
        def sb(name, shape, dt=F32):
            return ctx.enter_context(nc.sbuf_tensor(tag + name, shape, dt))

        def sem(name):
            return ctx.enter_context(nc.semaphore(tag + name))

        def unit(u):
            g, j = divmod(u, UPG)
            return g, j % per, HPU * (j // per)

        ps = P["ps"]
        wq = sb("wq", [rows0, DC, width])
        wk = sb("wk", [rows0, DC, width])
        wv = sb("wv", [rows0, DC, width])
        wo = sb("wo", [128, tiles, DIM])
        qT = sb("qT", [128, tiles, NTOK])
        kT = sb("kT", [128, tiles, NTOK])
        v = sb("v", [GT, NG, width])
        zT = sb("zT", [128, tiles, NTOK])
        peak = sb("peak", [GT, 4, HPU])
        minus_peak = sb("minus_peak", [GT, 4, HPU])
        probs = sb("probs", [GT, 3, HPU, GT])
        sums = sb("sums", [GT, 4, HPU])
        inv_sums = sb("inv_sums", [GT, 4, HPU])
        probs_n = sb("probs_n", [GT, 2, HPU, GT])
        probs_T = sb("probs_T", [GT, 2, HPU, GT])
        stats = sb("stats", [GT, 2, NG, 6])
        mv = sb("mv", [GT, 2, NG, 2])
        var_eps = sb("var_eps", [GT, 2, NG])
        rstd = sb("rstd", [GT, 2, NG])
        xhat = sb("xhat", [GT, 2, DIM])
        affine = sb("affine", [CH, 2, DC])
        if layer == 0:
            ob = sb("ob", [GT, DIM])
        else:
            wr = sb("wr", [CH, DC, EXPERTS])
            logits = sb("logits", [GT, NG, EXPERTS])
            top = sb("top", [GT, NG, 8])
            top_at = sb("top_at", [GT, NG, 8], U32)
            top_f = sb("top_f", [GT, NG, 2])
            gap = sb("gap", [GT, NG])
            second = sb("second", [GT, NG])
            total = sb("total", [GT, NG])
            share = sb("share", [GT, 2, NG])
            pick = sb("pick", [GT, 2, NG, EXPERTS])

        loaded = sem("loaded")
        proj_ready = sem("proj_ready")
        proj_act = sem("proj_act")
        proj_dve = sem("proj_dve")
        scores_ready = sem("scores_ready")
        peak_ready = sem("peak_ready")
        minus_peak_ready = sem("minus_peak_ready")
        probs_ready = sem("probs_ready")
        inv_sums_ready = sem("inv_sums_ready")
        probs_n_ready = sem("probs_n_ready")
        probs_T_ready = sem("probs_T_ready")
        probs_T_copied = sem("probs_T_copied")
        z_ready = sem("z_ready")
        z_copied = sem("z_copied")
        o_ready = sem("o_ready")
        base_ready = sem("base_ready")
        sum_ready = sem("sum_ready")
        norm_step = sem("norm_step")
        mv_ready = sem("mv_ready")
        rstd_ready = sem("rstd_ready")
        pool_step = sem("pool_step")
        x_ready = sem("x_ready")
        xhat_ready = sem("xhat_ready")
        xT_ready = sem("xT_ready")
        xT_copied = sem("xT_copied")
        logits_ready = sem("logits_ready")
        route_step = sem("route_step")
        gap_ready = sem("gap_ready")
        second_ready = sem("second_ready")
        NORMS = 2 - layer
        n_loads = 7 if layer == 0 else 7
        TAIL = range(-3, NU + 8)

        PROJ = [(w, i) for i in range(tiles) for w in "qk"] + [("v", g) for g in range(NG)]
        cut = width // 2 if width > 512 else width

        def proj_copied(eng, u):
            eng.wait_ge((proj_act, proj_dve)[u % 2], u // 2 + 1)

        def proj_views(u):
            w, i = PROJ[u]
            bank = 2 * (u % 3)
            if w == "v":
                t0, n = GROUPS[i]
                return ps[0:n, bank:bank + width // cut, 0:cut], v[0:n, i, :].rearrange("p (a c) -> p a c", c=cut)
            return ps[:, bank:bank + 2, 0:HALF], (qT if w == "q" else kT)[:, i, :].rearrange("p (a c) -> p a c", a=2)

        with nc.Block() as block:
            @block.sync
            def _(sp):
                for name, tile in (("wq", wq), ("wk", wk), ("wv", wv)):
                    sp.dma_start(tile[0:CH, :, :], D[tag + name]).then_inc(loaded, 16)
                    if layer == 0:
                        sp.dma_start(tile[CH:CH + 1, 0, :], D[tag + name + "_bias"]).then_inc(loaded, 16)
                sp.dma_start(wo[:, :, :], D[tag + "wo"]).then_inc(loaded, 16)
                sp.dma_start(affine[:, :, :], D[tag + "affine"]).then_inc(loaded, 16)
                if layer == 0:
                    sp.dma_start(ob[:, :], D["ob"].to_broadcast((GT, DIM))).then_inc(loaded, 16)
                else:
                    sp.dma_start(wr[:, :, :], D["wr"]).then_inc(loaded, 16)

            LOADS = 16 * (9 if layer == 0 else 6)

            @block.tensor
            def _(pe):
                pe.wait_ge(loaded, LOADS)
                for u, (w, i) in enumerate(PROJ):
                    if u >= 3:
                        proj_copied(pe, u - 3)
                    bank = 2 * (u % 3)
                    for a in range(width // cut if w == "v" else 2):
                        for c in range(DC):
                            r = rows0 if c == 0 else CH
                            if w == "v":
                                t0, n = GROUPS[i]
                                ins = nc.tensor.matmul(ps[0:n, bank + a, 0:cut], P["xT"][0:r, c, t0:t0 + n], wv[0:r, c, a * cut:(a + 1) * cut], start=(c == 0), stop=(c == DC - 1))
                            else:
                                ins = nc.tensor.matmul(ps[:, bank + a, 0:HALF], (wq if w == "q" else wk)[0:r, c, i * 128:(i + 1) * 128], P["xT"][0:r, c, a * HALF:(a + 1) * HALF], start=(c == 0), stop=(c == DC - 1))
                    ins.then_inc(proj_ready, 1)
                for u in range(len(PROJ) - 3, len(PROJ)):
                    proj_copied(pe, u)

                def scores(u):
                    g, r, i0 = unit(u)
                    t0, n = GROUPS[g]
                    part = slice(r * hd, (r + 1) * hd)
                    if u >= 3:
                        pe.wait_ge(probs_ready, HPU * (u - 2))
                    masked = n > TPI
                    if masked:
                        nc.tensor.matmul(ps[0:n, u % 3, 0:HPU * n], P["mask_q"][part, 0:n], P["mask_k"][part, 0:HPU * n], start=True, stop=False)
                    for j in range(HPU):
                        ins = nc.tensor.matmul(ps[0:n, u % 3, j * n:(j + 1) * n], qT[part, i0 + j, t0:t0 + n], kT[part, i0 + j, t0:t0 + n], start=not masked, stop=(not masked or j == HPU - 1))
                    ins.then_inc(scores_ready, 1)

                def transposes(u):
                    g, r, i0 = unit(u)
                    n = GROUPS[g][1]
                    pe.wait_ge(probs_n_ready, u + 1)
                    if u >= 2:
                        pe.wait_ge(probs_T_copied, u - 1)
                    for j in range(HPU):
                        ins = nc.tensor.transpose(ps[0:n, 3 + u % 2, j * n:(j + 1) * n], probs_n[0:n, u % 2, j, 0:n], P["ident"][0:n, 0:n])
                    ins.then_inc(probs_T_ready, 1)

                def values(u):
                    g, r, i0 = unit(u)
                    n = GROUPS[g][1]
                    pe.wait_ge(probs_T_copied, u + 1)
                    if u >= 1:
                        pe.wait_ge(z_copied, u)
                    for j in range(HPU):
                        h = (i0 + j) * per + r
                        ins = nc.tensor.matmul(ps[r * hd:(r + 1) * hd, 5, j * n:(j + 1) * n], v[0:n, g, h * hd:(h + 1) * hd], probs_T[0:n, u % 2, j, 0:n], start=True, stop=True)
                    ins.then_inc(z_ready, 1)

                def output(g):
                    t0, n = GROUPS[g]
                    pe.wait_ge(z_copied, UPG * (g + 1))
                    if g >= 1:
                        pe.wait_ge(sum_ready, g)
                    for i in range(tiles):
                        ins = nc.tensor.matmul(ps[0:n, 6, 0:DIM], zT[:, i, t0:t0 + n], wo[:, i, :], start=(i == 0), stop=(i == tiles - 1))
                    ins.then_inc(o_ready, 1)

                def transpose_x(g):
                    n = GROUPS[g][1]
                    pe.wait_ge(xhat_ready, g + 1)
                    if g >= 1:
                        pe.wait_ge(xT_copied, DC * g)
                    for c in range(DC):
                        ins = nc.tensor.transpose(ps[0:CH, 7, c * n:(c + 1) * n], xhat[0:n, g % 2, c * CH:(c + 1) * CH], P["ident"][0:n, 0:n])
                    ins.then_inc(xT_ready, 1)

                for u in TAIL:
                    if 0 <= u < NU:
                        transposes(u)
                    if 0 <= u - 1 < NU:
                        values(u - 1)
                    if 0 <= u + 3 < NU:
                        scores(u + 3)
                    if u >= 5 and (u - 5) % UPG == 0 and (u - 5) // UPG < NG:
                        output((u - 5) // UPG)
                    if u >= 9 and (u - 9) % UPG == 0 and (u - 9) // UPG < NG:
                        transpose_x((u - 9) // UPG)
                for g in range(NG):
                    if UPG * g + 9 >= NU + 8:
                        transpose_x(g)

                if layer == 1:
                    pe.wait_ge(xT_copied, DC * NG)
                    for g in range(NG):
                        t0, n = GROUPS[g]
                        for c in range(DC):
                            ins = nc.tensor.matmul(ps[0:n, g % 2, g * EXPERTS:(g + 1) * EXPERTS], P["xT"][0:CH, c, t0:t0 + n], wr[:, c, :], start=(c == 0), stop=(c == DC - 1))
                        ins.then_inc(logits_ready, 1)

            @block.scalar
            def _(act):
                for u in range(0, len(PROJ), 2):
                    act.wait_ge(proj_ready, u + 1)
                    src, dst = proj_views(u)
                    nc.scalar.activation(dst, src, ACT.Copy).then_inc(proj_act, 1)

                def exps(u):
                    g, r, i0 = unit(u)
                    n = GROUPS[g][1]
                    act.wait_ge(minus_peak_ready, u + 1)
                    if u >= 3:
                        act.wait_ge(probs_n_ready, u - 2)
                    if u >= 4:
                        act.wait_ge(inv_sums_ready, u - 3)
                    for j in range(HPU):
                        nc.scalar.activation(probs[0:n, u % 3, j, 0:n], ps[0:n, u % 3, j * n:(j + 1) * n], ACT.Exp, bias=minus_peak[0:n, u % 4, j:j + 1], scale=scale,
                                             accum_out=sums[0:n, u % 4, j:j + 1]).then_inc(probs_ready, 1)

                def copy_z(u):
                    g, r, i0 = unit(u)
                    t0, n = GROUPS[g]
                    part = slice(r * hd, (r + 1) * hd)
                    act.wait_ge(z_ready, u + 1)
                    nc.scalar.activation(zT[part, i0:i0 + HPU, t0:t0 + n], ps[part, 5, 0:HPU * n].rearrange("p (j t) -> p j t", j=HPU), ACT.Copy).then_inc(z_copied, 1)

                def copy_xT(g):
                    t0, n = GROUPS[g]
                    act.wait_ge(xT_ready, g + 1)
                    for c in range(DC):
                        nc.scalar.activation(P["xT"][0:CH, c, t0:t0 + n], ps[0:CH, 7, c * n:(c + 1) * n], ACT.Identity, bias=affine[:, 1, c:c + 1], scale=affine[:, 0, c:c + 1]).then_inc(xT_copied, 1)

                act.wait_ge(loaded, LOADS)
                for u in TAIL:
                    if 0 <= u + 2 < NU:
                        exps(u + 2)
                    if 0 <= u - 1 < NU:
                        copy_z(u - 1)
                    if u >= 9 and (u - 9) % UPG == 0 and (u - 9) // UPG < NG:
                        copy_xT((u - 9) // UPG)
                for g in range(NG):
                    if UPG * g + 9 >= NU + 8:
                        copy_xT(g)
                if layer == 1:
                    act.wait_ge(gap_ready, 1)
                    nc.scalar.activation(second[:, :], gap[:, :], ACT.Exp).then_inc(second_ready, 1)

            @block.vector
            def _(dve):
                for u in range(1, len(PROJ), 2):
                    dve.wait_ge(proj_ready, u + 1)
                    src, dst = proj_views(u)
                    nc.vector.tensor_copy(dst, src).then_inc(proj_dve, 1)
                steps = Steps(dve, norm_step)

                def peaks(u):
                    g, r, i0 = unit(u)
                    n = GROUPS[g][1]
                    dve.wait_ge(scores_ready, u + 1)
                    nc.vector.reduce_max(peak[0:n, u % 4, :], ps[0:n, u % 3, 0:HPU * n].rearrange("p (j t) -> p j t", j=HPU), axis=AX.X).then_inc(peak_ready, 1)
                    dve.wait_ge(peak_ready, u + 1)
                    if u >= 4:
                        dve.wait_ge(probs_ready, HPU * (u - 3))
                    nc.vector.tensor_scalar(minus_peak[0:n, u % 4, :], peak[0:n, u % 4, :], -scale, None, ALU.mult).then_inc(minus_peak_ready, 1)

                def inverse(u):
                    n = GROUPS[unit(u)[0]][1]
                    dve.wait_ge(probs_ready, HPU * (u + 1))
                    if u >= 4:
                        dve.wait_ge(probs_n_ready, u - 3)
                    nc.vector.reciprocal(inv_sums[0:n, u % 4, :], sums[0:n, u % 4, :]).then_inc(inv_sums_ready, 1)

                def copy_T(u):
                    n = GROUPS[unit(u)[0]][1]
                    dve.wait_ge(probs_T_ready, u + 1)
                    if u >= 2:
                        dve.wait_ge(z_ready, u - 1)
                    nc.vector.tensor_copy(probs_T[0:n, u % 2, :, 0:n], ps[0:n, 3 + u % 2, 0:HPU * n].rearrange("p (j t) -> p j t", j=HPU)).then_inc(probs_T_copied, 1)

                def norm_stats(src, k, g):
                    n = GROUPS[g][1]
                    steps.done(nc.vector.bn_stats(stats[0:n, k, g, :], src))
                    steps.wait()
                    nc.vector.bn_aggr(mv[0:n, k, g, :], stats[0:n, k, g, :]).then_inc(mv_ready, 1)

                def tail(g, step):
                    n = GROUPS[g][1]
                    h, x, rest = P["h"][0:n, g, :], P["x"][0:n, g, :], P["rest"][0:n, g, :]
                    src = h if layer == 0 else x
                    if step == 0:
                        dve.wait_ge(o_ready, g + 1)
                        if layer == 0:
                            dve.wait_ge(base_ready, g + 1)
                        nc.vector.tensor_tensor(src, ps[0:n, 6, 0:DIM], src, ALU.add).then_inc(sum_ready, 1)
                        dve.wait_ge(sum_ready, g + 1)
                        norm_stats(src, 0, g)
                    if step == 1 and layer == 0:
                        dve.wait_ge(rstd_ready, NORMS * g + 1)
                        nc.vector.tensor_scalar(x, h, mv[0:n, 0, g, 0:1], rstd[0:n, 0, g:g + 1], ALU.subtract, ALU.mult).then_inc(x_ready, 1)
                        dve.wait_ge(x_ready, g + 1)
                        norm_stats(x, 1, g)
                    if step == 2:
                        k = NORMS - 1
                        dve.wait_ge(rstd_ready, NORMS * (g + 1))
                        if g >= 2:
                            dve.wait_ge(xT_ready, g - 1)
                        nc.vector.tensor_scalar(xhat[0:n, g % 2, :], x, mv[0:n, k, g, 0:1], rstd[0:n, k, g:g + 1], ALU.subtract, ALU.mult).then_inc(xhat_ready, 1)

                done = set()

                def tails(u):
                    for g in range(NG):
                        for step in range(3):
                            if UPG * g + 6 + step <= u and (g, step) not in done:
                                done.add((g, step))
                                tail(g, step)

                for u in TAIL:
                    if 0 <= u < NU:
                        copy_T(u)
                    if 0 <= u + 3 < NU:
                        peaks(u + 3)
                    if 0 <= u + 2 < NU:
                        inverse(u + 2)
                    tails(u)
                tails(10 ** 6)

                if layer == 1:
                    route = Steps(dve, route_step)
                    route.done(nc.vector.memset(logits[:, :, :], 0.0))
                    dve.wait_ge(logits_ready, NG)
                    route.wait()
                    for g in range(NG):
                        n = GROUPS[g][1]
                        route.done(nc.vector.tensor_copy(logits[0:n, g, :], ps[0:n, g % 2, g * EXPERTS:(g + 1) * EXPERTS]))
                    route.wait()
                    for g in range(NG):
                        route.done(nc.vector.max(top[:, g, :], logits[:, g, :]))
                    route.wait()
                    for g in range(NG):
                        route.done(nc.vector.max_index(top_at[:, g, :], top[:, g, :], logits[:, g, :]))
                    nc.vector.tensor_tensor(gap[:, :], top[:, :, 1], top[:, :, 0], ALU.subtract).then_inc(gap_ready, 1)
                    route.wait()
                    route.done(nc.vector.tensor_copy(top_f[:, :, :], top_at[:, :, 0:2]))
                    dve.wait_ge(second_ready, 1)
                    route.done(nc.vector.tensor_scalar(total[:, :], second[:, :], 1.0, None, ALU.add))
                    route.wait()
                    route.done(nc.vector.reciprocal(share[:, 0, :], total[:, :]))
                    route.wait()
                    route.done(nc.vector.tensor_tensor(share[:, 1, :], second[:, :], share[:, 0, :], ALU.mult))
                    for k in range(2):
                        route.done(nc.vector.tensor_tensor(pick[:, k, :, :], P["iota"][:, :, :], top_f[:, :, k:k + 1].to_broadcast((GT, NG, EXPERTS)), ALU.is_equal))
                    route.wait()
                    for k in range(2):
                        route.done(nc.vector.tensor_tensor(pick[:, k, :, :], pick[:, k, :, :], share[:, k, :].unsqueeze(2).to_broadcast((GT, NG, EXPERTS)), ALU.mult))
                    route.wait()
                    route.done(nc.vector.tensor_tensor(P["gates"][:, :, :], pick[:, 0, :, :], pick[:, 1, :, :], ALU.add))

            @block.gpsimd
            def _(pool):
                steps = Steps(pool, pool_step)
                if layer == 0:
                    pool.wait_ge(loaded, LOADS)
                    for g in range(NG):
                        n = GROUPS[g][1]
                        nc.gpsimd.tensor_tensor(P["h"][0:n, g, :], P["h"][0:n, g, :], ob[0:n, :], ALU.add).then_inc(base_ready, 1)

                def normalise(u):
                    n = GROUPS[unit(u)[0]][1]
                    pool.wait_ge(inv_sums_ready, u + 1)
                    if u >= 2:
                        pool.wait_ge(probs_T_ready, u - 1)
                    nc.gpsimd.tensor_tensor(probs_n[0:n, u % 2, :, 0:n], probs[0:n, u % 3, :, 0:n], inv_sums[0:n, u % 4, :].unsqueeze(2).to_broadcast((n, HPU, n)), ALU.mult).then_inc(probs_n_ready, 1)

                def inverse_deviation(g, k):
                    n = GROUPS[g][1]
                    pool.wait_ge(mv_ready, NORMS * g + k + 1)
                    steps.done(nc.gpsimd.tensor_scalar(var_eps[0:n, k, g:g + 1], mv[0:n, k, g, 1:2], EPS, None, ALU.add))
                    steps.wait()
                    nc.gpsimd.tensor_tensor(rstd[0:n, k, g:g + 1], var_eps[0:n, k, g:g + 1], P["minus_half"][0:n, 0:1], ALU.pow).then_inc(rstd_ready, 1)
                    if k == 0:
                        pass

                done = set()
                for u in list(TAIL) + [10 ** 6]:
                    if 0 <= u + 2 < NU:
                        normalise(u + 2)
                    for g in range(NG):
                        for k in range(NORMS):
                            if UPG * g + 6 + k <= u and (g, k) not in done:
                                done.add((g, k))
                                inverse_deviation(g, k)
                for g in range(NG):
                    n = GROUPS[g][1]
                    if layer == 1:
                        pool.wait_ge(sum_ready, g + 1)
                        nc.gpsimd.tensor_tensor(P["rest"][0:n, g, :], P["h"][0:n, g, :], P["x"][0:n, g, :], ALU.add)


def stage_experts(nc, P, D, out):
    ctx = ExitStack()
    with ctx:
        def sb(name, shape, dt=F32):
            return ctx.enter_context(nc.sbuf_tensor(name, shape, dt))

        def sem(name):
            return ctx.enter_context(nc.semaphore(name))

        ps = P["ps"]
        w1 = sb("w1", [CH, 2, DC, FF])
        w2 = sb("w2", [128, 2, FT, DIM])
        hidden = sb("hidden", [128, 2, FT, NTOK])

        w1_loaded = [sem(f"w1_loaded{i}") for i in range(2)]
        w2_loaded = [sem(f"w2_loaded{i}") for i in range(2)]
        up_ready = sem("up_ready")
        hidden_ready = sem("hidden_ready")
        down_ready = sem("down_ready")
        added = sem("added")
        stored = sem("stored")

        with nc.Block() as block:
            @block.sync
            def _(sp):
                for e in range(EXPERTS):
                    if e >= 2:
                        sp.wait_ge(up_ready, FT * (e - 1))
                    sp.dma_start(w1[:, e % 2, :, :], D["w1"][e, :, :, :]).then_inc(w1_loaded[e % 2], 16)
                    if e >= 2:
                        sp.wait_ge(down_ready, NG * (e - 1))
                    sp.dma_start(w2[:, e % 2, :, :], D["w2"][e, :, :, :]).then_inc(w2_loaded[e % 2], 16)
                for g, (t0, n) in enumerate(GROUPS):
                    sp.wait_ge(added, NG * (EXPERTS - 1) + g + 1)
                    sp.dma_start(out[t0:t0 + n, :], P["rest"][0:n, g, :]).then_inc(stored, 16)
                sp.wait_ge(stored, 16 * NG)

            @block.tensor
            def _(pe):
                def up(e):
                    pe.wait_ge(w1_loaded[e % 2], 16 * (e // 2 + 1))
                    for f in range(FT):
                        u = FT * e + f
                        if u >= 2:
                            pe.wait_ge(hidden_ready, u - 1)
                        for a in range(2):
                            for c in range(DC):
                                ins = nc.tensor.matmul(ps[:, 2 * (u % 2) + a, 0:HALF], w1[:, e % 2, c, f * 128:(f + 1) * 128], P["xT"][0:CH, c, a * HALF:(a + 1) * HALF], start=(c == 0), stop=(c == DC - 1))
                        ins.then_inc(up_ready, 1)

                def down(e):
                    pe.wait_ge(w2_loaded[e % 2], 16 * (e // 2 + 1))
                    pe.wait_ge(hidden_ready, FT * (e + 1))
                    for g, (t0, n) in enumerate(GROUPS):
                        u = NG * e + g
                        if u >= 4:
                            pe.wait_ge(added, u - 3)
                        for f in range(FT):
                            ins = nc.tensor.matmul(ps[0:n, 4 + u % 4, 0:DIM], hidden[:, e % 2, f, t0:t0 + n], w2[:, e % 2, f, :], start=(f == 0), stop=(f == FT - 1))
                        ins.then_inc(down_ready, 1)

                up(0)
                for e in range(EXPERTS):
                    if e + 1 < EXPERTS:
                        up(e + 1)
                    down(e)

            @block.scalar
            def _(act):
                for e in range(EXPERTS):
                    for f in range(FT):
                        u = FT * e + f
                        act.wait_ge(up_ready, u + 1)
                        if e >= 2:
                            act.wait_ge(down_ready, NG * (e - 1))
                        nc.scalar.activation(hidden[:, e % 2, f, :].rearrange("p (a t) -> p a t", a=2), ps[:, 2 * (u % 2):2 * (u % 2) + 2, 0:HALF], ACT.Gelu).then_inc(hidden_ready, 1)

            @block.vector
            def _(dve):
                for e in range(EXPERTS):
                    for g, (t0, n) in enumerate(GROUPS):
                        u = NG * e + g
                        dve.wait_ge(down_ready, u + 1)
                        if e >= 1:
                            dve.wait_ge(added, u - NG + 1)
                        nc.vector.scalar_tensor_tensor(P["rest"][0:n, g, :], ps[0:n, 4 + u % 4, 0:DIM], P["gates"][0:n, g, e:e + 1], P["rest"][0:n, g, :], ALU.mult, ALU.add).then_inc(added, 1)


def build(nc, D, out):
    ctx = ExitStack()
    with ctx:
        def sb(name, shape, dt=F32):
            return ctx.enter_context(nc.sbuf_tensor(name, shape, dt))

        P = {"ps": ctx.enter_context(nc.psum_tensor("ps", [128, 8, 512], F32))}
        P["ident"] = sb("ident", [128, 128])
        P["minus_half"] = sb("minus_half", [128, 1])
        P["row_shift"] = sb("row_shift", [128, NT + 1])
        P["mask_q"] = sb("mask_q", [128, GT], BF16)
        P["mask_k"] = sb("mask_k", [128, IPG * GT], BF16)
        P["iota"] = sb("iota", [GT, NG, EXPERTS])
        P["gates"] = sb("gates", [GT, NG, EXPERTS])
        for name in ("h", "x", "rest"):
            P[name] = sb(name, [GT, NG, DIM])
        P["xT"] = sb("xT", [CH + 1, DC, NTOK])
        with ExitStack() as early:
            def eb(name, shape, dt=F32):
                return early.enter_context(nc.sbuf_tensor(name, shape, dt))

            P["stem_w"] = eb("stem_w", [KPATCH + 1, C1])
            P["parts"] = eb("parts", [C1 + 3, NTOK], BF16)
            P["spread"] = eb("spread_bf", [C1 + 3, 2, TAPS, 128], BF16)
            P["patches"] = eb("patches", [KPATCH + 1, B, PIX])
            P["dcn_w"] = eb("dcn_w", [C1 + 1, TAPS, DIM])
            samples_ctx = ExitStack()
            P["samples"] = eb("samples", [C1 + 1, TAPS, NTOK])
            stage_constants(nc, P, D)
            stage_offsets(nc, P, D)
            stage_sampling(nc, P, D)
        stage_attention(nc, P, D, 0)
        stage_attention(nc, P, D, 1)
        stage_experts(nc, P, D, out)


def stage_constants(nc, P, D):
    ctx = ExitStack()
    with ctx:
        mask_raw = ctx.enter_context(nc.sbuf_tensor("mask_raw", [128, GT + IPG * GT], F32))
        const_loaded = ctx.enter_context(nc.semaphore("const_loaded"))
        with nc.Block() as block:
            @block.sync
            def _(sp):
                sp.dma_start(P["ident"][:, :], D["ident"]).then_inc(const_loaded, 16)
                sp.dma_start(P["row_shift"][:, :], D["row_shift"]).then_inc(const_loaded, 16)
                sp.dma_start(P["iota"][:, :, :], D["iota"]).then_inc(const_loaded, 16)
                sp.dma_start(mask_raw[:, :], D["mask"]).then_inc(const_loaded, 16)

            @block.vector
            def _(dve):
                nc.vector.memset(P["minus_half"][:, :], -0.5)
                dve.wait_ge(const_loaded, 16 * 4)
                nc.vector.tensor_copy(P["mask_q"][:, :], mask_raw[:, 0:GT])
                nc.vector.tensor_copy(P["mask_k"][:, :], mask_raw[:, GT:])


def constants():
    import numpy as np
    grid = np.ones((3, B, SIDE2, SIDE2), np.float32)
    grid[1] = KS * np.arange(SIDE2)[None, :, None]
    grid[2] = KS * np.arange(SIDE2)[None, None, :]
    spread = np.zeros((C1 + 3, 2, TAPS, 128), np.float32)
    p = np.arange(128)
    for k in range(TAPS):
        for axis, tap, at in ((0, k // KS, p // SIDE), (1, k % KS, p % SIDE)):
            for part in range(3):
                spread[32 * part + 2 * k + axis, axis, k, :] = 1
            spread[C1, axis, k, :] = tap - at
            spread[C1 + 1 + axis, axis, k, :] = 1
    row_shift = np.ones((128, NT + 1), np.float32)
    row_shift[:, 0:NT] = -ROWS * np.arange(NT)
    mask_q, mask_k = np.zeros((128, GT), np.float32), np.zeros((128, IPG, GT), np.float32)
    image = np.arange(GT) // TPI
    for base in range(0, 128, 32):
        mask_q[base], mask_k[base] = 1, -BIG
        for i in range(IPG):
            mask_q[base + 1 + i], mask_k[base + 1 + i] = image == i, BIG * (image == i)
    bias_row = np.zeros((KPATCH + 1, 1), np.float32)
    bias_row[KPATCH] = 1
    iota = np.broadcast_to(np.arange(EXPERTS, dtype=np.float32), (GT, NG, EXPERTS))
    return {"grid": grid.reshape(3, NTOK), "spread": spread, "row_shift": row_shift, "bias_row": bias_row, "iota": iota, "ident": np.eye(128, dtype=np.float32),
            "mask": np.concatenate([mask_q, mask_k.reshape(128, IPG * GT)], 1)}


def layouts(I):
    import numpy as np

    def chunks(w):
        return w.reshape(DC, CH, -1).transpose(1, 0, 2)

    t = {n: np.asarray(a) for n, a in I.items()}
    tok = {n[len("L0_tok_"):]: a for n, a in t.items() if n.startswith("L0_tok_")}
    att = {n[len("L0_attn_"):]: a for n, a in t.items() if n.startswith("L0_attn_")}
    ffn = {n[len("L0_ffn_"):]: a for n, a in t.items() if n.startswith("L0_ffn_")}
    d = {
        "patches": t["x"].reshape(B, CIN, SIDE, KS, SIDE, KS).transpose(1, 3, 5, 0, 2, 4).reshape(KPATCH, B, PIX),
        "stem_w": tok["stem_w"].reshape(C1, KPATCH).T,
        "stem_par": np.stack([tok[n] for n in ("stem_b", "bn1_g", "bn1_b", "bn1_m", "bn1_v")]),
        "off_w": tok["off_w"].reshape(2 * TAPS, C1, TAPS).transpose(1, 2, 0),
        "off_b": tok["off_b"].reshape(2 * TAPS, 1),
        "dcn_w": tok["dcn_w"].reshape(DIM, C1, TAPS).transpose(1, 2, 0),
        "dcn_par": np.stack([tok[n] for n in ("dcn_b", "bn2_g", "bn2_b", "bn2_m", "bn2_v")]),
        "ob": att["Ob"].reshape(1, DIM),
        "a0_wo": att["O"].reshape(HEADS // 2, 128, DIM).transpose(1, 0, 2),
        "a0_affine": np.stack([ffn["ln1_g"].reshape(DC, CH).T, ffn["ln1_b"].reshape(DC, CH).T], 1),
        "a1_affine": np.stack([ffn["ln2_g"].reshape(DC, CH).T, ffn["ln2_b"].reshape(DC, CH).T], 1),
        "wr": chunks(ffn["Wrouter"]),
        "w1": ffn["W1"].reshape(EXPERTS, DC, CH, FF).transpose(0, 2, 1, 3),
        "w2": ffn["W2"].reshape(EXPERTS, FT, 128, DIM).transpose(0, 2, 1, 3),
    }
    for name, w, b in (("wq", "Qs", "Qbs"), ("wk", "Ks", "Kbs"), ("wv", "Vs", "Vbs")):
        d["a0_" + name] = chunks(att[w].transpose(1, 0, 2).reshape(DIM, -1))
        d["a0_" + name + "_bias"] = att[b].reshape(1, -1)
    qkv = np.zeros((3, DIM, HEADS, 32), ffn["Wqkv"].dtype)
    qkv[:, :, :, 0:16] = ffn["Wqkv"].reshape(DIM, 3, HEADS, 16).transpose(1, 0, 2, 3)
    for i, name in enumerate(("wq", "wk", "wv")):
        d["a1_" + name] = chunks(qkv[i].reshape(DIM, -1))
    proj = np.zeros((HEADS, 32, DIM), ffn["Wproj"].dtype)
    proj[:, 0:16] = ffn["Wproj"].reshape(HEADS, 16, DIM)
    d["a1_wo"] = proj.reshape(HEADS // 4, 128, DIM).transpose(1, 0, 2)
    return d


def kernel(**inputs):
    import numpy as np
    import concourse.bacc as bacc
    from concourse.bass_utils import run_bass_kernel_spmd

    nc = bacc.Bacc("TRN2", target_bir_lowering=False, num_devices=1)
    arrays, D = {}, {}
    for name, a in {**constants(), **layouts(inputs)}.items():
        arrays["in_" + name] = np.ascontiguousarray(a)
        D[name] = nc.dram_tensor("in_" + name, arrays["in_" + name].shape, mybir.dt.from_np(arrays["in_" + name].dtype), kind="ExternalInput").ap()
    out = nc.dram_tensor("out", (NTOK, DIM), F32, kind="ExternalOutput").ap()
    build(nc, D, out)
    r = run_bass_kernel_spmd(nc, [arrays], core_ids=[0])
    return r.results[0]["out"].reshape(B, TPI, DIM)
```

```python
import math
import concourse.bass as bass
from concourse import mybir
from contextlib import ExitStack

F32 = mybir.dt.float32
F32R = mybir.dt.float32r
BF16 = mybir.dt.bfloat16
U32 = mybir.dt.uint32
ALU = mybir.AluOpType
ACT = mybir.ActivationFunctionType
AX = mybir.AxisListType

B, CIN, IMG = 16, 3, 96
KS = 4
SIDE = IMG // KS
PIX = SIDE * SIDE
HALF = PIX // 2
C1 = 96
TAPS = KS * KS
SIDE2 = SIDE // KS
TPI = SIDE2 * SIDE2
NTOK = B * TPI
KPATCH = CIN * TAPS
DIM = 192
DC = 2
WIDE = 256
WIDE_PARTS = ((slice(0, DIM), slice(0, DIM)), (slice(128, DIM), slice(DIM, WIDE)))
WARM = 40
FILL = 5
FILL_END = (6, 6)
FILL_UNIT = (2, 4)
LOW = 64
RAW = 4
BLOCK = 32
SLOTS = TAPS * C1 // 128
ROWS = 5
TILE = ROWS * SIDE
NT = -(-SIDE // ROWS)
LAST = PIX - (NT - 1) * TILE
IPG = 3
GT = IPG * TPI
GROUPS = [(g * GT, min(GT, NTOK - g * GT)) for g in range(-(-NTOK // GT))]
NG = len(GROUPS)
XTILES = [(t * 128, min(128, NTOK - t * 128)) for t in range(-(-NTOK // 128))]
XT = len(XTILES)
HEADS = 12
FF = 768
EXPERTS = 8
FT = FF // 128
EPS = 1e-5
SLOPE = 0.01
QUAD = 4
BIG = 2.0 ** 100


class Steps:

    def __init__(self, eng, sem):
        self.eng, self.sem, self.n = eng, sem, 0

    def done(self, ins):
        ins.then_inc(self.sem, 1)
        self.n += 1
        return self.n

    def wait(self, n=None):
        self.eng.wait_ge(self.sem, self.n if n is None else n)


def pixel_rows(t):
    return TILE if t < NT - 1 else LAST


def inverse_root(dve, steps, var, root, out, tmp):
    steps.done(dve.reciprocal(out, root))
    steps.wait()
    steps.done(dve.tensor_tensor(tmp, out, out, ALU.mult))
    steps.wait()
    steps.done(dve.tensor_tensor(tmp, tmp, var, ALU.mult))
    steps.wait()
    steps.done(dve.tensor_scalar(tmp, tmp, -0.5, 1.5, ALU.mult, ALU.add))
    steps.wait()
    steps.done(dve.tensor_tensor(out, out, tmp, ALU.mult))
    steps.wait()


def split_x(dve, P, xT, g, copied, n_copied, hi_done, split_done):
    t0, n = XTILES[g]
    cols = slice(t0, t0 + n)
    full, hi, lo = xT[:, g % 2, :, 0:n], P["x_hi"][:, :, cols], P["x_lo"]
    dve.wait_ge(copied, n_copied)
    dve.tensor_copy(hi, full).then_inc(hi_done, 1)
    dve.wait_ge(hi_done, g + 1)
    dve.tensor_tensor(lo[:, 0, cols], full[:, 0, :], hi[:, 0, :].bitcast(F32), ALU.subtract).then_inc(split_done, 1)
    dve.tensor_tensor(lo[0:64, 1, cols], full[0:64, 1, :], hi[0:64, 1, :].bitcast(F32), ALU.subtract).then_inc(split_done, 1)


def split_w(eng, raw, hi, lo, steps):
    steps.done(eng.tensor_copy(hi, raw))
    steps.wait()
    steps.done(eng.tensor_tensor(lo, raw[:, 0, :], hi[:, 0, :].bitcast(F32), ALU.subtract))
    steps.done(eng.tensor_tensor(hi[64:128, 1, :], raw[64:128, 1, :], hi[64:128, 1, :].bitcast(F32), ALU.subtract))


def five(w_hi, w_lo, x_hi, x_lo):
    return ((w_hi[:, 0, :], x_hi[:, 0, :]), (w_lo, x_hi[:, 0, :]), (w_hi[:, 0, :], x_lo[:, 0, :]),
            (w_hi[:, 1, :], x_hi[:, 1, :]), (w_hi[:, 1, :], x_lo[:, 1, :]))


def pack_samples(sp, P, g):
    t0, n = XTILES[g]
    for block in range(C1 // BLOCK):
        sp.dma_start(P["samples"][C1:128, block::C1 // BLOCK, t0:t0 + n], P["extra"][block * BLOCK:(block + 1) * BLOCK, :, t0:t0 + n]).then_inc(P["packed"][g], 16)


def stage_images(nc, P, D):
    ctx = ExitStack()
    with ctx:
        def sb(name, shape, dt=F32):
            return ctx.enter_context(nc.sbuf_tensor(name, shape, dt))

        def sem(name):
            return ctx.enter_context(nc.semaphore(name))

        ps = P["ps"]
        NQ = B // QUAD
        RING = NT + 1
        POOL_T = 2
        PRING = 3
        DRING = 5
        stem_raw = sb("stem_raw", [KPATCH + 1, C1])
        stem_hi = sb("stem_hi", [LOW + KPATCH + 1, C1], F32R)
        stem_lo = sb("stem_lo", [KPATCH + 1, C1], F32R)
        stem_par = sb("stem_par", [KPATCH + 1, 4, C1])
        bias_row = sb("bias_row", [KPATCH + 1, 1])
        stem_inv = sb("stem_inv", [KPATCH + 1, C1])
        stem_var = sb("stem_var", [KPATCH + 1, C1])
        stem_root = sb("stem_root", [KPATCH + 1, C1])
        stem_shift = sb("stem_shift", [KPATCH + 1, C1])
        stem_w = sb("stem_w", [KPATCH + 1, C1])
        patches = sb("patches", [KPATCH + 1, RAW, PIX])
        patch_halves = sb("patch_halves", [LOW + KPATCH + 1, 2, PIX], F32R)
        off_w = sb("off_w", [C1, TAPS, 2 * TAPS])
        off_b = sb("off_b", [2 * TAPS, 1])
        grid = sb("grid", [2 * TAPS, NTOK])
        pos = sb("pos", [TILE, PRING, 2, PIX])
        h_lin = sb("h_lin", [C1, 2, PIX])
        h_act = sb("h_act", [C1, B, PIX])
        off = sb("off", [2 * TAPS, 2, QUAD * TPI])
        dist_x = sb("dist_x", [TILE, 2, PIX])
        hat_x = sb("hat_x", [TILE, 2, PIX])
        dist_y = sb("dist_y", [TILE, DRING, PIX])
        weights = sb("weights", [TILE, RING, PIX])
        dcn_par = sb("dcn_par", [128, 5, DIM])
        dcn_var = sb("dcn_var", [128, DIM])
        dcn_root = sb("dcn_root", [128, DIM])
        dcn_inv = sb("dcn_inv", [128, DIM])
        hT = sb("hT", [TILE, 2, NT, C1])

        warm_set = sem("warm_set")
        half_set = sem("half_set")
        gap_set = sem("gap_set")
        stem_loaded = sem("stem_loaded")
        patches_loaded = [sem(f"patches_loaded{i}") for i in range(RAW)]
        hi_split = sem("hi_split")
        lo_split = sem("lo_split")
        off_loaded = sem("off_loaded")
        place_loaded = sem("place_loaded")
        par_loaded = sem("par_loaded")
        var_ready = sem("var_ready")
        root_ready = sem("root_ready")
        prep_step = sem("prep_step")
        stem_w_ready = sem("stem_w_ready")
        h_ready = sem("h_ready")
        h_copied = sem("h_copied")
        h_done = sem("h_done")
        off_ready = sem("off_ready")
        off_copied = sem("off_copied")
        placed = sem("placed")
        pos_stored = [sem(f"pos_stored{q}") for q in range(NQ)]
        pos_loaded = [sem(f"pos_loaded{i}") for i in range(PRING)]
        hT_ready = sem("hT_ready")
        hT_copied = sem("hT_copied")
        dist_x_ready = sem("dist_x_ready")
        hat_x_ready = sem("hat_x_ready")
        dist_y_ready = sem("dist_y_ready")
        fall_ready = sem("fall_ready")
        weights_ready = sem("weights_ready")
        pool_weights = sem("pool_weights")
        weights_used = sem("weights_used")
        samples_ready = sem("samples_ready")
        samples_copied = sem("samples_copied")

        def wait_made(eng, b, t):
            if t == POOL_T:
                eng.wait_ge(pool_weights, b + 1)
            else:
                eng.wait_ge(weights_ready, (NT - 1) * b + t + 1 - (t > POOL_T))

        def product(eng, queue, b, t, ready):
            i = NT * b + t
            r = pixel_rows(t)
            queue.wait_ge(fall_ready, i + 1)
            if t in (0, POOL_T):
                queue.wait_ge(hat_x_ready, b + 1)
            if i >= RING:
                was_b, was_t = divmod(i - RING, NT)
                if was_t == NT - 1:
                    queue.wait_ge(samples_ready, was_b + 1)
                else:
                    queue.wait_ge(weights_used, (NT - 1) * was_b + was_t + 1)
            eng.tensor_tensor(weights[0:r, i % RING, :], dist_y[0:r, i % DRING, :], hat_x[0:r, b % 2, :], ALU.mult).then_inc(ready, 1)

        with nc.Block() as block:
            @block.sync
            def _(sp):
                sp.dma_start(stem_par[:, :, :].rearrange("p a c -> p (a c)"), D["stem_par"].to_broadcast((KPATCH + 1, 4 * C1))).then_inc(stem_loaded, 16)
                sp.dma_start(stem_raw[:, :], D["stem_w"]).then_inc(stem_loaded, 16)
                sp.dma_start(bias_row[:, :], D["bias_row"]).then_inc(stem_loaded, 16)

                def load_patches(b):
                    if b >= RAW:
                        sp.wait_ge(lo_split, b - RAW + 1)
                    sp.dma_start(patches[:, b % RAW, :], D["patches"][:, b, :]).then_inc(patches_loaded[b % RAW], 16)

                load_patches(0)
                load_patches(1)
                sp.dma_start(off_w[:, :, :], D["off_w"]).then_inc(off_loaded, 16)
                sp.dma_start(off_b[:, :], D["off_b"]).then_inc(off_loaded, 16)
                load_patches(2)
                load_patches(3)
                sp.dma_start(dcn_par[:, :, :].rearrange("p a c -> p (a c)"), D["dcn_par"].to_broadcast((128, 5 * DIM))).then_inc(par_loaded, 16)
                load_patches(4)
                sp.dma_start(P["dcn_w"][:, :, :], D["dcn_w"]).then_inc(par_loaded, 16)
                sp.dma_start(grid[:, :], D["grid"]).then_inc(place_loaded, 16)
                sp.dma_start(P["row_shift"][:, :], D["row_shift"]).then_inc(place_loaded, 16)
                sp.dma_start(P["ident"][:, :], D["ident"]).then_inc(place_loaded, 16)

                def store_positions(q):
                    sp.wait_ge(placed, q + 1)
                    sp.dma_start(P["pos_dram"][QUAD * q:QUAD * (q + 1), :, :].rearrange("i r t -> r i t"), off[:, q % 2, :].rearrange("r (i t) -> r i t", i=QUAD)).then_inc(pos_stored[q], 16)

                def load_positions(b):
                    if b % QUAD == 0:
                        sp.wait_ge(pos_stored[b // QUAD], 16)
                    if b >= PRING:
                        sp.wait_ge(dist_y_ready, NT * (b - PRING + 1))
                    sp.dma_start(pos[:, b % PRING, :, :].rearrange("p a s -> p (a s)"), P["pos_dram"][b:b + 1, :, :].rearrange("i r t -> i (r t)").to_broadcast((TILE, 2 * PIX))).then_inc(pos_loaded[b % PRING], 16)

                for b in range(5, B):
                    load_patches(b)
                    if b >= 2 * QUAD + 3 and (b + 1) % QUAD == 0:
                        store_positions((b + 1) // QUAD - 3)
                load_positions(0)
                load_positions(1)
                store_positions(NQ - 2)
                load_positions(2)
                store_positions(NQ - 1)
                images = [-(-(t0 + n) // TPI) for t0, n in XTILES]
                for b in range(PRING, B):
                    load_positions(b)
                    if b - PRING in images:
                        sp.wait_ge(samples_copied, 2 * (b - PRING))
                        pack_samples(sp, P, images.index(b - PRING))
                for t in range(XT - 1):
                    if images[t] >= B - PRING:
                        sp.wait_ge(samples_copied, 2 * images[t])
                        pack_samples(sp, P, t)

            @block.gpsimd
            def _(pool):
                nc.gpsimd.memset(P["zeros"][:, :], 0.0).then_inc(warm_set, 1)
                nc.gpsimd.memset(P["minus_half"][:, :], -0.5).then_inc(half_set, 1)
                pool.wait_ge(half_set, 1)
                nc.gpsimd.memset(patch_halves[32:LOW, :, :].bitcast(F32), 0.0).then_inc(gap_set, 1)
                nc.gpsimd.memset(stem_hi[32:LOW, :].bitcast(F32), 0.0).then_inc(gap_set, 1)
                for b in range(B):
                    pool.wait_ge(hi_split, b + 1)
                    nc.gpsimd.tensor_tensor(patch_halves[LOW:LOW + KPATCH + 1, b % 2, :], patches[:, b % RAW, :], patch_halves[0:KPATCH + 1, b % 2, :].bitcast(F32), ALU.subtract).then_inc(lo_split, 1)
                pool.wait_ge(lo_split, B)
                for b in range(B):
                    product(nc.gpsimd, pool, b, POOL_T, pool_weights)

            @block.vector
            def _(dve):
                shift = P["dcn_shift"]
                steps = Steps(dve, prep_step)
                dve.wait_ge(stem_loaded, 16 * 3)
                nc.vector.tensor_scalar(stem_var[:, :], stem_par[:, 3, :], EPS, None, ALU.add).then_inc(var_ready, 1)
                dve.wait_ge(root_ready, 1)
                inverse_root(nc.vector, steps, stem_var[:, :], stem_root[:, :], stem_inv[:, :], stem_shift[:, :])
                steps.done(nc.vector.tensor_tensor(stem_inv[:, :], stem_inv[:, :], stem_par[:, 0, :], ALU.mult))
                steps.wait()
                steps.done(nc.vector.tensor_tensor(stem_raw[:, :], stem_raw[:, :], stem_inv[:, :], ALU.mult))
                steps.done(nc.vector.tensor_tensor(stem_shift[:, :], stem_par[:, 2, :], stem_inv[:, :], ALU.mult))
                steps.wait()
                steps.done(nc.vector.tensor_tensor(stem_shift[:, :], stem_par[:, 1, :], stem_shift[:, :], ALU.subtract))
                steps.wait()
                steps.done(nc.vector.scalar_tensor_tensor(stem_w[:, :], stem_shift[:, :], bias_row[:, 0:1], stem_raw[:, :], ALU.mult, ALU.add))
                dve.wait_ge(gap_set, 2)
                steps.wait()
                steps.done(nc.vector.tensor_copy(stem_hi[0:KPATCH + 1, :], stem_w[:, :]))
                nc.vector.tensor_copy(stem_hi[LOW:LOW + KPATCH + 1, :], stem_w[:, :]).then_inc(stem_w_ready, 1)
                steps.wait()
                nc.vector.tensor_tensor(stem_lo[:, :], stem_w[:, :], stem_hi[0:KPATCH + 1, :].bitcast(F32), ALU.subtract).then_inc(stem_w_ready, 1)

                def leaky(b):
                    dve.wait_ge(h_copied, b + 1)
                    s = 2 * (b % 2)
                    nc.vector.scalar_tensor_tensor(h_act[:, b, :].rearrange("p (a c) -> p a c", a=2), ps[0:C1, s:s + 2, 0:HALF], SLOPE, h_lin[:, b % 2, :].rearrange("p (a c) -> p a c", a=2), ALU.mult, ALU.max).then_inc(h_done, 1)

                def place_offsets(q):
                    s = q % 2
                    dve.wait_ge(off_copied, q + 1)
                    if q == 0:
                        dve.wait_ge(place_loaded, 16 * 3)
                    nc.vector.tensor_tensor(off[:, s, :], grid[:, q * QUAD * TPI:(q + 1) * QUAD * TPI], off[:, s, :], ALU.add).then_inc(placed, 1)

                def falls(b, t):
                    i = NT * b + t
                    r = pixel_rows(t)
                    dve.wait_ge(dist_y_ready, i + 1)
                    nc.vector.tensor_scalar(dist_y[0:r, i % DRING, :], dist_y[0:r, i % DRING, :], 1.0, 0.0, ALU.subtract, ALU.min).then_inc(fall_ready, 1)

                def hats(b):
                    dve.wait_ge(dist_x_ready, b + 1)
                    if b >= 2:
                        dve.wait_ge(pool_weights, b - 1)
                    nc.vector.tensor_scalar(hat_x[:, b % 2, :], dist_x[:, b % 2, :], 1.0, 0.0, ALU.subtract, ALU.min).then_inc(hat_x_ready, 1)

                for b in range(B):
                    leaky(b)
                    if b == 2 * QUAD:
                        dve.wait_ge(par_loaded, 16 * 2)
                        nc.vector.tensor_scalar(dcn_var[:, :], dcn_par[:, 3, :], EPS, None, ALU.add).then_inc(var_ready, 1)
                    if b == 2 * QUAD + 1:
                        dve.wait_ge(root_ready, 2)
                        steps.done(nc.vector.reciprocal(dcn_inv[:, :], dcn_root[:, :]))
                    if b == 2 * QUAD + 2:
                        steps.wait()
                        steps.done(nc.vector.tensor_tensor(shift[:, :], dcn_inv[:, :], dcn_inv[:, :], ALU.mult))
                        steps.wait()
                        steps.done(nc.vector.tensor_tensor(shift[:, :], shift[:, :], dcn_var[:, :], ALU.mult))
                    if b == 2 * QUAD + 3:
                        steps.wait()
                        steps.done(nc.vector.tensor_scalar(shift[:, :], shift[:, :], -0.5, 1.5, ALU.mult, ALU.add))
                        steps.wait()
                        steps.done(nc.vector.tensor_tensor(dcn_inv[:, :], dcn_inv[:, :], shift[:, :], ALU.mult))
                        steps.wait()
                        steps.done(nc.vector.tensor_tensor(dcn_inv[:, :], dcn_inv[:, :], dcn_par[:, 0, :], ALU.mult))
                        steps.done(nc.vector.tensor_tensor(shift[:, :], dcn_par[:, 4, :], dcn_par[:, 2, :], ALU.subtract))
                        steps.wait()
                    if b == B - 2:
                        steps.done(nc.vector.tensor_tensor(shift[:, :], shift[:, :], dcn_inv[:, :], ALU.mult))
                    if b == B - 1:
                        steps.wait()
                        nc.vector.tensor_tensor(shift[:, :], shift[:, :], dcn_par[:, 1, :], ALU.add)
                    if b >= B - QUAD:
                        at = slice((b - B + QUAD) * SLOTS // QUAD, (b - B + QUAD + 1) * SLOTS // QUAD)
                        nc.vector.tensor_tensor(P["dcn_w"][:, at, :], P["dcn_w"][:, at, :], dcn_inv[:, :].unsqueeze(1).to_broadcast((128, at.stop - at.start, DIM)), ALU.mult)
                    if b % QUAD == QUAD - 1 and b >= QUAD:
                        place_offsets(b // QUAD - 1)
                hats(0)
                falls(0, 0)
                for i in range(NT * B):
                    b, t = divmod(i, NT)
                    if t == NT - 1 and b + 1 < B:
                        hats(b + 1)
                    if i + 1 < NT * B:
                        falls(*divmod(i + 1, NT))
                    if t != POOL_T:
                        product(nc.vector, dve, b, t, weights_ready)
                    if i == NT:
                        place_offsets(NQ - 1)

            @block.scalar
            def _(act):
                def high(b):
                    act.wait_ge(patches_loaded[b % RAW], 16 * (b // RAW + 1))
                    if b == 0:
                        act.wait_ge(gap_set, 1)
                    if b >= 2:
                        act.wait_ge(h_ready, b - 1)
                    nc.scalar.activation(patch_halves[0:KPATCH + 1, b % 2, :], patches[:, b % RAW, :], ACT.Copy).then_inc(hi_split, 1)

                def copy_h(b):
                    act.wait_ge(h_ready, b + 1)
                    if b >= 2:
                        act.wait_ge(h_done, b - 1)
                    s = 2 * (b % 2)
                    nc.scalar.activation(h_lin[:, b % 2, :].rearrange("p (a c) -> p a c", a=2), ps[0:C1, s:s + 2, 0:HALF], ACT.Copy).then_inc(h_copied, 1)

                def bias_offsets(q):
                    act.wait_ge(off_ready, q + 1)
                    if q >= 2:
                        act.wait_ge(pos_stored[q - 2], 16)
                    else:
                        act.wait_ge(off_loaded, 16 * 2)
                    nc.scalar.activation(off[:, q % 2, :], ps[0:2 * TAPS, 6 + q % 2, 0:QUAD * TPI], ACT.Identity, bias=off_b[:, 0:1]).then_inc(off_copied, 1)

                def copy_hT(b):
                    act.wait_ge(hT_ready, b + 1)
                    if b >= 2:
                        act.wait_ge(samples_ready, b - 1)
                    nc.scalar.activation(hT[:, b % 2, 0:NT - 1, :].rearrange("p t c -> p (t c)"), ps[0:TILE, 4 + b % 2, 0:(NT - 1) * C1], ACT.Copy).then_inc(hT_copied, 1)
                    nc.scalar.activation(hT[0:LAST, b % 2, NT - 1, :], ps[0:LAST, 4 + b % 2, (NT - 1) * C1:NT * C1], ACT.Copy).then_inc(hT_copied, 1)

                def distance_x(b):
                    act.wait_ge(pos_loaded[b % PRING], 16 * (b // PRING + 1))
                    if b >= 2:
                        act.wait_ge(hat_x_ready, b - 1)
                    nc.scalar.activation(dist_x[:, b % 2, :], pos[:, b % PRING, 1, :], ACT.Abs, bias=P["row_shift"][0:TILE, NT:NT + 1]).then_inc(dist_x_ready, 1)

                def distance_y(b, t):
                    i = NT * b + t
                    if i >= DRING:
                        wait_made(act, *divmod(i - DRING, NT))
                    nc.scalar.activation(dist_y[:, i % DRING, :], pos[:, b % PRING, 0, :], ACT.Abs, bias=P["row_shift"][0:TILE, t:t + 1]).then_inc(dist_y_ready, 1)

                def copy_samples(b):
                    act.wait_ge(samples_ready, b + 1)
                    taps = ps[0:C1, 2 * (b % 2):2 * (b % 2) + 2, 0:HALF].rearrange("p a (k t) -> p a k t", k=TAPS // 2)
                    nc.scalar.activation(P["samples"][0:C1, :, b * TPI:(b + 1) * TPI].rearrange("p (a k) t -> p a k t", a=2), taps[:, :, 0:SLOTS // 2, :], ACT.Copy).then_inc(samples_copied, 1)
                    nc.scalar.activation(P["extra"][:, :, b * TPI:(b + 1) * TPI].rearrange("p (a k) t -> p a k t", a=2), taps[:, :, SLOTS // 2:, :], ACT.Copy).then_inc(samples_copied, 1)

                act.wait_ge(var_ready, 1)
                nc.scalar.activation(stem_root[:, :], stem_var[:, :], ACT.Sqrt).then_inc(root_ready, 1)
                high(0)
                high(1)
                for b in range(B):
                    copy_h(b)
                    if b + 2 < B:
                        high(b + 2)
                    if b == 2 * QUAD:
                        act.wait_ge(var_ready, 2)
                        nc.scalar.activation(dcn_root[:, :], dcn_var[:, :], ACT.Sqrt).then_inc(root_ready, 1)
                    if b % QUAD == QUAD - 1 and b >= QUAD:
                        bias_offsets(b // QUAD - 1)
                act.wait_ge(place_loaded, 16 * 3)
                distance_x(0)
                for t in range(NT):
                    distance_y(0, t)
                    if t == 0:
                        copy_hT(0)
                bias_offsets(NQ - 1)
                for b in range(1, B):
                    distance_x(b)
                    distance_y(b, 0)
                    distance_y(b, 1)
                    copy_hT(b)
                    if b >= 2:
                        copy_samples(b - 2)
                    for t in range(2, NT):
                        distance_y(b, t)
                copy_samples(B - 2)
                copy_samples(B - 1)

            @block.tensor
            def _(pe):
                def stem(b):
                    pe.wait_ge(lo_split, b + 1)
                    if b >= 2:
                        pe.wait_ge(h_done, b - 1)
                    for a in range(2):
                        cols, bank = slice(a * HALF, (a + 1) * HALF), 2 * (b % 2) + a
                        nc.tensor.matmul(ps[0:C1, bank, 0:HALF], stem_hi[:, :], patch_halves[:, b % 2, cols], start=True, stop=False)
                        ins = nc.tensor.matmul(ps[0:C1, bank, 0:HALF], stem_lo[:, :], patch_halves[0:KPATCH + 1, b % 2, cols], start=False, stop=True)
                    ins.then_inc(h_ready, 1)

                def offsets(q, taps):
                    if taps[0] == 0:
                        if q == 0:
                            pe.wait_ge(off_loaded, 16 * 2)
                        pe.wait_ge(h_done, QUAD * (q + 1))
                        if q >= 2:
                            pe.wait_ge(off_copied, q - 1)
                    view = h_act[:, QUAD * q:QUAD * (q + 1), :].rearrange("c i (y u x v) -> c i y u x v", u=KS, v=KS, x=SIDE2)
                    for k in taps:
                        ins = nc.tensor.matmul(ps[0:2 * TAPS, 6 + q % 2, 0:QUAD * TPI], off_w[:, k, :], view[:, :, :, k // KS, :, k % KS], start=(k == 0), stop=(k == TAPS - 1))
                    if taps[-1] == TAPS - 1:
                        ins.then_inc(off_ready, 1)

                def transpose_h(b):
                    if b == 0:
                        pe.wait_ge(place_loaded, 16 * 3)
                        pe.wait_ge(h_done, B)
                    if b >= 2:
                        pe.wait_ge(hT_copied, 2 * (b - 1))
                    for t in range(NT):
                        ins = nc.tensor.transpose(ps[0:pixel_rows(t), 4 + b % 2, t * C1:(t + 1) * C1], h_act[:, b, t * TILE:t * TILE + pixel_rows(t)], P["ident"][0:C1, 0:C1])
                    ins.then_inc(hT_ready, 1)

                def sample(b):
                    pe.wait_ge(hT_copied, 2 * (b + 1))
                    if b >= 2:
                        pe.wait_ge(samples_copied, 2 * (b - 1))
                    for t in range(NT):
                        i = NT * b + t
                        r = pixel_rows(t)
                        wait_made(pe, b, t)
                        for a in range(2):
                            ins = nc.tensor.matmul(ps[0:C1, 2 * (b % 2) + a, 0:HALF], hT[0:r, b % 2, t, :], weights[0:r, i % RING, a * HALF:(a + 1) * HALF], start=(t == 0), stop=(t == NT - 1))
                        if t < NT - 1:
                            ins.then_inc(weights_used, 1)
                    ins.then_inc(samples_ready, 1)

                pe.wait_ge(warm_set, 1)
                for _ in range(WARM):
                    nc.tensor.matmul(ps[:, 4, 0:256], P["zeros"][:, 0:128], P["zeros"][:, :], start=True, stop=True)
                pe.wait_ge(stem_w_ready, 2)
                pe.wait_ge(gap_set, 2)
                for b in range(B):
                    stem(b)
                    if b >= QUAD:
                        offsets(b // QUAD - 1, range(4 * (b % QUAD), 4 * (b % QUAD) + 4))
                    else:
                        for _ in range(FILL):
                            nc.tensor.matmul(ps[:, 4, 0:256], P["zeros"][:, 0:128], P["zeros"][:, :], start=True, stop=True)
                transpose_h(0)
                offsets(NQ - 1, range(TAPS))
                for b in range(B):
                    if b + 1 < B:
                        transpose_h(b + 1)
                    sample(b)


def stage_tokens(nc, P, D, W):
    ctx = ExitStack()
    with ctx:
        def sb(name, shape, dt=F32):
            return ctx.enter_context(nc.sbuf_tensor(name, shape, dt))

        def sem(name):
            return ctx.enter_context(nc.semaphore(name))

        ps = P["ps"]
        FIRST = first_jobs(W)
        HELD = 6
        lin = sb("lin", [128, 2, DIM])
        stats = sb("stats", [128, XT, 6])
        mv = sb("mv", [128, XT, 2])
        var_eps = sb("var_eps", [128, XT])
        rstd = sb("rstd", [128, XT])
        xhat = sb("xhat", [128, 2, WIDE])
        xT = sb("xT", [128, 2, DC, 128])

        const_loaded = sem("const_loaded")
        conv_ready = sem("conv_ready")
        lin_ready = sem("lin_ready")
        h_ready = sem("tokens_ready")
        stats_ready = sem("stats_ready")
        mv_ready = sem("mv_ready")
        pool_step = sem("norm_step")
        rstd_ready = sem("rstd_ready")
        xhat_ready = sem("xhat_ready")
        xT_ready = sem("xT_ready")
        xT_copied = sem("xT_copied")
        hi_done = sem("hi_done")
        split_done = sem("split_done")

        with nc.Block() as block:
            @block.sync
            def _(sp):
                pack_samples(sp, P, XT - 1)
                sp.dma_start(P["iota"][:, :, :], D["iota"]).then_inc(const_loaded, 16)
                sp.dma_start(P["mask_q"][:, :], D["mask_q"].bitcast(BF16)).then_inc(const_loaded, 16)
                sp.dma_start(P["mask_k"][:, :], D["mask_k"].bitcast(BF16)).then_inc(const_loaded, 16)
                load_attention(sp, W, D)
                sp.wait_ge(const_loaded, 16 * 3)

            @block.tensor
            def _(pe):
                def conv(g):
                    t0, n = XTILES[g]
                    pe.wait_ge(P["packed"][g], 16 * C1 // BLOCK)
                    if g >= 2:
                        pe.wait_ge(lin_ready, g - 1)
                    for k in range(SLOTS):
                        ins = nc.tensor.matmul(ps[0:n, g % 2, 0:DIM], P["samples"][:, k, t0:t0 + n], P["dcn_w"][:, k, :], start=(k == 0), stop=(k == SLOTS - 1))
                    ins.then_inc(conv_ready, 1)

                def transpose(g):
                    t0, n = XTILES[g]
                    pe.wait_ge(xhat_ready, 2 * (g + 1))
                    if g >= 2:
                        pe.wait_ge(xT_copied, g - 1)
                    for c in range(DC):
                        ins = nc.tensor.transpose(ps[:, 2 + g % 2, c * n:(c + 1) * n], xhat[0:n, g % 2, c * 128:(c + 1) * 128], P["ident"][0:n, 0:n])
                    ins.then_inc(xT_ready, 1)

                def first(lo, hi):
                    if lo == 0:
                        pe.wait_ge(W["w_lo_done"], 2)
                        pe.wait_ge(W["w_rest_done"], 2)
                        pe.wait_ge(split_done, DC * (3))
                    for n in range(lo, hi):
                        if n >= 4:
                            pe.wait_ge(W["qk_copied"], n - 3)
                        project_qk(nc, P, W, FIRST[n], 4 + n % 4)

                for g in range(XT):
                    conv(g)
                    if g >= 1:
                        transpose(g - 1)
                first(0, HELD)
                transpose(XT - 1)
                first(HELD, len(FIRST))

            @block.scalar
            def _(act):
                def copy_T(g):
                    t0, n = XTILES[g]
                    act.wait_ge(xT_ready, g + 1)
                    if g >= 2:
                        act.wait_ge(split_done, DC * (g - 1))
                    nc.scalar.activation(xT[:, g % 2, :, 0:n], ps[:, 2 + g % 2, 0:DC * n].rearrange("p (c t) -> p c t", c=DC), ACT.Copy).then_inc(xT_copied, 1)

                for g in range(XT):
                    if g < 3:
                        split_high(nc.scalar, W, g)
                    if g == XT - 1:
                        for n in range(HELD):
                            copy_qk(nc, act, P, W, FIRST[n], 4 + n % 4, n + 1)
                    copy_T(g)
                for n in range(HELD, len(FIRST)):
                    copy_qk(nc, act, P, W, FIRST[n], 4 + n % 4, n + 1)

            @block.vector
            def _(dve):
                nc.vector.memset(P["x_lo"][64:128, 1, :].bitcast(F32), 0.0)
                for g in range(XT):
                    t0, n = XTILES[g]
                    h = P["h"][0:n, g, :]
                    dve.wait_ge(conv_ready, g + 1)
                    nc.vector.tensor_tensor(lin[0:n, g % 2, :], ps[0:n, g % 2, 0:DIM], P["dcn_shift"][0:n, :], ALU.add).then_inc(lin_ready, 1)
                    dve.wait_ge(lin_ready, g + 1)
                    nc.vector.scalar_tensor_tensor(h, lin[0:n, g % 2, :], SLOPE, lin[0:n, g % 2, :], ALU.mult, ALU.max).then_inc(h_ready, 1)
                    dve.wait_ge(h_ready, g + 1)
                    nc.vector.bn_stats(stats[0:n, g, :], h).then_inc(stats_ready, 1)
                    dve.wait_ge(stats_ready, g + 1)
                    nc.vector.bn_aggr(mv[0:n, g, :], stats[0:n, g, :]).then_inc(mv_ready, 1)
                    dve.wait_ge(rstd_ready, g + 1)
                    if g >= 2:
                        dve.wait_ge(xT_ready, g - 1)
                    for src, dst in WIDE_PARTS:
                        nc.vector.tensor_scalar(xhat[0:n, g % 2, dst], h[:, src], mv[0:n, g, 0:1], rstd[0:n, g:g + 1], ALU.subtract, ALU.mult).then_inc(xhat_ready, 1)
                    if g >= 1:
                        split_x(dve, P, xT, g - 1, xT_copied, g, hi_done, split_done)
                        if g - 1 < 3:
                            split_low(nc.vector, W, g - 1)
                split_x(dve, P, xT, XT - 1, xT_copied, XT, hi_done, split_done)

            @block.gpsimd
            def _(pool):
                steps = Steps(pool, pool_step)
                for g in range(XT):
                    n = XTILES[g][1]
                    if 1 <= g <= 3:
                        pool.wait_ge(rstd_ready, g)
                        split_rest(nc.gpsimd, W, g - 1)
                    if g == 4:
                        pool.wait_ge(W["rest_loaded"], 16 * 5)
                        nc.gpsimd.tensor_scalar(W["bias_q"][:, :], W["bias_qk"][:, 0, :], W["scale"], None, ALU.mult).then_inc(W["bias_ready"], 1)
                    pool.wait_ge(mv_ready, g + 1)
                    steps.done(nc.gpsimd.tensor_scalar(var_eps[0:n, g:g + 1], mv[0:n, g, 1:2], EPS, None, ALU.add))
                    steps.wait()
                    nc.gpsimd.tensor_tensor(rstd[0:n, g:g + 1], var_eps[0:n, g:g + 1], P["minus_half"][0:n, 0:1], ALU.pow).then_inc(rstd_ready, 1)


def attention_weights(nc, P, ctx, sems, layer, side):
    tag = f"a{layer}_"
    hd = (64, 32)[layer]
    width, tiles = HEADS * hd, HEADS * hd // 128

    def sb(name, shape, dt=F32):
        return ctx.enter_context(nc.sbuf_tensor(tag + name, shape, dt, side=side))

    W = {"layer": layer, "scalar": nc.scalar, "raw": sb("raw", [128, 3, DC, width]), "hi": sb("w_hi", [128, 3, DC, width], F32R), "lo": sb("w_lo", [128, 3, width], F32R),
         "tiles": tiles, "scale": (64, 16)[layer] ** -0.5, "qT": sb("qT", [128, tiles, NTOK]), "kT": sb("kT", [128, tiles, NTOK]),
         "wo": sb("wo", [128, tiles, DIM]), "affine": sb("affine", [128, 2, DC])}
    if layer == 0:
        W.update(ob=sb("ob", [128, DIM]), bias_qk=sb("bias_qk", [128, 2, tiles]), bias_q=sb("bias_q", [128, tiles]), bias_v=sb("bias_v", [GT, width]))
    else:
        W.update(wr=P["wr"], wr_hi=P["wr_hi"], wr_lo=P["wr_lo"])
    for name in ("qkv_loaded0", "qkv_loaded1", "qkv_loaded2", "rest_loaded", "w_hi_done", "w_lo_done", "w_rest_done", "qk_ready", "qk_copied", "bias_ready"):
        W[name] = sems.enter_context(nc.semaphore(tag + name))
    return W


def load_attention(sp, W, D):
    tag = f"a{W['layer']}_"
    for i, name in enumerate("qkv"):
        sp.dma_start(W["raw"][:, i, :, :], D[tag + "w" + name]).then_inc(W[f"qkv_loaded{i}"], 16)
    sp.dma_start(W["wo"][:, :, :], D[tag + "wo"]).then_inc(W["rest_loaded"], 16)
    sp.dma_start(W["affine"][:, :, :], D[tag + "affine"]).then_inc(W["rest_loaded"], 16)
    if W["layer"] == 0:
        sp.dma_start(W["ob"][:, :], D["ob"].to_broadcast((128, DIM))).then_inc(W["rest_loaded"], 16)
        sp.dma_start(W["bias_qk"][:, :, :], D["bias_qk"]).then_inc(W["rest_loaded"], 16)
        sp.dma_start(W["bias_v"][:, :], D["bias_v"].to_broadcast(W["bias_v"].shape)).then_inc(W["rest_loaded"], 16)
    else:
        sp.dma_start(W["wr"][:, :, :], D["wr"]).then_inc(W["rest_loaded"], 16)
    sp.wait_ge(W["rest_loaded"], 16 * (5 if W["layer"] == 0 else 3))


def split_raw(W, i):
    if i < 3:
        return W["raw"][:, i, :, :], W["hi"][:, i, :, :], W["lo"][:, i, :], (W[f"qkv_loaded{i}"], 16)
    return W["wr"][:, :, :], W["wr_hi"][:, :, :], W["wr_lo"][:, :], (W["rest_loaded"], 16 * 3)


def split_high(eng, W, i):
    raw, hi, lo, loaded = split_raw(W, i)
    eng.wait_ge(*loaded)
    if eng is W["scalar"]:
        eng.activation(hi, raw, ACT.Copy).then_inc(W["w_hi_done"], 1)
    else:
        eng.tensor_copy(hi, raw).then_inc(W["w_hi_done"], 1)


def split_low(eng, W, i):
    raw, hi, lo, _ = split_raw(W, i)
    eng.wait_ge(W["w_hi_done"], i + 1)
    eng.tensor_tensor(lo, raw[:, 0, :], hi[:, 0, :].bitcast(F32), ALU.subtract).then_inc(W["w_lo_done"], 1)


def split_rest(eng, W, i):
    raw, hi, lo, _ = split_raw(W, i)
    eng.wait_ge(W["w_hi_done"], i + 1)
    eng.tensor_tensor(hi[64:128, 1, :], raw[64:128, 1, :], hi[64:128, 1, :].bitcast(F32), ALU.subtract).then_inc(W["w_rest_done"], 1)
    eng.wait_ge(W["w_rest_done"], i + 1)


def first_jobs(W):
    return [(w, i, 0) for i in range(W["tiles"]) for w in "qk"]


def project_qk(nc, P, W, job, bank):
    w, i, a = job
    m, cols, toks = "qk".index(w), slice(i * 128, (i + 1) * 128), slice(a * HALF, (a + 1) * HALF)
    for k, (wp, xp) in enumerate(five(W["hi"][:, m, :, cols], W["lo"][:, m, cols], P["x_hi"][:, :, toks], P["x_lo"][:, :, toks])):
        ins = nc.tensor.matmul(P["ps"][:, bank, 0:HALF], wp, xp, start=(k == 0), stop=(k == 4))
    ins.then_inc(W["qk_ready"], 1)


def copy_qk(nc, act, P, W, job, bank, n):
    w, i, a = job
    act.wait_ge(W["qk_ready"], n)
    dst, src, scale = W[w + "T"][:, i, a * HALF:(a + 1) * HALF], P["ps"][:, bank, 0:HALF], (W["scale"] if w == "q" else 1.0)
    if W["layer"] == 0:
        if n == 1:
            act.wait_ge(W["bias_ready"], 1)
        nc.scalar.activation(dst, src, ACT.Identity, bias=(W["bias_q"][:, i:i + 1] if w == "q" else W["bias_qk"][:, 1, i:i + 1]), scale=scale).then_inc(W["qk_copied"], 1)
    else:
        nc.scalar.activation(dst, src, ACT.Copy, scale=scale).then_inc(W["qk_copied"], 1)


def stage_attention(nc, P, D, W, following):
    layer = W["layer"]
    hd = (64, 32)[layer]
    per = 128 // hd
    tiles = HEADS // per
    width = HEADS * hd
    scale = (64 ** -0.5, 16 ** -0.5)[layer]
    HPU = 3
    UPG = HEADS // HPU
    NU = NG * UPG
    tag = f"a{layer}_"
    ctx = ExitStack()
    with ctx:
        def sb(name, shape, dt=F32):
            return ctx.enter_context(nc.sbuf_tensor(tag + name, shape, dt))

        def sem(name):
            return ctx.enter_context(nc.semaphore(tag + name))

        def unit(u):
            g, j = divmod(u, UPG)
            return g, j % per, HPU * (j // per)

        ps = P["ps"]
        w_hi, w_lo, wo, affine = W["hi"], W["lo"], W["wo"], W["affine"]
        qT, kT, qk_copied = W["qT"], W["kT"], W["qk_copied"]
        v = sb("v", [GT, NG, width])
        zT = sb("zT", [128, tiles, NTOK])
        minus_peak = sb("minus_peak", [GT, 4, HPU])
        probs = sb("probs", [GT, 3, HPU, GT])
        sums = sb("sums", [GT, 4, HPU])
        inv_sums = sb("inv_sums", [GT, 4, HPU])
        probs_n = sb("probs_n", [GT, 2, HPU, GT])
        probs_T = sb("probs_T", [GT, 2, HPU, GT])
        stats = sb("stats", [128, 2, XT, 6])
        mv = sb("mv", [128, 2, XT, 2])
        var_eps = sb("var_eps", [128, 2, XT])
        rstd = sb("rstd", [128, 2, XT])
        xhat = sb("xhat", [128, 2, WIDE])
        xT = sb("xT", [128, 2, DC, 128])
        if layer == 0:
            ob, bias_v = W["ob"], W["bias_v"]

        v_ready = sem("v_ready")
        v_copied = sem("v_copied")
        scores_ready = sem("scores_ready")
        minus_peak_ready = sem("minus_peak_ready")
        probs_ready = sem("probs_ready")
        inv_sums_ready = sem("inv_sums_ready")
        probs_n_ready = sem("probs_n_ready")
        probs_T_ready = sem("probs_T_ready")
        probs_T_copied = sem("probs_T_copied")
        z_ready = sem("z_ready")
        z_copied = sem("z_copied")
        o_ready = sem("o_ready")
        base_ready = sem("base_ready")
        sum_ready = sem("sum_ready")
        norm_step = sem("norm_step")
        mv_ready = sem("mv_ready")
        rstd_ready = sem("rstd_ready")
        pool_step = sem("pool_step")
        x_ready = sem("x_ready")
        xhat_ready = sem("xhat_ready")
        xT_ready = sem("xT_ready")
        xT_copied = sem("xT_copied")
        hi_done = sem("hi_done")
        split_done = sem("split_done")
        NORMS = 2 - layer

        cut = width // 2 if layer == 0 else width
        VCUTS = width // cut
        FIRST = first_jobs(W)
        SECOND = [(w, i, 1) for i in range(tiles) for w in "qk"]
        SECOND_UNIT = UPG * next(g for g, (t0, n) in enumerate(GROUPS) if t0 + n > HALF)
        NQK = len(FIRST) + len(SECOND)
        O_TURN = 2 * UPG + 4
        STEP_TURN = {0: (0, 1, 2, 4), 1: (0, None, 1, 3)}[layer]
        T_TURN = O_TURN + STEP_TURN[2] + 1
        TURNS = O_TURN + UPG * (XT - 1) + STEP_TURN[3] + 1
        jobs = [[] for _ in range(TURNS)]
        for a in range(VCUTS):
            jobs[a].append(("v", 0, a))
        for n, job in enumerate(SECOND):
            jobs[n * SECOND_UNIT // len(SECOND)].append(job)
        for g in range(1, NG):
            for a in range(VCUTS):
                jobs[UPG * g + a - (0 if g > 1 else 2)].append(("v", g, a))
        for g in range(XT):
            jobs[O_TURN + UPG * g].append(("o", g, 0))
            jobs[T_TURN + UPG * g].append(("t", g, 0))
        NEXT_TURN = max(NU + 1, O_TURN + UPG * (SECOND_UNIT // UPG) + STEP_TURN[3] + 1)
        NEXT = first_jobs(following) if layer == 0 else []
        EXPERT_TURNS = (14, 15, 18, 19)
        SPLIT_TURNS = (13, 16, 19, 22)
        ORDER = [job for turn in jobs for job in turn]
        QK = FIRST + [job for job in ORDER if job[0] in "qk"]
        V = [job for job in ORDER if job[0] == "v"]

        def bank_of(job):
            return 6 + ORDER.index(job) % 2

        def wait_bank(pe, job):
            if ORDER.index(job) >= 2:
                before = ORDER[ORDER.index(job) - 2]
                kind, g, _ = before
                if kind in "qk":
                    pe.wait_ge(qk_copied, QK.index(before) + 1)
                elif kind == "v":
                    pe.wait_ge(v_copied, V.index(before) + 1)
                elif kind == "o":
                    pe.wait_ge(sum_ready, g + 1)
                else:
                    pe.wait_ge(xT_copied, DC * (g + 1))

        with nc.Block() as block:
            @block.sync
            def _(sp):
                if layer == 0:
                    load_attention(sp, following, D)
                else:
                    load_expert(sp, following, D, 0)
            @block.tensor
            def _(pe):
                def project(job):
                    w, i, a = job
                    wait_bank(pe, job)
                    if w != "v":
                        project_qk(nc, P, W, job, bank_of(job))
                        return
                    t0, n = GROUPS[i]
                    cols, toks = slice(a * cut, (a + 1) * cut), slice(t0, t0 + n)
                    for k, (wp, xp) in enumerate(five(w_hi[:, 2, :, cols], w_lo[:, 2, cols], P["x_hi"][:, :, toks], P["x_lo"][:, :, toks])):
                        ins = nc.tensor.matmul(ps[0:n, bank_of(job), 0:cut], xp, wp, start=(k == 0), stop=(k == 4))
                    ins.then_inc(v_ready, 1)

                def scores(u):
                    g, r, i0 = unit(u)
                    t0, n = GROUPS[g]
                    part = slice(r * hd, (r + 1) * hd)
                    if u == 0:
                        pe.wait_ge(qk_copied, len(FIRST))
                    if u == SECOND_UNIT:
                        pe.wait_ge(qk_copied, NQK)
                    if u >= 3:
                        pe.wait_ge(probs_ready, HPU * (u - 2))
                    masked = n > TPI
                    if masked:
                        nc.tensor.matmul(ps[0:n, u % 3, 0:HPU * n], P["mask_q"][part, 0:n], P["mask_k"][part, 0:HPU * n], start=True, stop=False)
                    for j in range(HPU):
                        ins = nc.tensor.matmul(ps[0:n, u % 3, j * n:(j + 1) * n], qT[part, i0 + j, t0:t0 + n], kT[part, i0 + j, t0:t0 + n], start=not masked, stop=(not masked or j == HPU - 1))
                    ins.then_inc(scores_ready, 1)

                def transposes(u):
                    g, r, i0 = unit(u)
                    n = GROUPS[g][1]
                    pe.wait_ge(probs_n_ready, u + 1)
                    if u >= 2:
                        pe.wait_ge(probs_T_copied, u - 1)
                    for _ in range(FILL_UNIT[layer]):
                        nc.tensor.matmul(ps[:, 3 + u % 2, 384:512], P["zeros"][:, 0:128], P["zeros"][:, 0:128], start=True, stop=True)
                    for j in range(HPU):
                        ins = nc.tensor.transpose(ps[0:n, 3 + u % 2, j * n:(j + 1) * n], probs_n[0:n, u % 2, j, 0:n], P["ident"][0:n, 0:n])
                    ins.then_inc(probs_T_ready, 1)

                def values(u):
                    g, r, i0 = unit(u)
                    n = GROUPS[g][1]
                    pe.wait_ge(probs_T_copied, u + 1)
                    pe.wait_ge(v_copied, VCUTS * (g + 1))
                    if u >= 1:
                        pe.wait_ge(z_copied, u)
                    for j in range(HPU):
                        h = (i0 + j) * per + r
                        ins = nc.tensor.matmul(ps[r * hd:(r + 1) * hd, 5, j * n:(j + 1) * n], v[0:n, g, h * hd:(h + 1) * hd], probs_T[0:n, u % 2, j, 0:n], start=True, stop=True)
                    ins.then_inc(z_ready, 1)

                def output(g):
                    t0, n = XTILES[g]
                    pe.wait_ge(z_copied, UPG * (g + 2))
                    wait_bank(pe, ("o", g, 0))
                    for i in range(tiles):
                        ins = nc.tensor.matmul(ps[0:n, bank_of(("o", g, 0)), 0:DIM], zT[:, i, t0:t0 + n], wo[:, i, :], start=(i == 0), stop=(i == tiles - 1))
                    ins.then_inc(o_ready, 1)

                def transpose_x(g):
                    n = XTILES[g][1]
                    pe.wait_ge(xhat_ready, 2 * (g + 1))
                    wait_bank(pe, ("t", g, 0))
                    for c in range(DC):
                        ins = nc.tensor.transpose(ps[:, bank_of(("t", g, 0)), c * n:(c + 1) * n], xhat[0:n, g % 2, c * 128:(c + 1) * 128], P["ident"][0:n, 0:n])
                    ins.then_inc(xT_ready, 1)

                for turn in range(TURNS):
                    if 0 <= turn - 3 < NU:
                        transposes(turn - 3)
                    if 0 <= turn - 4 < NU:
                        values(turn - 4)
                    if turn < NU:
                        scores(turn)
                    for job in jobs[turn]:
                        if job[0] == "o":
                            output(job[1])
                        elif job[0] == "t":
                            transpose_x(job[1])
                        else:
                            project(job)
                    if 0 <= turn - NEXT_TURN < len(NEXT):
                        n = turn - NEXT_TURN
                        if n == 0:
                            pe.wait_ge(following["w_lo_done"], 2)
                            pe.wait_ge(following["w_rest_done"], 2)
                            pe.wait_ge(split_done, DC * (SECOND_UNIT // UPG + 1))
                            pe.wait_ge(probs_ready, HPU * NU)
                        if n >= 3:
                            pe.wait_ge(following["qk_copied"], n - 2)
                        project_qk(nc, P, following, NEXT[n], n % 3)
                    if turn >= NU + 3:
                        for _ in range(FILL_END[layer]):
                            nc.tensor.matmul(ps[:, 3, 0:256], P["zeros"][:, 0:128], P["zeros"][:, :], start=True, stop=True)

            @block.scalar
            def _(act):
                def exps(u):
                    g, r, i0 = unit(u)
                    n = GROUPS[g][1]
                    act.wait_ge(minus_peak_ready, u + 1)
                    if u >= 3:
                        act.wait_ge(probs_n_ready, u - 2)
                    if u >= 4:
                        act.wait_ge(inv_sums_ready, u - 3)
                    for j in range(HPU):
                        nc.scalar.activation(probs[0:n, u % 3, j, 0:n], ps[0:n, u % 3, j * n:(j + 1) * n], ACT.Exp, bias=minus_peak[0:n, u % 4, j:j + 1],
                                             accum_out=sums[0:n, u % 4, j:j + 1]).then_inc(probs_ready, 1)

                def copy_z(u):
                    g, r, i0 = unit(u)
                    t0, n = GROUPS[g]
                    part = slice(r * hd, (r + 1) * hd)
                    act.wait_ge(z_ready, u + 1)
                    nc.scalar.activation(zT[part, i0:i0 + HPU, t0:t0 + n], ps[part, 5, 0:HPU * n].rearrange("p (j t) -> p j t", j=HPU), ACT.Copy).then_inc(z_copied, 1)

                def copy_xT(g):
                    t0, n = XTILES[g]
                    act.wait_ge(xT_ready, g + 1)
                    for c in range(DC):
                        if c == 0 and g >= 2:
                            act.wait_ge(split_done, DC * (g - 1))
                        nc.scalar.activation(xT[:, g % 2, c, 0:n], ps[:, bank_of(("t", g, 0)), c * n:(c + 1) * n], ACT.Identity, bias=affine[:, 1, c:c + 1], scale=affine[:, 0, c:c + 1]).then_inc(xT_copied, 1)

                for turn in range(TURNS):
                    if 0 <= turn - 1 < NU:
                        exps(turn - 1)
                    if 0 <= turn - 4 < NU:
                        copy_z(turn - 4)
                    for job in jobs[turn]:
                        if job[0] in "qk":
                            copy_qk(nc, act, P, W, job, bank_of(job), QK.index(job) + 1)
                        if job[0] == "t":
                            copy_xT(job[1])
                    if 0 <= turn - NEXT_TURN < len(NEXT):
                        copy_qk(nc, act, P, following, NEXT[turn - NEXT_TURN], (turn - NEXT_TURN) % 3, turn - NEXT_TURN + 1)
            @block.vector
            def _(dve):
                def copy_v(job):
                    _, g, a = job
                    n, cols = GROUPS[g][1], slice(a * cut, (a + 1) * cut)
                    dve.wait_ge(v_ready, V.index(job) + 1)
                    if layer == 0:
                        nc.vector.tensor_tensor(v[0:n, g, cols], ps[0:n, bank_of(job), 0:cut], bias_v[0:n, cols], ALU.add).then_inc(v_copied, 1)
                    else:
                        nc.vector.tensor_copy(v[0:n, g, cols], ps[0:n, bank_of(job), 0:cut]).then_inc(v_copied, 1)

                steps = Steps(dve, norm_step)

                def peaks(u):
                    g, r, i0 = unit(u)
                    n = GROUPS[g][1]
                    dve.wait_ge(scores_ready, u + 1)
                    if u >= 4:
                        dve.wait_ge(probs_ready, HPU * (u - 3))
                    nc.vector.reduce_max(minus_peak[0:n, u % 4, :], ps[0:n, u % 3, 0:HPU * n].rearrange("p (j t) -> p j t", j=HPU), axis=AX.X, negate=True).then_inc(minus_peak_ready, 1)

                def inverse(u):
                    n = GROUPS[unit(u)[0]][1]
                    dve.wait_ge(probs_ready, HPU * (u + 1))
                    if u >= 4:
                        dve.wait_ge(probs_n_ready, u - 3)
                    nc.vector.reciprocal(inv_sums[0:n, u % 4, :], sums[0:n, u % 4, :]).then_inc(inv_sums_ready, 1)

                def copy_T(u):
                    n = GROUPS[unit(u)[0]][1]
                    dve.wait_ge(probs_T_ready, u + 1)
                    if u >= 2:
                        dve.wait_ge(z_ready, u - 1)
                    nc.vector.tensor_copy(probs_T[0:n, u % 2, :, 0:n], ps[0:n, 3 + u % 2, 0:HPU * n].rearrange("p (j t) -> p j t", j=HPU)).then_inc(probs_T_copied, 1)

                def norm_stats(src, k, g):
                    n = XTILES[g][1]
                    steps.done(nc.vector.bn_stats(stats[0:n, k, g, :], src))
                    steps.wait()
                    nc.vector.bn_aggr(mv[0:n, k, g, :], stats[0:n, k, g, :]).then_inc(mv_ready, 1)

                def tail(g, step):
                    n = XTILES[g][1]
                    h, x, rest = P["h"][0:n, g, :], P["x"][0:n, g, :], P["rest"][0:n, g, :]
                    src = h if layer == 0 else x
                    if step == 0:
                        dve.wait_ge(o_ready, g + 1)
                        if layer == 0:
                            dve.wait_ge(base_ready, g + 1)
                        nc.vector.tensor_tensor(src, ps[0:n, bank_of(("o", g, 0)), 0:DIM], src, ALU.add).then_inc(sum_ready, 1)
                        dve.wait_ge(sum_ready, g + 1)
                        norm_stats(src, 0, g)
                    if step == 1 and layer == 0:
                        dve.wait_ge(rstd_ready, NORMS * g + 1)
                        nc.vector.tensor_scalar(x, h, mv[0:n, 0, g, 0:1], rstd[0:n, 0, g:g + 1], ALU.subtract, ALU.mult).then_inc(x_ready, 1)
                        dve.wait_ge(x_ready, g + 1)
                        norm_stats(x, 1, g)
                    if step == 2:
                        k = NORMS - 1
                        dve.wait_ge(rstd_ready, NORMS * (g + 1))
                        if g >= 2:
                            dve.wait_ge(xT_ready, g - 1)
                        for src, dst in WIDE_PARTS:
                            nc.vector.tensor_scalar(xhat[0:n, g % 2, dst], x[:, src], mv[0:n, k, g, 0:1], rstd[0:n, k, g:g + 1], ALU.subtract, ALU.mult).then_inc(xhat_ready, 1)
                    if step == 3:
                        split_x(nc.vector, P, xT, g, xT_copied, DC * (g + 1), hi_done, split_done)

                for turn in range(TURNS):
                    if 0 <= turn - 3 < NU:
                        copy_T(turn - 3)
                    if turn < NU:
                        peaks(turn)
                    if 0 <= turn - 1 < NU:
                        inverse(turn - 1)
                    for job in jobs[turn]:
                        if job[0] == "v":
                            copy_v(job)
                    for g in range(XT):
                        for step in range(4):
                            if STEP_TURN[step] is not None and turn == O_TURN + UPG * g + STEP_TURN[step]:
                                tail(g, step)
                    if layer == 0 and turn in SPLIT_TURNS:
                        split_high(nc.vector, following, SPLIT_TURNS.index(turn))
                    if layer == 0 and turn - 1 in SPLIT_TURNS:
                        split_low(nc.vector, following, SPLIT_TURNS.index(turn - 1))
                    if layer == 1 and turn in EXPERT_TURNS:
                        (split_w1_high, split_w1_low, split_w2_high, split_w2_low)[EXPERT_TURNS.index(turn)](nc.vector, following, 0)

            @block.gpsimd
            def _(pool):
                steps = Steps(pool, pool_step)
                if layer == 0:
                    for g in range(XT):
                        n = XTILES[g][1]
                        nc.gpsimd.tensor_tensor(P["h"][0:n, g, :], P["h"][0:n, g, :], ob[0:n, :], ALU.add).then_inc(base_ready, 1)

                def normalise(u):
                    n = GROUPS[unit(u)[0]][1]
                    pool.wait_ge(inv_sums_ready, u + 1)
                    if u >= 2:
                        pool.wait_ge(probs_T_ready, u - 1)
                    nc.gpsimd.tensor_tensor(probs_n[0:n, u % 2, :, 0:n], probs[0:n, u % 3, :, 0:n], inv_sums[0:n, u % 4, :].unsqueeze(2).to_broadcast((n, HPU, n)), ALU.mult).then_inc(probs_n_ready, 1)

                def inverse_deviation(g, k):
                    n = XTILES[g][1]
                    pool.wait_ge(mv_ready, NORMS * g + k + 1)
                    steps.done(nc.gpsimd.tensor_scalar(var_eps[0:n, k, g:g + 1], mv[0:n, k, g, 1:2], EPS, None, ALU.add))
                    steps.wait()
                    nc.gpsimd.tensor_tensor(rstd[0:n, k, g:g + 1], var_eps[0:n, k, g:g + 1], P["minus_half"][0:n, 0:1], ALU.pow).then_inc(rstd_ready, 1)

                for turn in range(TURNS):
                    if 0 <= turn - 1 < NU:
                        normalise(turn - 1)
                    if layer == 0 and turn - 1 in SPLIT_TURNS:
                        pool.wait_ge(probs_n_ready, turn)
                        split_rest(nc.gpsimd, following, SPLIT_TURNS.index(turn - 1))
                    if layer == 1 and turn == EXPERT_TURNS[1]:
                        pool.wait_ge(probs_n_ready, turn)
                        split_w1_rest(nc.gpsimd, following, 0)
                        pool.wait_ge(following["w1_rest_done"], 1)
                    for g in range(XT):
                        for k in range(NORMS):
                            if turn == O_TURN + UPG * g + k:
                                inverse_deviation(g, k)
                        if layer == 1 and turn == O_TURN + UPG * g + 2:
                            n = XTILES[g][1]
                            pool.wait_ge(sum_ready, g + 1)
                            nc.gpsimd.tensor_tensor(P["rest"][0:n, g, :], P["h"][0:n, g, :], P["x"][0:n, g, :], ALU.add)

def expert_weights(nc, ctx):
    def sb(name, shape, dt=F32):
        return ctx.enter_context(nc.sbuf_tensor(name, shape, dt))

    W = {"raw1": sb("raw1", [128, DC, FF]), "raw2": sb("raw2", [128, FT, DIM]),
         "hi1": [sb(f"w1_hi{i}", [128, DC, FF], F32R) for i in range(2)], "lo1": [sb(f"w1_lo{i}", [128, FF], F32R) for i in range(2)],
         "both2": [sb(f"w2_{i}", [128, FT, 2, DIM], F32R) for i in range(2)]}
    for name in ("raw1_loaded", "raw2_loaded", "w1_hi_done", "w1_lo_done", "w1_rest_done", "w2_hi_done", "w2_done"):
        W[name] = ctx.enter_context(nc.semaphore(name))
    return W


def load_expert(sp, W, D, e):
    if e >= 1:
        sp.wait_ge(W["w1_lo_done"], e)
        sp.wait_ge(W["w1_rest_done"], e)
    sp.dma_start(W["raw1"][:, :, :], D["w1"][e, :, :, :]).then_inc(W["raw1_loaded"], 16)
    if e >= 1:
        sp.wait_ge(W["w2_done"], e)
    sp.dma_start(W["raw2"][:, :, :], D["w2"][e, :, :, :]).then_inc(W["raw2_loaded"], 16)


def split_w1_high(eng, W, e):
    eng.wait_ge(W["raw1_loaded"], 16 * (e + 1))
    eng.tensor_copy(W["hi1"][e % 2][:, :, :], W["raw1"][:, :, :]).then_inc(W["w1_hi_done"], 1)


def split_w1_low(eng, W, e):
    eng.wait_ge(W["w1_hi_done"], e + 1)
    eng.tensor_tensor(W["lo1"][e % 2][:, :], W["raw1"][:, 0, :], W["hi1"][e % 2][:, 0, :].bitcast(F32), ALU.subtract).then_inc(W["w1_lo_done"], 1)


def split_w1_rest(eng, W, e):
    hi = W["hi1"][e % 2]
    eng.wait_ge(W["w1_hi_done"], e + 1)
    eng.tensor_tensor(hi[64:128, 1, :], W["raw1"][64:128, 1, :], hi[64:128, 1, :].bitcast(F32), ALU.subtract).then_inc(W["w1_rest_done"], 1)


def split_w2_high(eng, W, e):
    eng.wait_ge(W["raw2_loaded"], 16 * (e + 1))
    eng.tensor_copy(W["both2"][e % 2][:, :, 0, :], W["raw2"][:, :, :]).then_inc(W["w2_hi_done"], 1)


def split_w2_low(eng, W, e):
    both = W["both2"][e % 2]
    eng.wait_ge(W["w2_hi_done"], e + 1)
    eng.tensor_tensor(both[:, :, 1, :], W["raw2"][:, :, :], both[:, :, 0, :].bitcast(F32), ALU.subtract).then_inc(W["w2_done"], 1)


def stage_experts(nc, P, D, W, out):
    ctx = ExitStack()
    with ctx:
        def sb(name, shape, dt=F32):
            return ctx.enter_context(nc.sbuf_tensor(name, shape, dt))

        def sem(name):
            return ctx.enter_context(nc.semaphore(name))

        ps = P["ps"]
        w1_hi, w1_lo, w2 = W["hi1"], W["lo1"], W["both2"]
        w2_done = W["w2_done"]
        hidden = sb("hidden", [128, 3, NTOK])
        hid_hi = sb("hid_hi", [128, 2, FT, NTOK], F32R)
        hid_lo = sb("hid_lo", [128, 2, FT, NTOK], F32R)
        acc = P["rest"]

        logits = sb("logits", [128, XT, EXPERTS])
        top = sb("top", [128, XT, 8])
        top_at = sb("top_at", [128, XT, 8], U32)
        top_f = sb("top_f", [128, XT, 2])
        gap = sb("gap", [128, XT])
        second = sb("second", [128, XT])
        total = sb("total", [128, XT])
        share = sb("share", [128, 2, XT])
        pick = sb("pick", [128, 2, XT, EXPERTS])

        base = sb("base", [128, XT])
        base_set = sem("base_set")
        logits_ready = sem("logits_ready")
        logits_copied = sem("logits_copied")
        route_step = sem("route_step")
        gap_ready = sem("gap_ready")
        second_ready = sem("second_ready")
        gates_ready = sem("gates_ready")
        up_ready = sem("up_ready")
        gelu_done = sem("gelu_done")
        hid_hi_done = sem("hid_hi_done")
        hidden_ready = sem("hidden_ready")
        down_ready = sem("down_ready")
        added = sem("added")
        stored = sem("stored")

        with nc.Block() as block:
            @block.sync
            def _(sp):
                load_expert(sp, W, D, 1)
                for e in range(2, EXPERTS):
                    load_expert(sp, W, D, e)
                for t, (t0, n) in enumerate(XTILES):
                    sp.wait_ge(added, 2 * (XT * (EXPERTS - 1) + t + 1))
                    sp.dma_start(out[t0:t0 + n, :], acc[0:n, t, :]).then_inc(stored, 16)
                sp.wait_ge(stored, 16 * XT)

            @block.tensor
            def _(pe):
                def up(e):
                    pe.wait_ge(W["w1_lo_done"], e + 1)
                    pe.wait_ge(W["w1_rest_done"], e + 1)
                    for f in range(FT):
                        u = FT * e + f
                        if u >= 2:
                            pe.wait_ge(gelu_done, u - 1)
                        cols = slice(f * 128, (f + 1) * 128)
                        for a in range(2):
                            toks = slice(a * HALF, (a + 1) * HALF)
                            for k, (wp, xp) in enumerate(five(w1_hi[e % 2][:, :, cols], w1_lo[e % 2][:, cols], P["x_hi"][:, :, toks], P["x_lo"][:, :, toks])):
                                ins = nc.tensor.matmul(ps[:, 2 * (u % 2) + a, 0:HALF], wp, xp, start=(k == 0), stop=(k == 4))
                        ins.then_inc(up_ready, 1)

                def down(e):
                    pe.wait_ge(w2_done, e + 1)
                    pe.wait_ge(hidden_ready, FT * (e + 1))
                    if e == 0:
                        pe.wait_ge(logits_copied, XT)
                    for t, (t0, n) in enumerate(XTILES):
                        u = XT * e + t
                        if u >= 4:
                            pe.wait_ge(added, 2 * (u - 3))
                        for f in range(FT):
                            nc.tensor.matmul(ps[0:n, 4 + u % 4, 0:2 * DIM], hid_hi[:, e % 2, f, t0:t0 + n], w2[e % 2][:, f, :, :].rearrange("p a d -> p (a d)"), start=(f == 0), stop=False)
                            ins = nc.tensor.matmul(ps[0:n, 4 + u % 4, 0:DIM], hid_lo[:, e % 2, f, t0:t0 + n], w2[e % 2][:, f, 0, :], start=False, stop=(f == FT - 1))
                        ins.then_inc(down_ready, 1)

                up(0)
                for t, (t0, n) in enumerate(XTILES):
                    for k, (wp, xp) in enumerate(five(P["wr_hi"], P["wr_lo"][:, :], P["x_hi"][:, :, t0:t0 + n], P["x_lo"][:, :, t0:t0 + n])):
                        ins = nc.tensor.matmul(ps[0:n, 4 + t % 4, t * EXPERTS:(t + 1) * EXPERTS], xp, wp, start=(k == 0), stop=(k == 4))
                    ins.then_inc(logits_ready, 1)
                for e in range(EXPERTS):
                    if e + 1 < EXPERTS:
                        up(e + 1)
                    down(e)

            @block.scalar
            def _(act):
                for e in range(EXPERTS):
                    for f in range(FT):
                        u = FT * e + f
                        act.wait_ge(up_ready, u + 1)
                        if u >= 3:
                            act.wait_ge(hidden_ready, u - 2)
                        nc.scalar.activation(hidden[:, u % 3, :].rearrange("p (a t) -> p a t", a=2), ps[:, 2 * (u % 2):2 * (u % 2) + 2, 0:HALF], ACT.Gelu).then_inc(gelu_done, 1)
                        act.wait_ge(gelu_done, u + 1)
                        if e >= 2 and f == 0:
                            act.wait_ge(down_ready, XT * (e - 1))
                        nc.scalar.activation(hid_hi[:, e % 2, f, :], hidden[:, u % 3, :], ACT.Copy).then_inc(hid_hi_done, 1)

            @block.gpsimd
            def _(pool):
                split_w1_rest(nc.gpsimd, W, 1)
                pool.wait_ge(W["w1_rest_done"], 2)
                nc.gpsimd.memset(base[:, :], math.e).then_inc(base_set, 1)
                pool.wait_ge(base_set, 1)
                pool.wait_ge(gap_ready, 1)
                nc.gpsimd.tensor_tensor(second[:, :], base[:, :], gap[:, :], ALU.pow).then_inc(second_ready, 1)
                pool.wait_ge(second_ready, 1)
                for e in range(2, EXPERTS):
                    split_w1_rest(nc.gpsimd, W, e)

            @block.vector
            def _(dve):
                def split1(e):
                    if e >= 2:
                        dve.wait_ge(up_ready, FT * (e - 1))
                    split_w1_high(nc.vector, W, e)
                    split_w1_low(nc.vector, W, e)

                def split2(e):
                    if e >= 2:
                        dve.wait_ge(down_ready, XT * (e - 1))
                    split_w2_high(nc.vector, W, e)
                    split_w2_low(nc.vector, W, e)

                def low(e, f):
                    u = FT * e + f
                    dve.wait_ge(hid_hi_done, u + 1)
                    if e >= 2 and f == 0:
                        dve.wait_ge(down_ready, XT * (e - 1))
                    nc.vector.tensor_tensor(hid_lo[:, e % 2, f, :], hidden[:, u % 3, :], hid_hi[:, e % 2, f, :].bitcast(F32), ALU.subtract).then_inc(hidden_ready, 1)

                def add(e, t):
                    n = XTILES[t][1]
                    u = XT * e + t
                    dve.wait_ge(down_ready, u + 1)
                    if e == 0:
                        dve.wait_ge(gates_ready, 1)
                    else:
                        dve.wait_ge(added, 2 * (u - XT + 1))
                    for a in range(2):
                        if a == 1:
                            dve.wait_ge(added, 2 * u + 1)
                        nc.vector.scalar_tensor_tensor(acc[0:n, t, :], ps[0:n, 4 + u % 4, a * DIM:(a + 1) * DIM], P["gates"][0:n, t, e:e + 1], acc[0:n, t, :], ALU.mult, ALU.add).then_inc(added, 1)

                route = Steps(dve, route_step)

                def nothing():
                    pass

                def copy_logits():
                    route.done(nc.vector.memset(logits[:, :, :], 0.0))
                    dve.wait_ge(logits_ready, XT)
                    route.wait()
                    for t, (t0, n) in enumerate(XTILES):
                        nc.vector.tensor_copy(logits[0:n, t, :], ps[0:n, 4 + t % 4, t * EXPERTS:(t + 1) * EXPERTS]).then_inc(logits_copied, 1)

                def largest():
                    dve.wait_ge(logits_copied, XT)
                    for t in range(XT):
                        route.done(nc.vector.max(top[:, t, :], logits[:, t, :]))

                def places():
                    route.wait()
                    for t in range(XT):
                        route.done(nc.vector.max_index(top_at[:, t, :], top[:, t, :], logits[:, t, :]))
                    nc.vector.tensor_tensor(gap[:, :], top[:, :, 1], top[:, :, 0], ALU.subtract).then_inc(gap_ready, 1)

                def picks():
                    route.wait()
                    route.done(nc.vector.tensor_copy(top_f[:, :, :], top_at[:, :, 0:2]))
                    route.wait()
                    for k in range(2):
                        route.done(nc.vector.tensor_tensor(pick[:, k, :, :], P["iota"][:, :, :], top_f[:, :, k:k + 1].to_broadcast((128, XT, EXPERTS)), ALU.is_equal))

                def gates():
                    dve.wait_ge(second_ready, 1)
                    route.done(nc.vector.tensor_scalar(total[:, :], second[:, :], 1.0, None, ALU.add))
                    route.wait()
                    route.done(nc.vector.reciprocal(share[:, 0, :], total[:, :]))
                    route.wait()
                    route.done(nc.vector.tensor_tensor(share[:, 1, :], second[:, :], share[:, 0, :], ALU.mult))
                    route.wait()
                    for k in range(2):
                        route.done(nc.vector.tensor_tensor(pick[:, k, :, :], pick[:, k, :, :], share[:, k, :].unsqueeze(2).to_broadcast((128, XT, EXPERTS)), ALU.mult))
                    route.wait()
                    nc.vector.tensor_tensor(P["gates"][:, :, :], pick[:, 0, :, :], pick[:, 1, :, :], ALU.add).then_inc(gates_ready, 1)

                low(0, 0)
                split1(1)
                for f in range(1, FT):
                    low(0, f)
                    if f == 3:
                        split2(1)
                for e in range(EXPERTS):
                    if e + 1 < EXPERTS:
                        for f in range(FT):
                            low(e + 1, f)
                            if f == 0 and e >= 1:
                                split2(e + 1)
                            if e == 0:
                                (copy_logits, largest, places, picks, gates, nothing)[f]()
                            if f == 3 and e + 2 < EXPERTS:
                                split1(e + 2)
                    for t in range(XT):
                        add(e, t)


def build(nc, D, out):
    ctx = ExitStack()
    with ctx:
        def sb(name, shape, dt=F32):
            return ctx.enter_context(nc.sbuf_tensor(name, shape, dt))

        P = {"ps": ctx.enter_context(nc.psum_tensor("ps", [128, 8, 512], F32))}
        P["pos_dram"] = nc.dram_tensor("pos_dram", (B, 2 * TAPS, TPI), F32).ap()
        P["zeros"] = sb("zeros", [128, 256], BF16)
        P["ident"] = sb("ident", [128, 128])
        P["minus_half"] = sb("minus_half", [128, 1])
        P["row_shift"] = sb("row_shift", [128, NT + 1])
        for name, shape, dt in (("wr", [128, DC, EXPERTS], F32), ("wr_hi", [128, DC, EXPERTS], F32R), ("wr_lo", [128, EXPERTS], F32R)):
            P[name] = sb(name, shape, dt)
        P["mask_q"] = sb("mask_q", [128, GT], BF16)
        P["mask_k"] = sb("mask_k", [128, IPG * GT], BF16)
        P["iota"] = sb("iota", [128, XT, EXPERTS])
        P["gates"] = sb("gates", [128, XT, EXPERTS])
        for name in ("h", "x", "rest"):
            P[name] = sb(name, [128, XT, DIM])
        P["x_hi"] = sb("x_hi", [128, DC, NTOK], F32R)
        P["x_lo"] = sb("x_lo", [128, DC, NTOK], F32R)
        early, late = ExitStack(), ExitStack()
        P["packed"] = [ctx.enter_context(nc.semaphore(f"packed{t}")) for t in range(XT)]
        for name, shape in (("samples", [128, SLOTS, NTOK]), ("dcn_w", [128, SLOTS, DIM]), ("dcn_shift", [128, DIM]), ("extra", [C1, TAPS - SLOTS, NTOK])):
            P[name] = early.enter_context(nc.sbuf_tensor(name, shape, F32, side="right"))
        stage_images(nc, P, D)
        with ExitStack() as first:
            W0 = attention_weights(nc, P, first, ctx, 0, "left")
            stage_tokens(nc, P, D, W0)
            early.close()
            W1 = attention_weights(nc, P, late, ctx, 1, "right")
            stage_attention(nc, P, D, W0, W1)
        WE = expert_weights(nc, ctx)
        stage_attention(nc, P, D, W1, WE)
        late.close()
        stage_experts(nc, P, D, WE, out)


def constants():
    import numpy as np
    k, token = np.arange(TAPS)[:, None], np.arange(NTOK)[None, :] % TPI
    grid = np.concatenate([k // KS + KS * (token // SIDE2), k % KS + KS * (token % SIDE2)]).astype(np.float32)
    p = np.arange(128)
    row_shift = np.zeros((128, NT + 1), np.float32)
    row_shift[:, 0:NT] = -(p[:, None] // SIDE + ROWS * np.arange(NT))
    row_shift[:, NT] = -(p % SIDE)
    mask_q, mask_k = np.zeros((128, GT), np.float32), np.zeros((128, IPG, GT), np.float32)
    image = np.arange(GT) // TPI
    for base in range(0, 128, 32):
        mask_q[base], mask_k[base] = 1, -BIG
        for i in range(IPG):
            mask_q[base + 1 + i], mask_k[base + 1 + i] = image == i, BIG * (image == i)
    bias_row = np.zeros((KPATCH + 1, 1), np.float32)
    bias_row[KPATCH] = 1
    iota = np.broadcast_to(np.arange(EXPERTS, dtype=np.float32), (128, XT, EXPERTS))
    def bf16(a):
        return (np.ascontiguousarray(a, np.float32).view(np.uint32) >> 16).astype(np.uint16)

    return {"grid": grid, "row_shift": row_shift, "bias_row": bias_row, "iota": iota, "ident": np.eye(128, dtype=np.float32),
            "mask_q": bf16(mask_q), "mask_k": bf16(mask_k.reshape(128, IPG * GT))}


def layouts(I):
    import numpy as np

    def chunks(w):
        return np.stack([w[0:128], np.concatenate([w[128:DIM], w[128:DIM]])], 1)

    t = {n: np.asarray(a) for n, a in I.items()}
    tok = {n[len("L0_tok_"):]: a for n, a in t.items() if n.startswith("L0_tok_")}
    att = {n[len("L0_attn_"):]: a for n, a in t.items() if n.startswith("L0_attn_")}
    ffn = {n[len("L0_ffn_"):]: a for n, a in t.items() if n.startswith("L0_ffn_")}
    patches = np.ones((KPATCH + 1, B, PIX), np.float32)
    patches[0:KPATCH] = t["x"].reshape(B, CIN, SIDE, KS, SIDE, KS).transpose(1, 3, 5, 0, 2, 4).reshape(KPATCH, B, PIX)
    taps = tok["dcn_w"].reshape(DIM, C1, 2, TAPS // 2).transpose(1, 2, 3, 0)
    beside = taps[:, :, SLOTS // 2:].reshape(C1 // BLOCK, BLOCK, TAPS - SLOTS, DIM).transpose(1, 2, 0, 3).reshape(BLOCK, SLOTS, DIM)
    dcn_w = np.concatenate([taps[:, :, 0:SLOTS // 2].reshape(C1, SLOTS, DIM), beside])
    d = {
        "patches": patches,
        "stem_w": np.concatenate([tok["stem_w"].reshape(C1, KPATCH).T, tok["stem_b"][None, :]]),
        "stem_par": np.concatenate([tok[n] for n in ("bn1_g", "bn1_b", "bn1_m", "bn1_v")])[None, :],
        "off_w": tok["off_w"].reshape(TAPS, 2, C1, TAPS).transpose(2, 3, 1, 0).reshape(C1, TAPS, 2 * TAPS),
        "off_b": tok["off_b"].reshape(TAPS, 2).T.reshape(2 * TAPS, 1),
        "dcn_w": dcn_w,
        "dcn_par": np.concatenate([tok[n] for n in ("bn2_g", "bn2_b", "bn2_m", "bn2_v", "dcn_b")])[None, :],
        "ob": att["Ob"].reshape(1, DIM),
        "a0_wo": att["O"].reshape(HEADS // 2, 128, DIM).transpose(1, 0, 2),
        "a0_affine": np.stack([chunks(ffn["ln1_g"]), chunks(ffn["ln1_b"])], 1),
        "a1_affine": np.stack([chunks(ffn["ln2_g"]), chunks(ffn["ln2_b"])], 1),
        "wr": chunks(ffn["Wrouter"]),
        "w1": np.stack([chunks(w) for w in ffn["W1"]]),
        "w2": ffn["W2"].reshape(EXPERTS, FT, 128, DIM).transpose(0, 2, 1, 3),
    }
    d["bias_qk"] = np.stack([att[n].reshape(HEADS // 2, 128).T for n in ("Qbs", "Kbs")], 1)
    d["bias_v"] = att["Vbs"].reshape(1, -1)
    for name, w in (("wq", "Qs"), ("wk", "Ks"), ("wv", "Vs")):
        d["a0_" + name] = chunks(att[w].transpose(1, 0, 2).reshape(DIM, -1))
    qkv = np.zeros((3, DIM, HEADS, 32), ffn["Wqkv"].dtype)
    qkv[:, :, :, 0:16] = ffn["Wqkv"].reshape(DIM, 3, HEADS, 16).transpose(1, 0, 2, 3)
    for i, name in enumerate(("wq", "wk", "wv")):
        d["a1_" + name] = chunks(qkv[i].reshape(DIM, -1))
    proj = np.zeros((HEADS, 32, DIM), ffn["Wproj"].dtype)
    proj[:, 0:16] = ffn["Wproj"].reshape(HEADS, 16, DIM)
    d["a1_wo"] = proj.reshape(HEADS // 4, 128, DIM).transpose(1, 0, 2)
    return d


def kernel(**inputs):
    import numpy as np
    import concourse.bacc as bacc
    from concourse.bass_utils import run_bass_kernel_spmd

    nc = bacc.Bacc("TRN2", target_bir_lowering=False, num_devices=1)
    arrays, D = {}, {}
    for name, a in {**constants(), **layouts(inputs)}.items():
        arrays["in_" + name] = np.ascontiguousarray(a)
        D[name] = nc.dram_tensor("in_" + name, arrays["in_" + name].shape, mybir.dt.from_np(arrays["in_" + name].dtype), kind="ExternalInput").ap()
    out = nc.dram_tensor("out", (NTOK, DIM), F32, kind="ExternalOutput").ap()
    build(nc, D, out)
    r = run_bass_kernel_spmd(nc, [arrays], core_ids=[0])
    return r.results[0]["out"].reshape(B, TPI, DIM)
```

```python
import math
import concourse.bass as bass
from concourse import mybir
from contextlib import ExitStack

F32 = mybir.dt.float32
F32R = mybir.dt.float32r
BF16 = mybir.dt.bfloat16
U32 = mybir.dt.uint32
ALU = mybir.AluOpType
ACT = mybir.ActivationFunctionType
AX = mybir.AxisListType

B, CIN, IMG = 16, 3, 96
KS = 4
SIDE = IMG // KS
PIX = SIDE * SIDE
HALF = PIX // 2
C1 = 96
TAPS = KS * KS
SIDE2 = SIDE // KS
TPI = SIDE2 * SIDE2
NTOK = B * TPI
KPATCH = CIN * TAPS
DIM = 192
DC = 2
WIDE = 256
WIDE_PARTS = ((slice(0, DIM), slice(0, DIM)), (slice(128, DIM), slice(DIM, WIDE)))
WARM = 40
FILL = 6
FILL_UNIT = (2, 4)
FILL_END = (4, 4)
LOW = 64
RAW = 4
BLOCK = 32
SLOTS = TAPS * C1 // 128
ROWS = 5
TILE = ROWS * SIDE
NT = -(-SIDE // ROWS)
LAST = PIX - (NT - 1) * TILE
IPG = 3
GT = IPG * TPI
GROUPS = [(g * GT, min(GT, NTOK - g * GT)) for g in range(-(-NTOK // GT))]
NG = len(GROUPS)
XTILES = [(t * 128, min(128, NTOK - t * 128)) for t in range(-(-NTOK // 128))]
XT = len(XTILES)
HEADS = 12
FF = 768
EXPERTS = 8
FT = FF // 128
UP_EARLY = 2
EPS = 1e-5
SLOPE = 0.01
QUAD = 4
BIG = 2.0 ** 100


class Steps:

    def __init__(self, eng, sem):
        self.eng, self.sem, self.n = eng, sem, 0

    def done(self, ins):
        ins.then_inc(self.sem, 1)
        self.n += 1
        return self.n

    def wait(self, n=None):
        self.eng.wait_ge(self.sem, self.n if n is None else n)


def pixel_rows(t):
    return TILE if t < NT - 1 else LAST


def inverse_root(dve, steps, var, root, out, tmp):
    steps.done(dve.reciprocal(out, root))
    steps.wait()
    steps.done(dve.tensor_tensor(tmp, out, out, ALU.mult))
    steps.wait()
    steps.done(dve.tensor_tensor(tmp, tmp, var, ALU.mult))
    steps.wait()
    steps.done(dve.tensor_scalar(tmp, tmp, -0.5, 1.5, ALU.mult, ALU.add))
    steps.wait()
    steps.done(dve.tensor_tensor(out, out, tmp, ALU.mult))
    steps.wait()


def split_x(dve, P, xT, g, copied, n_copied, hi_done, split_done):
    t0, n = XTILES[g]
    cols = slice(t0, t0 + n)
    full, hi, lo = xT[:, g % 2, :, 0:n], P["x_hi"][:, :, cols], P["x_lo"]
    dve.wait_ge(copied, n_copied)
    dve.tensor_copy(hi, full).then_inc(hi_done, 1)
    dve.wait_ge(hi_done, g + 1)
    dve.tensor_tensor(lo[:, 0, cols], full[:, 0, :], hi[:, 0, :].bitcast(F32), ALU.subtract).then_inc(split_done, 1)
    dve.tensor_tensor(lo[0:64, 1, cols], full[0:64, 1, :], hi[0:64, 1, :].bitcast(F32), ALU.subtract).then_inc(split_done, 1)


def five(w_hi, w_lo, x_hi, x_lo):
    return ((w_hi[:, 0, :], x_hi[:, 0, :]), (w_lo, x_hi[:, 0, :]), (w_hi[:, 0, :], x_lo[:, 0, :]),
            (w_hi[:, 1, :], x_hi[:, 1, :]), (w_hi[:, 1, :], x_lo[:, 1, :]))


def pack_samples(sp, P, g):
    t0, n = XTILES[g]
    for block in range(C1 // BLOCK):
        sp.dma_start(P["samples"][C1:128, block::C1 // BLOCK, t0:t0 + n], P["extra"][block * BLOCK:(block + 1) * BLOCK, :, t0:t0 + n]).then_inc(P["packed"][g], 16)


def stage_images(nc, P, D):
    ctx = ExitStack()
    with ctx:
        def sb(name, shape, dt=F32):
            return ctx.enter_context(nc.sbuf_tensor(name, shape, dt))

        def sem(name):
            return ctx.enter_context(nc.semaphore(name))

        ps = P["ps"]
        NQ = B // QUAD
        POOL_T = 2
        PRING = 2
        stem_raw = sb("stem_raw", [KPATCH + 1, C1])
        stem_hi = sb("stem_hi", [LOW + KPATCH + 1, C1], F32R)
        stem_lo = sb("stem_lo", [KPATCH + 1, C1], F32R)
        stem_par = sb("stem_par", [KPATCH + 1, 4, C1])
        bias_row = sb("bias_row", [KPATCH + 1, 1])
        stem_inv = sb("stem_inv", [KPATCH + 1, C1])
        stem_var = sb("stem_var", [KPATCH + 1, C1])
        stem_root = sb("stem_root", [KPATCH + 1, C1])
        stem_shift = sb("stem_shift", [KPATCH + 1, C1])
        stem_w = sb("stem_w", [KPATCH + 1, C1])
        patches = sb("patches", [KPATCH + 1, RAW, PIX])
        patch_halves = sb("patch_halves", [LOW + KPATCH + 1, 2, PIX], F32R)
        off_w = sb("off_w", [C1, TAPS, 2 * TAPS])
        off_b = sb("off_b", [2 * TAPS, 1])
        grid = sb("grid", [2 * TAPS, NTOK])
        pos = sb("pos", [TILE, PRING, 2, PIX])
        h_lin = sb("h_lin", [C1, 2, PIX])
        h_act = sb("h_act", [C1, B, PIX])
        off = sb("off", [2 * TAPS, 2, QUAD * TPI])
        dist_x = sb("dist_x", [TILE, 2, PIX])
        hat_x = sb("hat_x", [TILE, 2, PIX])
        dist_y = sb("dist_y", [TILE, NT, PIX])
        weights = sb("weights", [TILE, NT, PIX])
        dcn_par = sb("dcn_par", [128, 5, DIM])
        dcn_var = sb("dcn_var", [128, DIM])
        dcn_root = sb("dcn_root", [128, DIM])
        dcn_inv = sb("dcn_inv", [128, DIM])
        hT = sb("hT", [TILE, 2, NT, C1])

        warm_set = sem("warm_set")
        half_set = sem("half_set")
        gap_set = sem("gap_set")
        stem_loaded = sem("stem_loaded")
        patches_loaded = [sem(f"patches_loaded{i}") for i in range(RAW)]
        hi_split = sem("hi_split")
        lo_split = sem("lo_split")
        off_loaded = sem("off_loaded")
        place_loaded = sem("place_loaded")
        par_loaded = sem("par_loaded")
        var_ready = sem("var_ready")
        root_ready = sem("root_ready")
        prep_step = sem("prep_step")
        stem_w_ready = sem("stem_w_ready")
        h_ready = sem("h_ready")
        h_copied = sem("h_copied")
        h_done = sem("h_done")
        off_ready = sem("off_ready")
        off_copied = sem("off_copied")
        placed = sem("placed")
        pos_stored = [sem(f"pos_stored{q}") for q in range(NQ)]
        pos_loaded = [sem(f"pos_loaded{i}") for i in range(PRING)]
        hT_ready = sem("hT_ready")
        hT_copied = sem("hT_copied")
        dist_x_ready = sem("dist_x_ready")
        hat_x_ready = sem("hat_x_ready")
        dist_y_ready = sem("dist_y_ready")
        fall_ready = sem("fall_ready")
        weights_ready = sem("weights_ready")
        pool_weights = sem("pool_weights")
        weights_used = sem("weights_used")
        samples_ready = sem("samples_ready")
        samples_copied = sem("samples_copied")

        def wait_made(eng, b, t):
            if t == POOL_T:
                eng.wait_ge(pool_weights, b + 1)
            else:
                eng.wait_ge(weights_ready, b * (NT - 1) + (t + 1 - (t > POOL_T)))

        def product(eng, queue, b, s, t, ready, waits=True):
            r = pixel_rows(t)
            queue.wait_ge(fall_ready, b * NT + (t + 1))
            if t in (0, POOL_T):
                queue.wait_ge(hat_x_ready, b + 1)
            if waits:
                if t == NT - 1:
                    queue.wait_ge(samples_ready, b)
                else:
                    queue.wait_ge(weights_used, b * (NT - 1) + (t + 1 - (NT - 1)))
            eng.tensor_tensor(weights[0:r, t, :], dist_y[0:r, t, :], hat_x[0:r, s, :], ALU.mult).then_inc(ready, 1)

        with nc.Block() as block:
            @block.sync
            def _(sp):
                sp.dma_start(stem_par[:, :, :].rearrange("p a c -> p (a c)"), D["stem_par"].to_broadcast((KPATCH + 1, 4 * C1))).then_inc(stem_loaded, 16)
                sp.dma_start(stem_raw[:, :], D["stem_w"]).then_inc(stem_loaded, 16)
                sp.dma_start(bias_row[:, :], D["bias_row"]).then_inc(stem_loaded, 16)

                def load_patches(b):
                    if b >= RAW:
                        sp.wait_ge(lo_split, b - RAW + 1)
                    sp.dma_start(patches[:, b % RAW, :], D["patches"][:, b, :]).then_inc(patches_loaded[b % RAW], 16)

                load_patches(0)
                load_patches(1)
                sp.dma_start(off_w[:, :, :], D["off_w"]).then_inc(off_loaded, 16)
                sp.dma_start(off_b[:, :], D["off_b"]).then_inc(off_loaded, 16)
                load_patches(2)
                load_patches(3)
                sp.dma_start(dcn_par[:, :, :].rearrange("p a c -> p (a c)"), D["dcn_par"].to_broadcast((128, 5 * DIM))).then_inc(par_loaded, 16)
                load_patches(4)
                sp.dma_start(P["dcn_w"][:, :, :], D["dcn_w"]).then_inc(par_loaded, 16)
                sp.dma_start(grid[:, :], D["grid"]).then_inc(place_loaded, 16)
                sp.dma_start(P["row_shift"][:, :], D["row_shift"]).then_inc(place_loaded, 16)
                sp.dma_start(P["ident"][:, :], D["ident"]).then_inc(place_loaded, 16)

                def store_positions(q):
                    sp.wait_ge(placed, q + 1)
                    sp.dma_start(P["pos_dram"][QUAD * q:QUAD * (q + 1), :, :].rearrange("i r t -> r i t"), off[:, q % 2, :].rearrange("r (i t) -> r i t", i=QUAD)).then_inc(pos_stored[q], 16)

                def load_positions(b):
                    if b % QUAD == 0:
                        sp.wait_ge(pos_stored[b // QUAD], 16)
                    if b >= PRING:
                        sp.wait_ge(dist_y_ready, NT * (b - PRING + 1))
                    sp.dma_start(pos[:, b % PRING, :, :].rearrange("p a s -> p (a s)"), P["pos_dram"][b:b + 1, :, :].rearrange("i r t -> i (r t)").to_broadcast((TILE, 2 * PIX))).then_inc(pos_loaded[b % PRING], 16)

                for b in range(5, B):
                    load_patches(b)
                    if b >= 2 * QUAD + 3 and (b + 1) % QUAD == 0:
                        store_positions((b + 1) // QUAD - 3)
                load_positions(0)
                load_positions(1)
                store_positions(NQ - 2)
                store_positions(NQ - 1)
                images = [-(-(t0 + n) // TPI) for t0, n in XTILES]
                for b in range(PRING, B):
                    load_positions(b)
                    if b - PRING in images:
                        sp.wait_ge(samples_copied, 2 * (b - PRING))
                        pack_samples(sp, P, images.index(b - PRING))
                for t in range(XT - 1):
                    if images[t] >= B - PRING:
                        sp.wait_ge(samples_copied, 2 * images[t])
                        pack_samples(sp, P, t)

            @block.gpsimd
            def _(pool):
                nc.gpsimd.memset(P["zeros"][:, :], 0.0).then_inc(warm_set, 1)
                nc.gpsimd.memset(P["minus_half"][:, :], -0.5).then_inc(half_set, 1)
                pool.wait_ge(half_set, 1)
                nc.gpsimd.memset(patch_halves[32:LOW, :, :].bitcast(F32), 0.0).then_inc(gap_set, 1)
                nc.gpsimd.memset(stem_hi[32:LOW, :].bitcast(F32), 0.0).then_inc(gap_set, 1)
                with nc.gpsimd.Fori(0, B // RAW) as turn:
                    for i in range(RAW):
                        pool.wait_ge(hi_split, turn * RAW + (i + 1))
                        nc.gpsimd.tensor_tensor(patch_halves[LOW:LOW + KPATCH + 1, i % 2, :], patches[:, i, :], patch_halves[0:KPATCH + 1, i % 2, :].bitcast(F32), ALU.subtract).then_inc(lo_split, 1)
                pool.wait_ge(lo_split, B)
                product(nc.gpsimd, pool, 0, 0, POOL_T, pool_weights, waits=False)
                product(nc.gpsimd, pool, 1, 1, POOL_T, pool_weights)
                with nc.gpsimd.Fori(1, B // 2) as pair:
                    for s in range(2):
                        product(nc.gpsimd, pool, pair * 2 + s, s, POOL_T, pool_weights)

            @block.vector
            def _(dve):
                shift = P["dcn_shift"]
                steps = Steps(dve, prep_step)
                dve.wait_ge(stem_loaded, 16 * 3)
                nc.vector.tensor_scalar(stem_var[:, :], stem_par[:, 3, :], EPS, None, ALU.add).then_inc(var_ready, 1)
                dve.wait_ge(root_ready, 1)
                inverse_root(nc.vector, steps, stem_var[:, :], stem_root[:, :], stem_inv[:, :], stem_shift[:, :])
                steps.done(nc.vector.tensor_tensor(stem_inv[:, :], stem_inv[:, :], stem_par[:, 0, :], ALU.mult))
                steps.wait()
                steps.done(nc.vector.tensor_tensor(stem_raw[:, :], stem_raw[:, :], stem_inv[:, :], ALU.mult))
                steps.done(nc.vector.tensor_tensor(stem_shift[:, :], stem_par[:, 2, :], stem_inv[:, :], ALU.mult))
                steps.wait()
                steps.done(nc.vector.tensor_tensor(stem_shift[:, :], stem_par[:, 1, :], stem_shift[:, :], ALU.subtract))
                steps.wait()
                steps.done(nc.vector.scalar_tensor_tensor(stem_w[:, :], stem_shift[:, :], bias_row[:, 0:1], stem_raw[:, :], ALU.mult, ALU.add))
                dve.wait_ge(gap_set, 2)
                steps.wait()
                steps.done(nc.vector.tensor_copy(stem_hi[0:KPATCH + 1, :], stem_w[:, :]))
                nc.vector.tensor_copy(stem_hi[LOW:LOW + KPATCH + 1, :], stem_w[:, :]).then_inc(stem_w_ready, 1)
                steps.wait()
                nc.vector.tensor_tensor(stem_lo[:, :], stem_w[:, :], stem_hi[0:KPATCH + 1, :].bitcast(F32), ALU.subtract).then_inc(stem_w_ready, 1)

                def leaky(b):
                    dve.wait_ge(h_copied, b + 1)
                    s = 2 * (b % 2)
                    nc.vector.scalar_tensor_tensor(h_act[:, b, :].rearrange("p (a c) -> p a c", a=2), ps[0:C1, s:s + 2, 0:HALF], SLOPE, h_lin[:, b % 2, :].rearrange("p (a c) -> p a c", a=2), ALU.mult, ALU.max).then_inc(h_done, 1)

                def place_offsets(q):
                    s = q % 2
                    dve.wait_ge(off_copied, q + 1)
                    if q == 0:
                        dve.wait_ge(place_loaded, 16 * 3)
                    nc.vector.tensor_tensor(off[:, s, :], grid[:, q * QUAD * TPI:(q + 1) * QUAD * TPI], off[:, s, :], ALU.add).then_inc(placed, 1)

                def falls(b, t):
                    r = pixel_rows(t)
                    dve.wait_ge(dist_y_ready, b * NT + (t + 1))
                    nc.vector.tensor_scalar(dist_y[0:r, t, :], dist_y[0:r, t, :], 1.0, 0.0, ALU.subtract, ALU.min).then_inc(fall_ready, 1)

                def hats(b, s, waits=True):
                    dve.wait_ge(dist_x_ready, b + 1)
                    if waits:
                        dve.wait_ge(pool_weights, b - 1)
                    nc.vector.tensor_scalar(hat_x[:, s, :], dist_x[:, s, :], 1.0, 0.0, ALU.subtract, ALU.min).then_inc(hat_x_ready, 1)

                def image_weights(b, s, first=False, last=False):
                    for t in range(NT):
                        if t < NT - 1:
                            falls(b, t + 1)
                        elif not last:
                            hats(b + 1, 1 - s, waits=not first)
                            falls(b + 1, 0)
                        if t != POOL_T:
                            product(nc.vector, dve, b, s, t, weights_ready, waits=not first)

                for b in range(B):
                    leaky(b)
                    if b == 2 * QUAD:
                        dve.wait_ge(par_loaded, 16 * 2)
                        nc.vector.tensor_scalar(dcn_var[:, :], dcn_par[:, 3, :], EPS, None, ALU.add).then_inc(var_ready, 1)
                    if b == 2 * QUAD + 1:
                        dve.wait_ge(root_ready, 2)
                        steps.done(nc.vector.reciprocal(dcn_inv[:, :], dcn_root[:, :]))
                    if b == 2 * QUAD + 2:
                        steps.wait()
                        steps.done(nc.vector.tensor_tensor(shift[:, :], dcn_inv[:, :], dcn_inv[:, :], ALU.mult))
                        steps.wait()
                        steps.done(nc.vector.tensor_tensor(shift[:, :], shift[:, :], dcn_var[:, :], ALU.mult))
                    if b == 2 * QUAD + 3:
                        steps.wait()
                        steps.done(nc.vector.tensor_scalar(shift[:, :], shift[:, :], -0.5, 1.5, ALU.mult, ALU.add))
                        steps.wait()
                        steps.done(nc.vector.tensor_tensor(dcn_inv[:, :], dcn_inv[:, :], shift[:, :], ALU.mult))
                        steps.wait()
                        steps.done(nc.vector.tensor_tensor(dcn_inv[:, :], dcn_inv[:, :], dcn_par[:, 0, :], ALU.mult))
                        steps.done(nc.vector.tensor_tensor(shift[:, :], dcn_par[:, 4, :], dcn_par[:, 2, :], ALU.subtract))
                        steps.wait()
                    if b == B - 2:
                        steps.done(nc.vector.tensor_tensor(shift[:, :], shift[:, :], dcn_inv[:, :], ALU.mult))
                    if b == B - 1:
                        steps.wait()
                        nc.vector.tensor_tensor(shift[:, :], shift[:, :], dcn_par[:, 1, :], ALU.add)
                    if b >= B - QUAD:
                        at = slice((b - B + QUAD) * SLOTS // QUAD, (b - B + QUAD + 1) * SLOTS // QUAD)
                        nc.vector.tensor_tensor(P["dcn_w"][:, at, :], P["dcn_w"][:, at, :], dcn_inv[:, :].unsqueeze(1).to_broadcast((128, at.stop - at.start, DIM)), ALU.mult)
                    if b % QUAD == QUAD - 1 and b >= QUAD:
                        place_offsets(b // QUAD - 1)
                hats(0, 0, waits=False)
                falls(0, 0)
                image_weights(0, 0, first=True)
                place_offsets(NQ - 1)
                image_weights(1, 1)
                with nc.vector.Fori(1, B // 2 - 1) as pair:
                    for s in range(2):
                        image_weights(pair * 2 + s, s)
                image_weights(B - 2, 0)
                image_weights(B - 1, 1, last=True)

            @block.scalar
            def _(act):
                def high(b):
                    act.wait_ge(patches_loaded[b % RAW], 16 * (b // RAW + 1))
                    if b == 0:
                        act.wait_ge(gap_set, 1)
                    if b >= 2:
                        act.wait_ge(h_ready, b - 1)
                    nc.scalar.activation(patch_halves[0:KPATCH + 1, b % 2, :], patches[:, b % RAW, :], ACT.Copy).then_inc(hi_split, 1)

                def copy_h(b):
                    act.wait_ge(h_ready, b + 1)
                    if b >= 2:
                        act.wait_ge(h_done, b - 1)
                    s = 2 * (b % 2)
                    nc.scalar.activation(h_lin[:, b % 2, :].rearrange("p (a c) -> p a c", a=2), ps[0:C1, s:s + 2, 0:HALF], ACT.Copy).then_inc(h_copied, 1)

                def bias_offsets(q):
                    act.wait_ge(off_ready, q + 1)
                    if q >= 2:
                        act.wait_ge(pos_stored[q - 2], 16)
                    else:
                        act.wait_ge(off_loaded, 16 * 2)
                    nc.scalar.activation(off[:, q % 2, :], ps[0:2 * TAPS, 6 + q % 2, 0:QUAD * TPI], ACT.Identity, bias=off_b[:, 0:1]).then_inc(off_copied, 1)

                def copy_hT(b, s, waits=True):
                    act.wait_ge(hT_ready, b + 1)
                    if waits:
                        act.wait_ge(samples_ready, b - 1)
                    nc.scalar.activation(hT[:, s, 0:NT - 1, :].rearrange("p t c -> p (t c)"), ps[0:TILE, 4 + s, 0:(NT - 1) * C1], ACT.Copy).then_inc(hT_copied, 1)
                    nc.scalar.activation(hT[0:LAST, s, NT - 1, :], ps[0:LAST, 4 + s, (NT - 1) * C1:NT * C1], ACT.Copy).then_inc(hT_copied, 1)

                def distance_x(b, s, loads, waits=True):
                    act.wait_ge(pos_loaded[s], loads * 16)
                    if waits:
                        act.wait_ge(hat_x_ready, b - 1)
                    nc.scalar.activation(dist_x[:, s, :], pos[:, s, 1, :], ACT.Abs, bias=P["row_shift"][0:TILE, NT:NT + 1]).then_inc(dist_x_ready, 1)

                def distance_y(b, s, t, waits=True):
                    if waits:
                        wait_made(act, b - 1, t)
                    nc.scalar.activation(dist_y[:, t, :], pos[:, s, 0, :], ACT.Abs, bias=P["row_shift"][0:TILE, t:t + 1]).then_inc(dist_y_ready, 1)

                def copy_samples(b, s, at):
                    act.wait_ge(samples_ready, b + 1)
                    taps = ps[0:C1, 2 * s:2 * s + 2, 0:HALF].rearrange("p a (k t) -> p a k t", k=TAPS // 2)
                    nc.scalar.activation(P["samples"][0:C1, :, at].rearrange("p (a k) t -> p a k t", a=2), taps[:, :, 0:SLOTS // 2, :], ACT.Copy).then_inc(samples_copied, 1)
                    nc.scalar.activation(P["extra"][:, :, at].rearrange("p (a k) t -> p a k t", a=2), taps[:, :, SLOTS // 2:, :], ACT.Copy).then_inc(samples_copied, 1)

                act.wait_ge(var_ready, 1)
                nc.scalar.activation(stem_root[:, :], stem_var[:, :], ACT.Sqrt).then_inc(root_ready, 1)
                high(0)
                high(1)
                for b in range(B):
                    copy_h(b)
                    if b + 2 < B:
                        high(b + 2)
                    if b == 2 * QUAD:
                        act.wait_ge(var_ready, 2)
                        nc.scalar.activation(dcn_root[:, :], dcn_var[:, :], ACT.Sqrt).then_inc(root_ready, 1)
                    if b % QUAD == QUAD - 1 and b >= QUAD:
                        bias_offsets(b // QUAD - 1)
                act.wait_ge(place_loaded, 16 * 3)
                distance_x(0, 0, 1, waits=False)
                for t in range(NT):
                    distance_y(0, 0, t, waits=False)
                    if t == 0:
                        copy_hT(0, 0, waits=False)
                bias_offsets(NQ - 1)
                distance_x(1, 1, 1, waits=False)
                distance_y(1, 1, 0)
                distance_y(1, 1, 1)
                copy_hT(1, 1, waits=False)
                for t in range(2, NT):
                    distance_y(1, 1, t)
                with nc.scalar.Fori(1, B // 2) as pair:
                    for s in range(2):
                        b = pair * 2 + s
                        distance_x(b, s, pair + 1)
                        distance_y(b, s, 0)
                        distance_y(b, s, 1)
                        copy_hT(b, s)
                        copy_samples(b - 2, s, bass.ds((b - 2) * TPI, TPI))
                        for t in range(2, NT):
                            distance_y(b, s, t)
                copy_samples(B - 2, 0, slice((B - 2) * TPI, (B - 1) * TPI))
                copy_samples(B - 1, 1, slice((B - 1) * TPI, B * TPI))

            @block.tensor
            def _(pe):
                def stem(b):
                    pe.wait_ge(lo_split, b + 1)
                    if b >= 2:
                        pe.wait_ge(h_done, b - 1)
                    for a in range(2):
                        cols, bank = slice(a * HALF, (a + 1) * HALF), 2 * (b % 2) + a
                        nc.tensor.matmul(ps[0:C1, bank, 0:HALF], stem_hi[:, :], patch_halves[:, b % 2, cols], start=True, stop=False)
                        ins = nc.tensor.matmul(ps[0:C1, bank, 0:HALF], stem_lo[:, :], patch_halves[0:KPATCH + 1, b % 2, cols], start=False, stop=True)
                    ins.then_inc(h_ready, 1)

                def offsets(q, taps):
                    if taps[0] == 0:
                        if q == 0:
                            pe.wait_ge(off_loaded, 16 * 2)
                        pe.wait_ge(h_done, QUAD * (q + 1))
                        if q >= 2:
                            pe.wait_ge(off_copied, q - 1)
                    view = h_act[:, QUAD * q:QUAD * (q + 1), :].rearrange("c i (y u x v) -> c i y u x v", u=KS, v=KS, x=SIDE2)
                    for k in taps:
                        ins = nc.tensor.matmul(ps[0:2 * TAPS, 6 + q % 2, 0:QUAD * TPI], off_w[:, k, :], view[:, :, :, k // KS, :, k % KS], start=(k == 0), stop=(k == TAPS - 1))
                    if taps[-1] == TAPS - 1:
                        ins.then_inc(off_ready, 1)

                def transpose_h(b):
                    if b == 0:
                        pe.wait_ge(place_loaded, 16 * 3)
                        pe.wait_ge(h_done, B)
                    if b >= 2:
                        pe.wait_ge(hT_copied, 2 * (b - 1))
                    for t in range(NT):
                        ins = nc.tensor.transpose(ps[0:pixel_rows(t), 4 + b % 2, t * C1:(t + 1) * C1], h_act[:, b, t * TILE:t * TILE + pixel_rows(t)], P["ident"][0:C1, 0:C1])
                    ins.then_inc(hT_ready, 1)

                def sample(b):
                    pe.wait_ge(hT_copied, 2 * (b + 1))
                    if b >= 2:
                        pe.wait_ge(samples_copied, 2 * (b - 1))
                    for t in range(NT):
                        r = pixel_rows(t)
                        wait_made(pe, b, t)
                        for a in range(2):
                            ins = nc.tensor.matmul(ps[0:C1, 2 * (b % 2) + a, 0:HALF], hT[0:r, b % 2, t, :], weights[0:r, t, a * HALF:(a + 1) * HALF], start=(t == 0), stop=(t == NT - 1))
                        if t < NT - 1:
                            ins.then_inc(weights_used, 1)
                    ins.then_inc(samples_ready, 1)

                pe.wait_ge(warm_set, 1)
                for _ in range(WARM):
                    nc.tensor.matmul(ps[:, 4, 0:256], P["zeros"][:, 0:128], P["zeros"][:, :], start=True, stop=True)
                pe.wait_ge(stem_w_ready, 2)
                pe.wait_ge(gap_set, 2)
                for b in range(B):
                    stem(b)
                    if b >= QUAD:
                        offsets(b // QUAD - 1, range(4 * (b % QUAD), 4 * (b % QUAD) + 4))
                    else:
                        for _ in range(FILL):
                            nc.tensor.matmul(ps[:, 4, 0:256], P["zeros"][:, 0:128], P["zeros"][:, :], start=True, stop=True)
                transpose_h(0)
                offsets(NQ - 1, range(TAPS))
                for b in range(B):
                    if b + 1 < B:
                        transpose_h(b + 1)
                    sample(b)


def stage_tokens(nc, P, D, W):
    ctx = ExitStack()
    with ctx:
        def sb(name, shape, dt=F32):
            return ctx.enter_context(nc.sbuf_tensor(name, shape, dt))

        def sem(name):
            return ctx.enter_context(nc.semaphore(name))

        ps = P["ps"]
        FIRST = first_jobs(W)
        HELD = 6
        lin = sb("lin", [128, 2, DIM])
        stats = sb("stats", [128, XT, 6])
        mv = sb("mv", [128, XT, 2])
        var_eps = sb("var_eps", [128, XT])
        rstd = sb("rstd", [128, XT])
        xhat = sb("xhat", [128, 2, WIDE])
        xT = sb("xT", [128, 2, DC, 128])

        const_loaded = sem("const_loaded")
        conv_ready = sem("conv_ready")
        lin_ready = sem("lin_ready")
        h_ready = sem("tokens_ready")
        stats_ready = sem("stats_ready")
        mv_ready = sem("mv_ready")
        pool_step = sem("norm_step")
        rstd_ready = sem("rstd_ready")
        xhat_ready = sem("xhat_ready")
        xT_ready = sem("xT_ready")
        xT_copied = sem("xT_copied")
        hi_done = sem("hi_done")
        split_done = sem("split_done")

        with nc.Block() as block:
            @block.sync
            def _(sp):
                pack_samples(sp, P, XT - 1)
                sp.dma_start(P["iota"][:, :, :], D["iota"]).then_inc(const_loaded, 16)
                sp.dma_start(P["mask_q"][:, :], D["mask_q"].bitcast(BF16)).then_inc(const_loaded, 16)
                sp.dma_start(P["mask_k"][:, :], D["mask_k"].bitcast(BF16)).then_inc(const_loaded, 16)
                load_attention(sp, W, D)
                sp.wait_ge(const_loaded, 16 * 3)

            @block.tensor
            def _(pe):
                def conv(g):
                    t0, n = XTILES[g]
                    pe.wait_ge(P["packed"][g], 16 * C1 // BLOCK)
                    if g >= 2:
                        pe.wait_ge(lin_ready, g - 1)
                    for k in range(SLOTS):
                        ins = nc.tensor.matmul(ps[0:n, g % 2, 0:DIM], P["samples"][:, k, t0:t0 + n], P["dcn_w"][:, k, :], start=(k == 0), stop=(k == SLOTS - 1))
                    ins.then_inc(conv_ready, 1)

                def transpose(g):
                    t0, n = XTILES[g]
                    pe.wait_ge(xhat_ready, 2 * (g + 1))
                    if g >= 2:
                        pe.wait_ge(xT_copied, g - 1)
                    for c in range(DC):
                        ins = nc.tensor.transpose(ps[:, 2 + g % 2, c * n:(c + 1) * n], xhat[0:n, g % 2, c * 128:(c + 1) * 128], P["ident"][0:n, 0:n])
                    ins.then_inc(xT_ready, 1)

                def first(lo, hi):
                    if lo == 0:
                        pe.wait_ge(W["w_lo_done"], 2)
                        pe.wait_ge(W["w_rest_done"], 2)
                        pe.wait_ge(split_done, DC * 3)
                    for n in range(lo, hi):
                        if n >= 4:
                            pe.wait_ge(W["qk_copied"], n - 3)
                        project_qk(nc, P, W, FIRST[n], 4 + n % 4)

                for g in range(XT):
                    conv(g)
                    if g >= 1:
                        transpose(g - 1)
                first(0, HELD)
                transpose(XT - 1)
                first(HELD, len(FIRST))

            @block.scalar
            def _(act):
                def copy_T(g):
                    t0, n = XTILES[g]
                    act.wait_ge(xT_ready, g + 1)
                    if g >= 2:
                        act.wait_ge(split_done, DC * (g - 1))
                    nc.scalar.activation(xT[:, g % 2, :, 0:n], ps[:, 2 + g % 2, 0:DC * n].rearrange("p (c t) -> p c t", c=DC), ACT.Copy).then_inc(xT_copied, 1)

                for g in range(XT):
                    if g < 3:
                        split_high(nc.scalar, W, g, on_scalar=True)
                    if g == XT - 1:
                        for n in range(HELD):
                            copy_qk(nc, act, P, W, FIRST[n], 4 + n % 4, n + 1)
                    copy_T(g)
                for n in range(HELD, len(FIRST)):
                    copy_qk(nc, act, P, W, FIRST[n], 4 + n % 4, n + 1)

            @block.vector
            def _(dve):
                nc.vector.memset(P["x_lo"][64:128, 1, :].bitcast(F32), 0.0)
                for g in range(XT):
                    t0, n = XTILES[g]
                    h = P["h"][0:n, g, :]
                    dve.wait_ge(conv_ready, g + 1)
                    nc.vector.tensor_tensor(lin[0:n, g % 2, :], ps[0:n, g % 2, 0:DIM], P["dcn_shift"][0:n, :], ALU.add).then_inc(lin_ready, 1)
                    dve.wait_ge(lin_ready, g + 1)
                    nc.vector.scalar_tensor_tensor(h, lin[0:n, g % 2, :], SLOPE, lin[0:n, g % 2, :], ALU.mult, ALU.max).then_inc(h_ready, 1)
                    dve.wait_ge(h_ready, g + 1)
                    nc.vector.bn_stats(stats[0:n, g, :], h).then_inc(stats_ready, 1)
                    dve.wait_ge(stats_ready, g + 1)
                    nc.vector.bn_aggr(mv[0:n, g, :], stats[0:n, g, :]).then_inc(mv_ready, 1)
                    dve.wait_ge(rstd_ready, g + 1)
                    if g >= 2:
                        dve.wait_ge(xT_ready, g - 1)
                    for src, dst in WIDE_PARTS:
                        nc.vector.tensor_scalar(xhat[0:n, g % 2, dst], h[:, src], mv[0:n, g, 0:1], rstd[0:n, g:g + 1], ALU.subtract, ALU.mult).then_inc(xhat_ready, 1)
                    if g >= 1:
                        split_x(dve, P, xT, g - 1, xT_copied, g, hi_done, split_done)
                        if g - 1 < 3:
                            split_low(nc.vector, W, g - 1)
                split_x(dve, P, xT, XT - 1, xT_copied, XT, hi_done, split_done)

            @block.gpsimd
            def _(pool):
                steps = Steps(pool, pool_step)
                for g in range(XT):
                    n = XTILES[g][1]
                    if 1 <= g <= 3:
                        pool.wait_ge(rstd_ready, g)
                        split_rest(nc.gpsimd, W, g - 1)
                    if g == 4:
                        pool.wait_ge(W["rest_loaded"], 16 * 5)
                        nc.gpsimd.tensor_scalar(W["bias_q"][:, :], W["bias_qk"][:, 0, :], W["scale"], None, ALU.mult).then_inc(W["bias_ready"], 1)
                    pool.wait_ge(mv_ready, g + 1)
                    steps.done(nc.gpsimd.tensor_scalar(var_eps[0:n, g:g + 1], mv[0:n, g, 1:2], EPS, None, ALU.add))
                    steps.wait()
                    nc.gpsimd.tensor_tensor(rstd[0:n, g:g + 1], var_eps[0:n, g:g + 1], P["minus_half"][0:n, 0:1], ALU.pow).then_inc(rstd_ready, 1)


def attention_weights(nc, P, ctx, sems, layer, side):
    tag = f"a{layer}_"
    hd = (64, 32)[layer]
    width, tiles = HEADS * hd, HEADS * hd // 128

    def sb(name, shape, dt=F32):
        return ctx.enter_context(nc.sbuf_tensor(tag + name, shape, dt, side=side))

    W = {"layer": layer, "raw": sb("raw", [128, 3, DC, width]), "hi": sb("w_hi", [128, 3, DC, width], F32R), "lo": sb("w_lo", [128, 3, width], F32R),
         "tiles": tiles, "scale": (64, 16)[layer] ** -0.5, "qT": sb("qT", [128, tiles, NTOK]), "kT": sb("kT", [128, tiles, NTOK]),
         "wo": sb("wo", [128, tiles, DIM]), "affine": sb("affine", [128, 2, DC])}
    if layer == 0:
        W.update(ob=sb("ob", [128, DIM]), bias_qk=sb("bias_qk", [128, 2, tiles]), bias_q=sb("bias_q", [128, tiles]), bias_v=sb("bias_v", [GT, width]))
    else:
        W.update(wr=P["wr"], wr_hi=P["wr_hi"], wr_lo=P["wr_lo"])
    for name in ("qkv_loaded0", "qkv_loaded1", "qkv_loaded2", "rest_loaded", "w_hi_done", "w_lo_done", "w_rest_done", "qk_ready", "qk_copied", "bias_ready"):
        W[name] = sems.enter_context(nc.semaphore(tag + name))
    return W


def load_attention(sp, W, D):
    tag = f"a{W['layer']}_"
    for i, name in enumerate("qkv"):
        sp.dma_start(W["raw"][:, i, :, :], D[tag + "w" + name]).then_inc(W[f"qkv_loaded{i}"], 16)
    sp.dma_start(W["wo"][:, :, :], D[tag + "wo"]).then_inc(W["rest_loaded"], 16)
    sp.dma_start(W["affine"][:, :, :], D[tag + "affine"]).then_inc(W["rest_loaded"], 16)
    if W["layer"] == 0:
        sp.dma_start(W["ob"][:, :], D["ob"].to_broadcast((128, DIM))).then_inc(W["rest_loaded"], 16)
        sp.dma_start(W["bias_qk"][:, :, :], D["bias_qk"]).then_inc(W["rest_loaded"], 16)
        sp.dma_start(W["bias_v"][:, :], D["bias_v"].to_broadcast(W["bias_v"].shape)).then_inc(W["rest_loaded"], 16)
    else:
        sp.dma_start(W["wr"][:, :, :], D["wr"]).then_inc(W["rest_loaded"], 16)
    sp.wait_ge(W["rest_loaded"], 16 * (5 if W["layer"] == 0 else 3))


def split_raw(W, i):
    if i < 3:
        return W["raw"][:, i, :, :], W["hi"][:, i, :, :], W["lo"][:, i, :], (W[f"qkv_loaded{i}"], 16)
    return W["wr"][:, :, :], W["wr_hi"][:, :, :], W["wr_lo"][:, :], (W["rest_loaded"], 16 * 3)


def split_high(eng, W, i, on_scalar=False):
    raw, hi, lo, loaded = split_raw(W, i)
    eng.wait_ge(*loaded)
    if on_scalar:
        eng.activation(hi, raw, ACT.Copy).then_inc(W["w_hi_done"], 1)
    else:
        eng.tensor_copy(hi, raw).then_inc(W["w_hi_done"], 1)


def split_low(eng, W, i):
    raw, hi, lo, _ = split_raw(W, i)
    eng.wait_ge(W["w_hi_done"], i + 1)
    eng.tensor_tensor(lo, raw[:, 0, :], hi[:, 0, :].bitcast(F32), ALU.subtract).then_inc(W["w_lo_done"], 1)


def split_rest(eng, W, i):
    raw, hi, lo, _ = split_raw(W, i)
    eng.wait_ge(W["w_hi_done"], i + 1)
    eng.tensor_tensor(hi[64:128, 1, :], raw[64:128, 1, :], hi[64:128, 1, :].bitcast(F32), ALU.subtract).then_inc(W["w_rest_done"], 1)
    eng.wait_ge(W["w_rest_done"], i + 1)


def first_jobs(W):
    return [(w, i, 0) for i in range(W["tiles"]) for w in "qk"]


def project_qk(nc, P, W, job, bank):
    w, i, a = job
    m, cols, toks = "qk".index(w), slice(i * 128, (i + 1) * 128), slice(a * HALF, (a + 1) * HALF)
    for k, (wp, xp) in enumerate(five(W["hi"][:, m, :, cols], W["lo"][:, m, cols], P["x_hi"][:, :, toks], P["x_lo"][:, :, toks])):
        ins = nc.tensor.matmul(P["ps"][:, bank, 0:HALF], wp, xp, start=(k == 0), stop=(k == 4))
    ins.then_inc(W["qk_ready"], 1)


def copy_qk(nc, act, P, W, job, bank, n):
    w, i, a = job
    act.wait_ge(W["qk_ready"], n)
    dst, src, scale = W[w + "T"][:, i, a * HALF:(a + 1) * HALF], P["ps"][:, bank, 0:HALF], (W["scale"] if w == "q" else 1.0)
    if W["layer"] == 0:
        if n == 1:
            act.wait_ge(W["bias_ready"], 1)
        nc.scalar.activation(dst, src, ACT.Identity, bias=(W["bias_q"][:, i:i + 1] if w == "q" else W["bias_qk"][:, 1, i:i + 1]), scale=scale).then_inc(W["qk_copied"], 1)
    else:
        nc.scalar.activation(dst, src, ACT.Copy, scale=scale).then_inc(W["qk_copied"], 1)


def stage_attention(nc, P, D, W, following):
    layer = W["layer"]
    hd = (64, 32)[layer]
    per = 128 // hd
    tiles = HEADS // per
    width = HEADS * hd
    scale = (64 ** -0.5, 16 ** -0.5)[layer]
    HPU = 3
    UPG = HEADS // HPU
    NU = NG * UPG
    tag = f"a{layer}_"
    ctx = ExitStack()
    with ctx:
        def sb(name, shape, dt=F32):
            return ctx.enter_context(nc.sbuf_tensor(tag + name, shape, dt))

        def sem(name):
            return ctx.enter_context(nc.semaphore(tag + name))

        def unit(u):
            g, j = divmod(u, UPG)
            return g, j % per, HPU * (j // per)

        ps = P["ps"]
        w_hi, w_lo, wo, affine = W["hi"], W["lo"], W["wo"], W["affine"]
        qT, kT, qk_copied = W["qT"], W["kT"], W["qk_copied"]
        v = sb("v", [GT, NG, width])
        zT = sb("zT", [128, tiles, NTOK])
        minus_peak = sb("minus_peak", [GT, 4, HPU])
        probs = sb("probs", [GT, 3, HPU, GT])
        sums = sb("sums", [GT, 4, HPU])
        inv_sums = sb("inv_sums", [GT, 4, HPU])
        probs_n = sb("probs_n", [GT, 2, HPU, GT])
        probs_T = sb("probs_T", [GT, 2, HPU, GT])
        stats = sb("stats", [128, 2, XT, 6])
        mv = sb("mv", [128, 2, XT, 2])
        var_eps = sb("var_eps", [128, 2, XT])
        rstd = sb("rstd", [128, 2, XT])
        xhat = sb("xhat", [128, 2, WIDE])
        xT = sb("xT", [128, 2, DC, 128])
        if layer == 1:
            table_row = sb("table_row", [128, 1])
        if layer == 0:
            ob, bias_v = W["ob"], W["bias_v"]

        v_ready = sem("v_ready")
        v_copied = sem("v_copied")
        scores_ready = sem("scores_ready")
        minus_peak_ready = sem("minus_peak_ready")
        probs_ready = sem("probs_ready")
        inv_sums_ready = sem("inv_sums_ready")
        probs_n_ready = sem("probs_n_ready")
        probs_T_ready = sem("probs_T_ready")
        probs_T_copied = sem("probs_T_copied")
        z_ready = sem("z_ready")
        z_copied = sem("z_copied")
        o_ready = sem("o_ready")
        base_ready = sem("base_ready")
        sum_ready = sem("sum_ready")
        norm_step = sem("norm_step")
        mv_ready = sem("mv_ready")
        rstd_ready = sem("rstd_ready")
        pool_step = sem("pool_step")
        x_ready = sem("x_ready")
        xhat_ready = sem("xhat_ready")
        xT_ready = sem("xT_ready")
        xT_copied = sem("xT_copied")
        hi_done = sem("hi_done")
        split_done = sem("split_done")
        NORMS = 2 - layer

        cut = width // 2 if layer == 0 else width
        VCUTS = width // cut
        FIRST = first_jobs(W)
        SECOND = [(w, i, 1) for i in range(tiles) for w in "qk"]
        SECOND_UNIT = UPG * next(g for g, (t0, n) in enumerate(GROUPS) if t0 + n > HALF)
        NQK = len(FIRST) + len(SECOND)
        O_TURN = 2 * UPG + 4
        STEP_TURN = {0: (0, 1, 2, 4), 1: (0, None, 1, 3)}[layer]
        T_TURN = O_TURN + STEP_TURN[2] + 1
        TURNS = O_TURN + UPG * (XT - 1) + STEP_TURN[3] + 1
        jobs = [[] for _ in range(TURNS)]
        for a in range(VCUTS):
            jobs[a].append(("v", 0, a))
        for n, job in enumerate(SECOND):
            jobs[n * SECOND_UNIT // len(SECOND)].append(job)
        for g in range(1, NG):
            for a in range(VCUTS):
                jobs[UPG * g + a - (0 if g > 1 else 2)].append(("v", g, a))
        for g in range(XT):
            jobs[O_TURN + UPG * g].append(("o", g, 0))
            jobs[T_TURN + UPG * g].append(("t", g, 0))
        NEXT_TURN = max(NU + 1, O_TURN + UPG * (SECOND_UNIT // UPG) + STEP_TURN[3] + 1)
        NEXT = first_jobs(following) if layer == 0 else []
        UP_TURN = NEXT_TURN + 3
        SPLIT_TURNS = (10, 14, 18, 22)
        EXPERT_TURNS = (14, 15, 18, 19)
        ORDER = [job for turn in jobs for job in turn]
        QK = FIRST + [job for job in ORDER if job[0] in "qk"]
        V = [job for job in ORDER if job[0] == "v"]

        def bank_of(job):
            return 6 + ORDER.index(job) % 2

        def wait_bank(pe, job):
            if ORDER.index(job) >= 2:
                before = ORDER[ORDER.index(job) - 2]
                kind, g, _ = before
                if kind in "qk":
                    pe.wait_ge(qk_copied, QK.index(before) + 1)
                elif kind == "v":
                    pe.wait_ge(v_copied, V.index(before) + 1)
                elif kind == "o":
                    pe.wait_ge(sum_ready, g + 1)
                else:
                    pe.wait_ge(xT_copied, DC * (g + 1))

        with nc.Block() as block:
            @block.sync
            def _(sp):
                if layer == 0:
                    load_attention(sp, following, D)
                else:
                    load_expert(sp, following, D, 0, waits=False)

            @block.tensor
            def _(pe):
                def project(job):
                    w, i, a = job
                    wait_bank(pe, job)
                    if w != "v":
                        project_qk(nc, P, W, job, bank_of(job))
                        return
                    t0, n = GROUPS[i]
                    cols, toks = slice(a * cut, (a + 1) * cut), slice(t0, t0 + n)
                    for k, (wp, xp) in enumerate(five(w_hi[:, 2, :, cols], w_lo[:, 2, cols], P["x_hi"][:, :, toks], P["x_lo"][:, :, toks])):
                        ins = nc.tensor.matmul(ps[0:n, bank_of(job), 0:cut], xp, wp, start=(k == 0), stop=(k == 4))
                    ins.then_inc(v_ready, 1)

                def scores(u):
                    g, r, i0 = unit(u)
                    t0, n = GROUPS[g]
                    part = slice(r * hd, (r + 1) * hd)
                    if u == 0:
                        pe.wait_ge(qk_copied, len(FIRST))
                    if u == SECOND_UNIT:
                        pe.wait_ge(qk_copied, NQK)
                    if u >= 3:
                        pe.wait_ge(probs_ready, HPU * (u - 2))
                    masked = n > TPI
                    if masked:
                        nc.tensor.matmul(ps[0:n, u % 3, 0:HPU * n], P["mask_q"][part, 0:n], P["mask_k"][part, 0:HPU * n], start=True, stop=False)
                    for j in range(HPU):
                        ins = nc.tensor.matmul(ps[0:n, u % 3, j * n:(j + 1) * n], qT[part, i0 + j, t0:t0 + n], kT[part, i0 + j, t0:t0 + n], start=not masked, stop=(not masked or j == HPU - 1))
                    ins.then_inc(scores_ready, 1)

                def transposes(u):
                    g, r, i0 = unit(u)
                    n = GROUPS[g][1]
                    pe.wait_ge(probs_n_ready, u + 1)
                    if u >= 2:
                        pe.wait_ge(probs_T_copied, u - 1)
                    for _ in range(FILL_UNIT[layer]):
                        nc.tensor.matmul(ps[:, 3 + u % 2, 384:512], P["zeros"][:, 0:128], P["zeros"][:, 0:128], start=True, stop=True)
                    for j in range(HPU):
                        ins = nc.tensor.transpose(ps[0:n, 3 + u % 2, j * n:(j + 1) * n], probs_n[0:n, u % 2, j, 0:n], P["ident"][0:n, 0:n])
                    ins.then_inc(probs_T_ready, 1)

                def values(u):
                    g, r, i0 = unit(u)
                    n = GROUPS[g][1]
                    pe.wait_ge(probs_T_copied, u + 1)
                    pe.wait_ge(v_copied, VCUTS * (g + 1))
                    if u >= 1:
                        pe.wait_ge(z_copied, u)
                    for j in range(HPU):
                        h = (i0 + j) * per + r
                        ins = nc.tensor.matmul(ps[r * hd:(r + 1) * hd, 5, j * n:(j + 1) * n], v[0:n, g, h * hd:(h + 1) * hd], probs_T[0:n, u % 2, j, 0:n], start=True, stop=True)
                    ins.then_inc(z_ready, 1)

                def output(g):
                    t0, n = XTILES[g]
                    pe.wait_ge(z_copied, UPG * (g + 2))
                    wait_bank(pe, ("o", g, 0))
                    for i in range(tiles):
                        ins = nc.tensor.matmul(ps[0:n, bank_of(("o", g, 0)), 0:DIM], zT[:, i, t0:t0 + n], wo[:, i, :], start=(i == 0), stop=(i == tiles - 1))
                    ins.then_inc(o_ready, 1)

                def transpose_x(g):
                    n = XTILES[g][1]
                    pe.wait_ge(xhat_ready, 2 * (g + 1))
                    wait_bank(pe, ("t", g, 0))
                    for c in range(DC):
                        ins = nc.tensor.transpose(ps[:, bank_of(("t", g, 0)), c * n:(c + 1) * n], xhat[0:n, g % 2, c * 128:(c + 1) * 128], P["ident"][0:n, 0:n])
                    ins.then_inc(xT_ready, 1)

                for turn in range(TURNS):
                    if 0 <= turn - 3 < NU:
                        transposes(turn - 3)
                    if 0 <= turn - 4 < NU:
                        values(turn - 4)
                    if turn < NU:
                        scores(turn)
                    for job in jobs[turn]:
                        if job[0] == "o":
                            output(job[1])
                        elif job[0] == "t":
                            transpose_x(job[1])
                        else:
                            project(job)
                    if 0 <= turn - NEXT_TURN < len(NEXT):
                        n = turn - NEXT_TURN
                        if n == 0:
                            pe.wait_ge(following["w_lo_done"], 2)
                            pe.wait_ge(following["w_rest_done"], 2)
                            pe.wait_ge(split_done, DC * (SECOND_UNIT // UPG + 1))
                            pe.wait_ge(probs_ready, HPU * NU)
                        if n >= 3:
                            pe.wait_ge(following["qk_copied"], n - 2)
                        project_qk(nc, P, following, NEXT[n], n % 3)
                    if layer == 1 and 0 <= turn - UP_TURN < UP_EARLY:
                        if turn == UP_TURN:
                            pe.wait_ge(following["w1_lo_done"], 1)
                            pe.wait_ge(following["w1_rest_done"], 1)
                            pe.wait_ge(split_done, DC * (SECOND_UNIT // UPG + 1))
                            pe.wait_ge(probs_ready, HPU * NU)
                        up_half(nc, P, following, 0, turn - UP_TURN, 0)
                    if turn >= NU + 3:
                        for _ in range(FILL_END[layer]):
                            nc.tensor.matmul(ps[:, 3, 0:256], P["zeros"][:, 0:128], P["zeros"][:, :], start=True, stop=True)

            @block.scalar
            def _(act):
                def exps(u):
                    g, r, i0 = unit(u)
                    n = GROUPS[g][1]
                    act.wait_ge(minus_peak_ready, u + 1)
                    if u >= 3:
                        act.wait_ge(probs_n_ready, u - 2)
                    if u >= 4:
                        act.wait_ge(inv_sums_ready, u - 3)
                    for j in range(HPU):
                        nc.scalar.activation(probs[0:n, u % 3, j, 0:n], ps[0:n, u % 3, j * n:(j + 1) * n], ACT.Exp, bias=minus_peak[0:n, u % 4, j:j + 1],
                                             accum_out=sums[0:n, u % 4, j:j + 1]).then_inc(probs_ready, 1)

                def copy_z(u):
                    g, r, i0 = unit(u)
                    t0, n = GROUPS[g]
                    part = slice(r * hd, (r + 1) * hd)
                    act.wait_ge(z_ready, u + 1)
                    nc.scalar.activation(zT[part, i0:i0 + HPU, t0:t0 + n], ps[part, 5, 0:HPU * n].rearrange("p (j t) -> p j t", j=HPU), ACT.Copy).then_inc(z_copied, 1)

                def copy_xT(g):
                    t0, n = XTILES[g]
                    act.wait_ge(xT_ready, g + 1)
                    for c in range(DC):
                        if c == 0 and g >= 2:
                            act.wait_ge(split_done, DC * (g - 1))
                        nc.scalar.activation(xT[:, g % 2, c, 0:n], ps[:, bank_of(("t", g, 0)), c * n:(c + 1) * n], ACT.Identity, bias=affine[:, 1, c:c + 1], scale=affine[:, 0, c:c + 1]).then_inc(xT_copied, 1)

                for turn in range(TURNS):
                    if 0 <= turn - 1 < NU:
                        exps(turn - 1)
                    if layer == 1 and turn == NU + 1:
                        nc.scalar.activation(table_row[:, :], P["minus_half"][:, :], ACT.Gelu)
                    if 0 <= turn - 4 < NU:
                        copy_z(turn - 4)
                    for job in jobs[turn]:
                        if job[0] in "qk":
                            copy_qk(nc, act, P, W, job, bank_of(job), QK.index(job) + 1)
                        if job[0] == "t":
                            copy_xT(job[1])
                    if 0 <= turn - NEXT_TURN < len(NEXT):
                        copy_qk(nc, act, P, following, NEXT[turn - NEXT_TURN], (turn - NEXT_TURN) % 3, turn - NEXT_TURN + 1)

            @block.vector
            def _(dve):
                steps = Steps(dve, norm_step)

                def copy_v(job):
                    _, g, a = job
                    n, cols = GROUPS[g][1], slice(a * cut, (a + 1) * cut)
                    dve.wait_ge(v_ready, V.index(job) + 1)
                    if layer == 0:
                        nc.vector.tensor_tensor(v[0:n, g, cols], ps[0:n, bank_of(job), 0:cut], bias_v[0:n, cols], ALU.add).then_inc(v_copied, 1)
                    else:
                        nc.vector.tensor_copy(v[0:n, g, cols], ps[0:n, bank_of(job), 0:cut]).then_inc(v_copied, 1)

                def peaks(u):
                    g, r, i0 = unit(u)
                    n = GROUPS[g][1]
                    dve.wait_ge(scores_ready, u + 1)
                    if u >= 4:
                        dve.wait_ge(probs_ready, HPU * (u - 3))
                    nc.vector.reduce_max(minus_peak[0:n, u % 4, :], ps[0:n, u % 3, 0:HPU * n].rearrange("p (j t) -> p j t", j=HPU), axis=AX.X, negate=True).then_inc(minus_peak_ready, 1)

                def inverse(u):
                    n = GROUPS[unit(u)[0]][1]
                    dve.wait_ge(probs_ready, HPU * (u + 1))
                    if u >= 4:
                        dve.wait_ge(probs_n_ready, u - 3)
                    nc.vector.reciprocal(inv_sums[0:n, u % 4, :], sums[0:n, u % 4, :]).then_inc(inv_sums_ready, 1)

                def copy_T(u):
                    n = GROUPS[unit(u)[0]][1]
                    dve.wait_ge(probs_T_ready, u + 1)
                    if u >= 2:
                        dve.wait_ge(z_ready, u - 1)
                    nc.vector.tensor_copy(probs_T[0:n, u % 2, :, 0:n], ps[0:n, 3 + u % 2, 0:HPU * n].rearrange("p (j t) -> p j t", j=HPU)).then_inc(probs_T_copied, 1)

                def norm_stats(src, k, g):
                    n = XTILES[g][1]
                    steps.done(nc.vector.bn_stats(stats[0:n, k, g, :], src))
                    steps.wait()
                    nc.vector.bn_aggr(mv[0:n, k, g, :], stats[0:n, k, g, :]).then_inc(mv_ready, 1)

                def tail(g, step):
                    n = XTILES[g][1]
                    h, x, rest = P["h"][0:n, g, :], P["x"][0:n, g, :], P["rest"][0:n, g, :]
                    src = h if layer == 0 else x
                    if step == 0:
                        dve.wait_ge(o_ready, g + 1)
                        if layer == 0:
                            dve.wait_ge(base_ready, g + 1)
                        nc.vector.tensor_tensor(src, ps[0:n, bank_of(("o", g, 0)), 0:DIM], src, ALU.add).then_inc(sum_ready, 1)
                        dve.wait_ge(sum_ready, g + 1)
                        norm_stats(src, 0, g)
                    if step == 1 and layer == 0:
                        dve.wait_ge(rstd_ready, NORMS * g + 1)
                        nc.vector.tensor_scalar(x, h, mv[0:n, 0, g, 0:1], rstd[0:n, 0, g:g + 1], ALU.subtract, ALU.mult).then_inc(x_ready, 1)
                        dve.wait_ge(x_ready, g + 1)
                        norm_stats(x, 1, g)
                    if step == 2:
                        k = NORMS - 1
                        dve.wait_ge(rstd_ready, NORMS * (g + 1))
                        if g >= 2:
                            dve.wait_ge(xT_ready, g - 1)
                        for src, dst in WIDE_PARTS:
                            nc.vector.tensor_scalar(xhat[0:n, g % 2, dst], x[:, src], mv[0:n, k, g, 0:1], rstd[0:n, k, g:g + 1], ALU.subtract, ALU.mult).then_inc(xhat_ready, 1)
                    if step == 3:
                        split_x(nc.vector, P, xT, g, xT_copied, DC * (g + 1), hi_done, split_done)

                for turn in range(TURNS):
                    if 0 <= turn - 3 < NU:
                        copy_T(turn - 3)
                    if turn < NU:
                        peaks(turn)
                    if 0 <= turn - 1 < NU:
                        inverse(turn - 1)
                    for job in jobs[turn]:
                        if job[0] == "v":
                            copy_v(job)
                    for g in range(XT):
                        for step in range(4):
                            if STEP_TURN[step] is not None and turn == O_TURN + UPG * g + STEP_TURN[step]:
                                tail(g, step)
                    if layer == 0 and turn in SPLIT_TURNS:
                        split_high(nc.vector, following, SPLIT_TURNS.index(turn))
                    if layer == 0 and turn - 1 in SPLIT_TURNS:
                        split_low(nc.vector, following, SPLIT_TURNS.index(turn - 1))
                    if layer == 1 and turn in EXPERT_TURNS:
                        (split_w1_high, split_w1_low, split_w2_high, split_w2_low)[EXPERT_TURNS.index(turn)](nc.vector, following, 0, 0)

            @block.gpsimd
            def _(pool):
                steps = Steps(pool, pool_step)
                if layer == 0:
                    for g in range(XT):
                        n = XTILES[g][1]
                        nc.gpsimd.tensor_tensor(P["h"][0:n, g, :], P["h"][0:n, g, :], ob[0:n, :], ALU.add).then_inc(base_ready, 1)

                def normalise(u):
                    n = GROUPS[unit(u)[0]][1]
                    pool.wait_ge(inv_sums_ready, u + 1)
                    if u >= 2:
                        pool.wait_ge(probs_T_ready, u - 1)
                    nc.gpsimd.tensor_tensor(probs_n[0:n, u % 2, :, 0:n], probs[0:n, u % 3, :, 0:n], inv_sums[0:n, u % 4, :].unsqueeze(2).to_broadcast((n, HPU, n)), ALU.mult).then_inc(probs_n_ready, 1)

                def inverse_deviation(g, k):
                    n = XTILES[g][1]
                    pool.wait_ge(mv_ready, NORMS * g + k + 1)
                    steps.done(nc.gpsimd.tensor_scalar(var_eps[0:n, k, g:g + 1], mv[0:n, k, g, 1:2], EPS, None, ALU.add))
                    steps.wait()
                    nc.gpsimd.tensor_tensor(rstd[0:n, k, g:g + 1], var_eps[0:n, k, g:g + 1], P["minus_half"][0:n, 0:1], ALU.pow).then_inc(rstd_ready, 1)

                for turn in range(TURNS):
                    if 0 <= turn - 1 < NU:
                        normalise(turn - 1)
                    if layer == 0 and turn - 1 in SPLIT_TURNS:
                        pool.wait_ge(probs_n_ready, turn)
                        split_rest(nc.gpsimd, following, SPLIT_TURNS.index(turn - 1))
                    if layer == 1 and turn == EXPERT_TURNS[1]:
                        pool.wait_ge(probs_n_ready, turn)
                        split_w1_rest(nc.gpsimd, following, 0, 0)
                        pool.wait_ge(following["w1_rest_done"], 1)
                    for g in range(XT):
                        for k in range(NORMS):
                            if turn == O_TURN + UPG * g + k:
                                inverse_deviation(g, k)
                        if layer == 1 and turn == O_TURN + UPG * g + 2:
                            n = XTILES[g][1]
                            pool.wait_ge(sum_ready, g + 1)
                            nc.gpsimd.tensor_tensor(P["rest"][0:n, g, :], P["h"][0:n, g, :], P["x"][0:n, g, :], ALU.add)


def expert_weights(nc, ctx):
    def sb(name, shape, dt=F32):
        return ctx.enter_context(nc.sbuf_tensor(name, shape, dt))

    W = {"raw1": sb("raw1", [128, DC, FF]), "raw2": sb("raw2", [128, FT, DIM]),
         "hi1": [sb(f"w1_hi{i}", [128, DC, FF], F32R) for i in range(2)], "lo1": [sb(f"w1_lo{i}", [128, FF], F32R) for i in range(2)],
         "both2": [sb(f"w2_{i}", [128, FT, 2, DIM], F32R) for i in range(2)]}
    for name in ("raw1_loaded", "raw2_loaded", "w1_hi_done", "w1_lo_done", "w1_rest_done", "w2_hi_done", "w2_done"):
        W[name] = ctx.enter_context(nc.semaphore(name))
    return W


def load_expert(sp, W, D, e, waits=True):
    if waits:
        sp.wait_ge(W["w1_lo_done"], e)
        sp.wait_ge(W["w1_rest_done"], e)
    sp.dma_start(W["raw1"][:, :, :], D["w1"][bass.ds(e, 1), :, :, :].rearrange("e p c n -> (e p) c n")).then_inc(W["raw1_loaded"], 16)
    if waits:
        sp.wait_ge(W["w2_done"], e)
    sp.dma_start(W["raw2"][:, :, :], D["w2"][bass.ds(e, 1), :, :, :].rearrange("e p f n -> (e p) f n")).then_inc(W["raw2_loaded"], 16)


def split_w1_high(eng, W, e, s):
    eng.wait_ge(W["raw1_loaded"], (e + 1) * 16)
    eng.tensor_copy(W["hi1"][s][:, :, :], W["raw1"][:, :, :]).then_inc(W["w1_hi_done"], 1)


def split_w1_low(eng, W, e, s):
    eng.wait_ge(W["w1_hi_done"], e + 1)
    eng.tensor_tensor(W["lo1"][s][:, :], W["raw1"][:, 0, :], W["hi1"][s][:, 0, :].bitcast(F32), ALU.subtract).then_inc(W["w1_lo_done"], 1)


def split_w1_rest(eng, W, e, s):
    eng.wait_ge(W["w1_hi_done"], e + 1)
    eng.tensor_tensor(W["hi1"][s][64:128, 1, :], W["raw1"][64:128, 1, :], W["hi1"][s][64:128, 1, :].bitcast(F32), ALU.subtract).then_inc(W["w1_rest_done"], 1)


def split_w2_high(eng, W, e, s):
    eng.wait_ge(W["raw2_loaded"], (e + 1) * 16)
    eng.tensor_copy(W["both2"][s][:, :, 0, :], W["raw2"][:, :, :]).then_inc(W["w2_hi_done"], 1)


def split_w2_low(eng, W, e, s):
    eng.wait_ge(W["w2_hi_done"], e + 1)
    eng.tensor_tensor(W["both2"][s][:, :, 1, :], W["raw2"][:, :, :], W["both2"][s][:, :, 0, :].bitcast(F32), ALU.subtract).then_inc(W["w2_done"], 1)


def up_half(nc, P, W, s, f, a):
    cols, toks, bank = slice(f * 128, (f + 1) * 128), slice(a * HALF, (a + 1) * HALF), 2 * (f % 2) + a
    for k, (wp, xp) in enumerate(five(W["hi1"][s][:, :, cols], W["lo1"][s][:, cols], P["x_hi"][:, :, toks], P["x_lo"][:, :, toks])):
        ins = nc.tensor.matmul(P["ps"][:, bank, 0:HALF], wp, xp, start=(k == 0), stop=(k == 4))
    return ins


def stage_experts(nc, P, D, W, out):
    ctx = ExitStack()
    with ctx:
        def sb(name, shape, dt=F32):
            return ctx.enter_context(nc.sbuf_tensor(name, shape, dt))

        def sem(name):
            return ctx.enter_context(nc.semaphore(name))

        ps = P["ps"]
        w2 = W["both2"]
        w2_done = W["w2_done"]
        hidden = sb("hidden", [128, 3, NTOK])
        hid_hi = sb("hid_hi", [128, 2, FT, NTOK], F32R)
        hid_lo = sb("hid_lo", [128, 2, FT, NTOK], F32R)
        acc = P["rest"]

        logits = sb("logits", [128, XT, EXPERTS])
        top = sb("top", [128, XT, 8])
        top_at = sb("top_at", [128, XT, 8], U32)
        top_f = sb("top_f", [128, XT, 2])
        gap = sb("gap", [128, XT])
        second = sb("second", [128, XT])
        total = sb("total", [128, XT])
        share = sb("share", [128, 2, XT])
        pick = sb("pick", [128, 2, XT, EXPERTS])

        euler = sb("euler", [128, XT])

        euler_set = sem("euler_set")
        logits_ready = sem("logits_ready")
        logits_copied = sem("logits_copied")
        route_step = sem("route_step")
        gap_ready = sem("gap_ready")
        second_ready = sem("second_ready")
        gates_ready = sem("gates_ready")
        up_ready = sem("up_ready")
        gelu_done = sem("gelu_done")
        hid_hi_done = sem("hid_hi_done")
        hidden_ready = sem("hidden_ready")
        down_ready = sem("down_ready")
        added = sem("added")
        stored = sem("stored")

        with nc.Block() as block:
            @block.sync
            def _(sp):
                load_expert(sp, W, D, 1)
                with nc.sync.Fori(2, EXPERTS) as e:
                    load_expert(sp, W, D, e)
                for t, (t0, n) in enumerate(XTILES):
                    sp.wait_ge(added, 2 * (XT * (EXPERTS - 1) + t + 1))
                    sp.dma_start(out[t0:t0 + n, :], acc[0:n, t, :]).then_inc(stored, 16)
                sp.wait_ge(stored, 16 * XT)

            @block.tensor
            def _(pe):
                def up(e, s, waits=True):
                    pe.wait_ge(W["w1_lo_done"], e + 1)
                    pe.wait_ge(W["w1_rest_done"], e + 1)
                    for f in range(FT):
                        if waits or f >= 2:
                            pe.wait_ge(gelu_done, e * FT + (f - 1))
                        for a in range(2):
                            if waits or a == 1 or f >= UP_EARLY:
                                ins = up_half(nc, P, W, s, f, a)
                        ins.then_inc(up_ready, 1)

                def down(e, s, first=False):
                    pe.wait_ge(w2_done, e + 1)
                    pe.wait_ge(hidden_ready, (e + 1) * FT)
                    for t, (t0, n) in enumerate(XTILES):
                        if t % 4 == 0 and not (first and t == 0):
                            pe.wait_ge(added, e * (2 * XT) + 2 * max(0, t - 3))
                        for f in range(FT):
                            nc.tensor.matmul(ps[0:n, 4 + t % 4, 0:2 * DIM], hid_hi[:, s, f, t0:t0 + n], w2[s][:, f, :, :].rearrange("p a d -> p (a d)"), start=(f == 0), stop=False)
                            ins = nc.tensor.matmul(ps[0:n, 4 + t % 4, 0:DIM], hid_lo[:, s, f, t0:t0 + n], w2[s][:, f, 0, :], start=False, stop=(f == FT - 1))
                        ins.then_inc(down_ready, 1)

                up(0, 0, waits=False)
                for t, (t0, n) in enumerate(XTILES):
                    for k, (wp, xp) in enumerate(five(P["wr_hi"], P["wr_lo"][:, :], P["x_hi"][:, :, t0:t0 + n], P["x_lo"][:, :, t0:t0 + n])):
                        ins = nc.tensor.matmul(ps[0:n, 4 + t % 4, t * EXPERTS:(t + 1) * EXPERTS], xp, wp, start=(k == 0), stop=(k == 4))
                    ins.then_inc(logits_ready, 1)
                up(1, 1)
                pe.wait_ge(logits_copied, XT)
                down(0, 0, first=True)
                with nc.tensor.Fori(0, EXPERTS // 2 - 1) as pair:
                    for s in (1, 0):
                        e = pair * 2 + (2 - s)
                        up(e + 1, 1 - s)
                        down(e, s)
                down(EXPERTS - 1, 1)

            @block.scalar
            def _(act):
                def gelus(e, s, waits=True):
                    for f in range(FT):
                        act.wait_ge(up_ready, e * FT + (f + 1))
                        if s != 0 or waits or f >= 3:
                            act.wait_ge(hidden_ready, e * FT + (f - 2))
                        nc.scalar.activation(hidden[:, f % 3, :].rearrange("p (a t) -> p a t", a=2), ps[:, 2 * (f % 2):2 * (f % 2) + 2, 0:HALF], ACT.Gelu).then_inc(gelu_done, 1)
                        act.wait_ge(gelu_done, e * FT + (f + 1))
                        if waits and f == 0:
                            act.wait_ge(down_ready, (e - 1) * XT)
                        nc.scalar.activation(hid_hi[:, s, f, :], hidden[:, f % 3, :], ACT.Copy).then_inc(hid_hi_done, 1)

                gelus(0, 0, waits=False)
                gelus(1, 1, waits=False)
                with nc.scalar.Fori(1, EXPERTS // 2) as pair:
                    for s in range(2):
                        gelus(pair * 2 + s, s)

            @block.gpsimd
            def _(pool):
                split_w1_rest(nc.gpsimd, W, 1, 1)
                pool.wait_ge(W["w1_rest_done"], 2)
                nc.gpsimd.memset(euler[:, :], math.e).then_inc(euler_set, 1)
                pool.wait_ge(euler_set, 1)
                pool.wait_ge(gap_ready, 1)
                nc.gpsimd.tensor_tensor(second[:, :], euler[:, :], gap[:, :], ALU.pow).then_inc(second_ready, 1)
                pool.wait_ge(second_ready, 1)
                with nc.gpsimd.Fori(1, EXPERTS // 2) as pair:
                    for s in range(2):
                        split_w1_rest(nc.gpsimd, W, pair * 2 + s, s)

            @block.vector
            def _(dve):
                def split1(e, s, waits=True):
                    if waits:
                        dve.wait_ge(up_ready, (e - 1) * FT)
                    split_w1_high(nc.vector, W, e, s)
                    split_w1_low(nc.vector, W, e, s)

                def split2(e, s, waits=True):
                    if waits:
                        dve.wait_ge(down_ready, (e - 1) * XT)
                    split_w2_high(nc.vector, W, e, s)
                    split_w2_low(nc.vector, W, e, s)

                def low(e, s, f, waits=True):
                    dve.wait_ge(hid_hi_done, e * FT + (f + 1))
                    if waits and f == 0:
                        dve.wait_ge(down_ready, (e - 1) * XT)
                    nc.vector.tensor_tensor(hid_lo[:, s, f, :], hidden[:, f % 3, :], hid_hi[:, s, f, :].bitcast(F32), ALU.subtract).then_inc(hidden_ready, 1)

                def add(e):
                    for t, (t0, n) in enumerate(XTILES):
                        dve.wait_ge(down_ready, e * XT + (t + 1))
                        if isinstance(e, int) and e == 0:
                            dve.wait_ge(gates_ready, 1)
                        else:
                            dve.wait_ge(added, (e - 1) * (2 * XT) + 2 * (t + 1))
                        for a in range(2):
                            if a == 1:
                                dve.wait_ge(added, e * (2 * XT) + (2 * t + 1))
                            nc.vector.scalar_tensor_tensor(acc[0:n, t, :], ps[0:n, 4 + t % 4, a * DIM:(a + 1) * DIM], P["gates"][0:n, t, bass.ds(e, 1)], acc[0:n, t, :], ALU.mult, ALU.add).then_inc(added, 1)

                def turn(e, s):
                    for f in range(FT):
                        low(e + 1, 1 - s, f)
                        if f == 0:
                            split2(e + 1, 1 - s)
                        if f == 3 and not (isinstance(e, int) and e == EXPERTS - 2):
                            split1(e + 2, s)
                    add(e)

                route = Steps(dve, route_step)

                def copy_logits():
                    route.done(nc.vector.memset(logits[:, :, :], 0.0))
                    dve.wait_ge(logits_ready, XT)
                    route.wait()
                    for t, (t0, n) in enumerate(XTILES):
                        nc.vector.tensor_copy(logits[0:n, t, :], ps[0:n, 4 + t % 4, t * EXPERTS:(t + 1) * EXPERTS]).then_inc(logits_copied, 1)

                def largest():
                    dve.wait_ge(logits_copied, XT)
                    for t in range(XT):
                        route.done(nc.vector.max(top[:, t, :], logits[:, t, :]))

                def places():
                    route.wait()
                    for t in range(XT):
                        route.done(nc.vector.max_index(top_at[:, t, :], top[:, t, :], logits[:, t, :]))
                    nc.vector.tensor_tensor(gap[:, :], top[:, :, 1], top[:, :, 0], ALU.subtract).then_inc(gap_ready, 1)

                def picks():
                    route.wait()
                    route.done(nc.vector.tensor_copy(top_f[:, :, :], top_at[:, :, 0:2]))
                    route.wait()
                    for k in range(2):
                        route.done(nc.vector.tensor_tensor(pick[:, k, :, :], P["iota"][:, :, :], top_f[:, :, k:k + 1].to_broadcast((128, XT, EXPERTS)), ALU.is_equal))

                def gates():
                    dve.wait_ge(second_ready, 1)
                    route.done(nc.vector.tensor_scalar(total[:, :], second[:, :], 1.0, None, ALU.add))
                    route.wait()
                    route.done(nc.vector.reciprocal(share[:, 0, :], total[:, :]))
                    route.wait()
                    route.done(nc.vector.tensor_tensor(share[:, 1, :], second[:, :], share[:, 0, :], ALU.mult))
                    route.wait()
                    for k in range(2):
                        route.done(nc.vector.tensor_tensor(pick[:, k, :, :], pick[:, k, :, :], share[:, k, :].unsqueeze(2).to_broadcast((128, XT, EXPERTS)), ALU.mult))
                    route.wait()
                    nc.vector.tensor_tensor(P["gates"][:, :, :], pick[:, 0, :, :], pick[:, 1, :, :], ALU.add).then_inc(gates_ready, 1)

                low(0, 0, 0, waits=False)
                split1(1, 1, waits=False)
                for f in range(1, FT):
                    low(0, 0, f, waits=False)
                    if f == 3:
                        split2(1, 1, waits=False)
                for f in range(FT):
                    low(1, 1, f, waits=False)
                    if f < 5:
                        (copy_logits, largest, places, picks, gates)[f]()
                    if f == 3:
                        split1(2, 0)
                add(0)
                with nc.vector.Fori(0, EXPERTS // 2 - 2) as pair:
                    for s in (1, 0):
                        turn(pair * 2 + (2 - s), s)
                turn(EXPERTS - 3, 1)
                turn(EXPERTS - 2, 0)
                add(EXPERTS - 1)


def build(nc, D, out):
    ctx = ExitStack()
    with ctx:
        def sb(name, shape, dt=F32):
            return ctx.enter_context(nc.sbuf_tensor(name, shape, dt))

        P = {"ps": ctx.enter_context(nc.psum_tensor("ps", [128, 8, 512], F32))}
        P["pos_dram"] = nc.dram_tensor("pos_dram", (B, 2 * TAPS, TPI), F32).ap()
        P["zeros"] = sb("zeros", [128, 256], BF16)
        P["ident"] = sb("ident", [128, 128])
        P["minus_half"] = sb("minus_half", [128, 1])
        P["row_shift"] = sb("row_shift", [128, NT + 1])
        for name, shape, dt in (("wr", [128, DC, EXPERTS], F32), ("wr_hi", [128, DC, EXPERTS], F32R), ("wr_lo", [128, EXPERTS], F32R)):
            P[name] = sb(name, shape, dt)
        P["mask_q"] = sb("mask_q", [128, GT], BF16)
        P["mask_k"] = sb("mask_k", [128, IPG * GT], BF16)
        P["iota"] = sb("iota", [128, XT, EXPERTS])
        P["gates"] = sb("gates", [128, XT, EXPERTS])
        for name in ("h", "x", "rest"):
            P[name] = sb(name, [128, XT, DIM])
        P["x_hi"] = sb("x_hi", [128, DC, NTOK], F32R)
        P["x_lo"] = sb("x_lo", [128, DC, NTOK], F32R)
        early, late = ExitStack(), ExitStack()
        P["packed"] = [ctx.enter_context(nc.semaphore(f"packed{t}")) for t in range(XT)]
        for name, shape in (("samples", [128, SLOTS, NTOK]), ("dcn_w", [128, SLOTS, DIM]), ("dcn_shift", [128, DIM]), ("extra", [C1, TAPS - SLOTS, NTOK])):
            P[name] = early.enter_context(nc.sbuf_tensor(name, shape, F32, side="right"))
        stage_images(nc, P, D)
        with ExitStack() as first:
            W0 = attention_weights(nc, P, first, ctx, 0, "left")
            stage_tokens(nc, P, D, W0)
            early.close()
            W1 = attention_weights(nc, P, late, ctx, 1, "right")
            stage_attention(nc, P, D, W0, W1)
        WE = expert_weights(nc, ctx)
        stage_attention(nc, P, D, W1, WE)
        late.close()
        stage_experts(nc, P, D, WE, out)


def constants():
    import numpy as np
    k, token = np.arange(TAPS)[:, None], np.arange(NTOK)[None, :] % TPI
    grid = np.concatenate([k // KS + KS * (token // SIDE2), k % KS + KS * (token % SIDE2)]).astype(np.float32)
    p = np.arange(128)
    row_shift = np.zeros((128, NT + 1), np.float32)
    row_shift[:, 0:NT] = -(p[:, None] // SIDE + ROWS * np.arange(NT))
    row_shift[:, NT] = -(p % SIDE)
    mask_q, mask_k = np.zeros((128, GT), np.float32), np.zeros((128, IPG, GT), np.float32)
    image = np.arange(GT) // TPI
    for base in range(0, 128, 32):
        mask_q[base], mask_k[base] = 1, -BIG
        for i in range(IPG):
            mask_q[base + 1 + i], mask_k[base + 1 + i] = image == i, BIG * (image == i)
    bias_row = np.zeros((KPATCH + 1, 1), np.float32)
    bias_row[KPATCH] = 1
    iota = np.broadcast_to(np.arange(EXPERTS, dtype=np.float32), (128, XT, EXPERTS))

    def bf16(a):
        return (np.ascontiguousarray(a, np.float32).view(np.uint32) >> 16).astype(np.uint16)

    return {"grid": grid, "row_shift": row_shift, "bias_row": bias_row, "iota": iota, "ident": np.eye(128, dtype=np.float32),
            "mask_q": bf16(mask_q), "mask_k": bf16(mask_k.reshape(128, IPG * GT))}


def layouts(I):
    import numpy as np

    def chunks(w):
        return np.stack([w[0:128], np.concatenate([w[128:DIM], w[128:DIM]])], 1)

    t = {n: np.asarray(a) for n, a in I.items()}
    tok = {n[len("L0_tok_"):]: a for n, a in t.items() if n.startswith("L0_tok_")}
    att = {n[len("L0_attn_"):]: a for n, a in t.items() if n.startswith("L0_attn_")}
    ffn = {n[len("L0_ffn_"):]: a for n, a in t.items() if n.startswith("L0_ffn_")}
    patches = np.ones((KPATCH + 1, B, PIX), np.float32)
    patches[0:KPATCH] = t["x"].reshape(B, CIN, SIDE, KS, SIDE, KS).transpose(1, 3, 5, 0, 2, 4).reshape(KPATCH, B, PIX)
    taps = tok["dcn_w"].reshape(DIM, C1, 2, TAPS // 2).transpose(1, 2, 3, 0)
    beside = taps[:, :, SLOTS // 2:].reshape(C1 // BLOCK, BLOCK, TAPS - SLOTS, DIM).transpose(1, 2, 0, 3).reshape(BLOCK, SLOTS, DIM)
    dcn_w = np.concatenate([taps[:, :, 0:SLOTS // 2].reshape(C1, SLOTS, DIM), beside])
    d = {
        "patches": patches,
        "stem_w": np.concatenate([tok["stem_w"].reshape(C1, KPATCH).T, tok["stem_b"][None, :]]),
        "stem_par": np.concatenate([tok[n] for n in ("bn1_g", "bn1_b", "bn1_m", "bn1_v")])[None, :],
        "off_w": tok["off_w"].reshape(TAPS, 2, C1, TAPS).transpose(2, 3, 1, 0).reshape(C1, TAPS, 2 * TAPS),
        "off_b": tok["off_b"].reshape(TAPS, 2).T.reshape(2 * TAPS, 1),
        "dcn_w": dcn_w,
        "dcn_par": np.concatenate([tok[n] for n in ("bn2_g", "bn2_b", "bn2_m", "bn2_v", "dcn_b")])[None, :],
        "ob": att["Ob"].reshape(1, DIM),
        "a0_wo": att["O"].reshape(HEADS // 2, 128, DIM).transpose(1, 0, 2),
        "a0_affine": np.stack([chunks(ffn["ln1_g"]), chunks(ffn["ln1_b"])], 1),
        "a1_affine": np.stack([chunks(ffn["ln2_g"]), chunks(ffn["ln2_b"])], 1),
        "wr": chunks(ffn["Wrouter"]),
        "w1": np.stack([chunks(w) for w in ffn["W1"]]),
        "w2": ffn["W2"].reshape(EXPERTS, FT, 128, DIM).transpose(0, 2, 1, 3),
    }
    d["bias_qk"] = np.stack([att[n].reshape(HEADS // 2, 128).T for n in ("Qbs", "Kbs")], 1)
    d["bias_v"] = att["Vbs"].reshape(1, -1)
    for name, w in (("wq", "Qs"), ("wk", "Ks"), ("wv", "Vs")):
        d["a0_" + name] = chunks(att[w].transpose(1, 0, 2).reshape(DIM, -1))
    qkv = np.zeros((3, DIM, HEADS, 32), ffn["Wqkv"].dtype)
    qkv[:, :, :, 0:16] = ffn["Wqkv"].reshape(DIM, 3, HEADS, 16).transpose(1, 0, 2, 3)
    for i, name in enumerate(("wq", "wk", "wv")):
        d["a1_" + name] = chunks(qkv[i].reshape(DIM, -1))
    proj = np.zeros((HEADS, 32, DIM), ffn["Wproj"].dtype)
    proj[:, 0:16] = ffn["Wproj"].reshape(HEADS, 16, DIM)
    d["a1_wo"] = proj.reshape(HEADS // 4, 128, DIM).transpose(1, 0, 2)
    return d


def kernel(**inputs):
    import numpy as np
    import concourse.bacc as bacc
    from concourse.bass_utils import run_bass_kernel_spmd

    nc = bacc.Bacc("TRN2", target_bir_lowering=False, num_devices=1)
    arrays, D = {}, {}
    for name, a in {**constants(), **layouts(inputs)}.items():
        arrays["in_" + name] = np.ascontiguousarray(a)
        D[name] = nc.dram_tensor("in_" + name, arrays["in_" + name].shape, mybir.dt.from_np(arrays["in_" + name].dtype), kind="ExternalInput").ap()
    out = nc.dram_tensor("out", (NTOK, DIM), F32, kind="ExternalOutput").ap()
    build(nc, D, out)
    r = run_bass_kernel_spmd(nc, [arrays], core_ids=[0])
    return r.results[0]["out"].reshape(B, TPI, DIM)
```
